# Optimizing a Trainium2 kernel written in Bass

```python
import numpy as np
import jax
import jax.numpy as jnp

def _softmax(x, axis=-1):
    return jax.nn.softmax(x, axis=axis)

def _gelu(x):
    return jax.nn.gelu(x, approximate=True)

def _silu(x):
    return jax.nn.silu(x)

def _sigmoid(x):
    return jax.nn.sigmoid(x)

def _layernorm(x, axis=-1, eps=1e-05):
    m = jnp.mean(x, axis=axis, keepdims=True)
    v = jnp.var(x, axis=axis, keepdims=True)
    return (x - m) / jnp.sqrt(v + eps)

def _scatter_add(tgt, idx, src, axis=0):
    return tgt.at[idx].add(src)

def _segment_sum(src, seg, n):
    return jax.ops.segment_sum(src, seg, n)
kernel_name = 'mk_gnn_resnorm_d4_gnn_r8_0e3061'

def setup_inputs(seed: int=0):
    np.random.seed(seed)
    _w = jnp.asarray

    def _rec_inputs():
        import jax
        import jax.numpy as jnp
        _gk = jax.random.key(seed)
        x = -0.0003713 + 1 * jax.random.normal(jax.random.fold_in(_gk, 1), (12500, 128), jnp.float32)
        src = jax.random.randint(jax.random.fold_in(_gk, 2), (200000,), 0, 12500, jnp.int32)
        dst = jax.random.randint(jax.random.fold_in(_gk, 3), (200000,), 0, 12500, jnp.int32)
        _o = jnp.argsort(dst, stable=True)
        src = src[_o]
        dst = dst[_o]
        edge_attr_128 = -8.513e-05 + 0.999844 * jax.random.normal(jax.random.fold_in(_gk, 12), (200000, 128), jnp.float32)
        edge_weight = jax.random.uniform(jax.random.fold_in(_gk, 14), (200000,), jnp.float32, 0.0, 0.999998)
        return (x, src, dst, edge_attr_128, edge_weight)
    x, src, dst, edge_attr_128, edge_weight = _rec_inputs()

    def _L0_gnn_setup():
        import jax, jax.numpy as jnp
        import numpy as np
        N = 12500
        E = 200000
        D_IN = 128
        D_OUT = 128
        key = jax.random.key(seed)
        k1, k2, k3, k4 = jax.random.split(key, 4)
        H = jax.random.normal(k1, (N, D_IN), dtype=jnp.float32)
        src = jax.random.randint(k2, (E,), 0, N, dtype=jnp.int32)
        dst = jax.random.randint(k3, (E,), 0, N, dtype=jnp.int32)
        W = jax.random.normal(k4, (D_OUT, 2 * D_IN), dtype=jnp.float32) * 0.05
        b = jnp.zeros((D_OUT,), dtype=jnp.float32)
        return {'H': H, 'src': src, 'dst': dst, 'W': W, 'b': b}
    _L0_gnn_all = _L0_gnn_setup()
    _L0_gnn_in = {k: v for k, v in _L0_gnn_all.items() if k in ('W', 'b')}
    del _L0_gnn_all

    def _L1_gnn_setup():
        import jax, jax.numpy as jnp
        import numpy as np
        N = 6250
        E = 100000
        NFEAT = 128
        HID = 32
        HEADS = 4
        SLOPE = 0.2

        def glorot(key, shape, fan_in, fan_out):
            lim = float(np.sqrt(6.0 / (fan_in + fan_out)))
            return jax.random.uniform(key, shape, jnp.float32, -lim, lim)

        def gat_layer(x, src, dst, ew, W, att_l, att_r, b):
            n = x.shape[0]
            h = (x @ W).reshape(n, HEADS, HID)
            a_l = jnp.einsum('nhc,hc->nh', h, att_l)
            a_r = jnp.einsum('nhc,hc->nh', h, att_r)
            e = jax.nn.leaky_relu(a_l[src] + a_r[dst], SLOPE) * ew[:, None]
            m = jax.ops.segment_max(e, dst, num_segments=n)
            m = jnp.where(jnp.isfinite(m), m, 0.0)
            ex = jnp.exp(e - m[dst])
            s = jax.ops.segment_sum(ex, dst, num_segments=n)
            alpha = ex / (s[dst] + 1e-16)
            out = jax.ops.segment_sum(h[src] * alpha[:, :, None], dst, num_segments=n)
            return out.reshape(n, HEADS * HID) + b
        key = jax.random.key(seed)
        ks = jax.random.split(key, 10)
        HC = HEADS * HID
        return {'x': jax.random.normal(ks[0], (N, NFEAT), jnp.float32), 'edge_index': jax.random.randint(ks[1], (2, E), 0, N, jnp.int32), 'edge_weight': jax.random.uniform(ks[2], (E,), jnp.float32), 'W1': glorot(ks[3], (NFEAT, HC), NFEAT, HC), 'att_l1': glorot(ks[4], (HEADS, HID), HID, HID), 'att_r1': glorot(ks[5], (HEADS, HID), HID, HID), 'b1': jnp.zeros((HC,), jnp.float32), 'W2': glorot(ks[6], (HC, HC), HC, HC), 'att_l2': glorot(ks[7], (HEADS, HID), HID, HID), 'att_r2': glorot(ks[8], (HEADS, HID), HID, HID), 'b2': jnp.zeros((HC,), jnp.float32)}
    _L1_gnn_all = _L1_gnn_setup()
    _L1_gnn_in = {k: v for k, v in _L1_gnn_all.items() if k in ('W1', 'att_l1', 'att_r1', 'b1', 'W2', 'att_l2', 'att_r2', 'b2')}
    del _L1_gnn_all

    def _L2_gnn_setup():
        import jax, jax.numpy as jnp
        import numpy as np
        EMBED = 128
        HIDDEN = 256
        N_NODES = 6250
        N_EDGES = 80000
        LN_EPS = 1e-05

        def _layer_norm(x, gamma, beta):
            mu = jnp.mean(x, axis=-1, keepdims=True)
            var = jnp.var(x, axis=-1, keepdims=True)
            return (x - mu) * jax.lax.rsqrt(var + LN_EPS) * gamma + beta
        key = jax.random.key(seed)
        ks = jax.random.split(key, 10)
        node_embeddings = jax.random.normal(ks[0], (N_NODES, EMBED), dtype=jnp.float32)
        edge_embeddings = jax.random.normal(ks[1], (N_EDGES, EMBED), dtype=jnp.float32)
        edge_index_list = jax.random.randint(ks[2], (2, N_EDGES), 0, N_NODES, dtype=jnp.int64 if jax.config.jax_enable_x64 else jnp.int32)
        ln_gamma = jnp.ones((EMBED,), dtype=jnp.float32)
        ln_beta = jnp.zeros((EMBED,), dtype=jnp.float32)
        W1 = jax.random.normal(ks[3], (EMBED, HIDDEN), dtype=jnp.float32) * (1.0 / np.sqrt(EMBED))
        b1 = jnp.zeros((HIDDEN,), dtype=jnp.float32)
        W2 = jax.random.normal(ks[4], (HIDDEN, EMBED), dtype=jnp.float32) * (1.0 / np.sqrt(HIDDEN))
        b2 = jnp.zeros((EMBED,), dtype=jnp.float32)
        Wt = jax.random.normal(ks[5], (EMBED, EMBED), dtype=jnp.float32) * (1.0 / np.sqrt(EMBED))
        bt = jnp.zeros((EMBED,), dtype=jnp.float32)
        return {'node_embeddings': node_embeddings, 'edge_embeddings': edge_embeddings, 'edge_index_list': edge_index_list, 'ln_gamma': ln_gamma, 'ln_beta': ln_beta, 'W1': W1, 'b1': b1, 'W2': W2, 'b2': b2, 'Wt': Wt, 'bt': bt}
    _L2_gnn_all = _L2_gnn_setup()
    _L2_gnn_in = {k: v for k, v in _L2_gnn_all.items() if k in ('ln_gamma', 'ln_beta', 'W1', 'b1', 'W2', 'b2', 'Wt', 'bt')}
    del _L2_gnn_all

    def _L3_gnn_setup():
        import jax, jax.numpy as jnp
        import numpy as np
        N = 12500
        E = 200000
        D = 128
        key = jax.random.key(seed)
        ks = jax.random.split(key, 8)
        return {'x': jax.random.normal(ks[0], (N, D), dtype=jnp.float32), 'W': jax.random.normal(ks[1], (D, D), dtype=jnp.float32) * (1.0 / np.sqrt(D)), 'b': jax.random.normal(ks[2], (D,), dtype=jnp.float32) * 0.01, 'Wres': jax.random.normal(ks[3], (D, D), dtype=jnp.float32) * (1.0 / np.sqrt(D)), 'bres': jax.random.normal(ks[4], (D,), dtype=jnp.float32) * 0.01, 'edge_val': jax.random.uniform(ks[5], (E,), dtype=jnp.float32), 'edge_row': jax.random.randint(ks[6], (E,), 0, N, dtype=jnp.int32), 'edge_col': jax.random.randint(ks[7], (E,), 0, N, dtype=jnp.int32)}
    _L3_gnn_all = _L3_gnn_setup()
    _L3_gnn_in = {k: v for k, v in _L3_gnn_all.items() if k in ('W', 'b', 'Wres', 'bres')}
    del _L3_gnn_all
    return {'x': x, 'src': src, 'dst': dst, 'edge_attr_128': edge_attr_128, 'edge_weight': edge_weight, 'L0_gnn_W': _L0_gnn_in['W'], 'L0_gnn_b': _L0_gnn_in['b'], 'L1_gnn_W1': _L1_gnn_in['W1'], 'L1_gnn_att_l1': _L1_gnn_in['att_l1'], 'L1_gnn_att_r1': _L1_gnn_in['att_r1'], 'L1_gnn_b1': _L1_gnn_in['b1'], 'L1_gnn_W2': _L1_gnn_in['W2'], 'L1_gnn_att_l2': _L1_gnn_in['att_l2'], 'L1_gnn_att_r2': _L1_gnn_in['att_r2'], 'L1_gnn_b2': _L1_gnn_in['b2'], 'L2_gnn_ln_gamma': _L2_gnn_in['ln_gamma'], 'L2_gnn_ln_beta': _L2_gnn_in['ln_beta'], 'L2_gnn_W1': _L2_gnn_in['W1'], 'L2_gnn_b1': _L2_gnn_in['b1'], 'L2_gnn_W2': _L2_gnn_in['W2'], 'L2_gnn_b2': _L2_gnn_in['b2'], 'L2_gnn_Wt': _L2_gnn_in['Wt'], 'L2_gnn_bt': _L2_gnn_in['bt'], 'L3_gnn_W': _L3_gnn_in['W'], 'L3_gnn_b': _L3_gnn_in['b'], 'L3_gnn_Wres': _L3_gnn_in['Wres'], 'L3_gnn_bres': _L3_gnn_in['bres']}

def reference(x, src, dst, edge_attr_128, edge_weight, L0_gnn_W, L0_gnn_b, L1_gnn_W1, L1_gnn_att_l1, L1_gnn_att_r1, L1_gnn_b1, L1_gnn_W2, L1_gnn_att_l2, L1_gnn_att_r2, L1_gnn_b2, L2_gnn_ln_gamma, L2_gnn_ln_beta, L2_gnn_W1, L2_gnn_b1, L2_gnn_W2, L2_gnn_b2, L2_gnn_Wt, L2_gnn_bt, L3_gnn_W, L3_gnn_b, L3_gnn_Wres, L3_gnn_bres):
    import jax
    import jax.numpy as jnp

    def _L0_gnn_ref(H, src, dst, W, b):
        import jax, jax.numpy as jnp
        import numpy as np
        N = 12500
        E = 200000
        D_IN = 128
        D_OUT = 128
        gathered = H[dst]
        agg = jax.ops.segment_max(gathered, src, num_segments=N)
        deg = jax.ops.segment_sum(jnp.ones((src.shape[0],), jnp.float32), src, num_segments=N)
        H_neigh = jnp.where(deg[:, None] > 0, agg, 0.0)
        H_concat = jnp.concatenate([H, H_neigh], axis=1)
        return H_concat @ W.T + b

    def _L1_gnn_ref(x, edge_index, edge_weight, W1, att_l1, att_r1, b1, W2, att_l2, att_r2, b2):
        import jax, jax.numpy as jnp
        import numpy as np
        N = 6250
        E = 100000
        NFEAT = 128
        HID = 32
        HEADS = 4
        SLOPE = 0.2

        def glorot(key, shape, fan_in, fan_out):
            lim = float(np.sqrt(6.0 / (fan_in + fan_out)))
            return jax.random.uniform(key, shape, jnp.float32, -lim, lim)

        def gat_layer(x, src, dst, ew, W, att_l, att_r, b):
            n = x.shape[0]
            h = (x @ W).reshape(n, HEADS, HID)
            a_l = jnp.einsum('nhc,hc->nh', h, att_l)
            a_r = jnp.einsum('nhc,hc->nh', h, att_r)
            e = jax.nn.leaky_relu(a_l[src] + a_r[dst], SLOPE) * ew[:, None]
            m = jax.ops.segment_max(e, dst, num_segments=n)
            m = jnp.where(jnp.isfinite(m), m, 0.0)
            ex = jnp.exp(e - m[dst])
            s = jax.ops.segment_sum(ex, dst, num_segments=n)
            alpha = ex / (s[dst] + 1e-16)
            out = jax.ops.segment_sum(h[src] * alpha[:, :, None], dst, num_segments=n)
            return out.reshape(n, HEADS * HID) + b
        src = edge_index[0]
        dst = edge_index[1]
        h = gat_layer(x, src, dst, edge_weight, W1, att_l1, att_r1, b1)
        logits = gat_layer(h, src, dst, edge_weight, W2, att_l2, att_r2, b2)
        return logits

    def _L2_gnn_ref(node_embeddings, edge_embeddings, edge_index_list, ln_gamma, ln_beta, W1, b1, W2, b2, Wt, bt):
        import jax, jax.numpy as jnp
        import numpy as np
        EMBED = 128
        HIDDEN = 256
        N_NODES = 6250
        N_EDGES = 80000
        LN_EPS = 1e-05

        def _layer_norm(x, gamma, beta):
            mu = jnp.mean(x, axis=-1, keepdims=True)
            var = jnp.var(x, axis=-1, keepdims=True)
            return (x - mu) * jax.lax.rsqrt(var + LN_EPS) * gamma + beta
        n_nodes = node_embeddings.shape[0]
        h = _layer_norm(node_embeddings, ln_gamma, ln_beta)
        center = edge_index_list[0]
        neighbor = edge_index_list[1]
        h_c = h[center]
        h_n = h[neighbor]
        s = edge_embeddings + h_c + h_n
        t = jax.nn.silu(s) @ W1 + b1
        theta_edge = jax.nn.silu(t) @ W2 + b2
        msg = h_n * theta_edge
        agg = jax.ops.segment_sum(msg, center, num_segments=n_nodes)
        out = jax.nn.silu(h + agg) @ Wt + bt
        return out

    def _L3_gnn_ref(x, W, b, Wres, bres, edge_val, edge_row, edge_col):
        import jax, jax.numpy as jnp
        import numpy as np
        N = 12500
        E = 200000
        D = 128
        h = x @ W + b
        msgs = edge_val[:, None] * h[edge_col]
        agg = jax.ops.segment_sum(msgs, edge_row, num_segments=N)
        a = jax.nn.relu(agg)
        out = a + (a @ Wres + bres)
        return out
    edge_index = jnp.stack([src, dst])
    x = _layernorm(x + _L0_gnn_ref(x, src, dst, L0_gnn_W, L0_gnn_b), axis=-1)
    x = _layernorm(x + _L1_gnn_ref(x, edge_index, edge_weight, L1_gnn_W1, L1_gnn_att_l1, L1_gnn_att_r1, L1_gnn_b1, L1_gnn_W2, L1_gnn_att_l2, L1_gnn_att_r2, L1_gnn_b2), axis=-1)
    x = _layernorm(x + _L2_gnn_ref(x, edge_attr_128, edge_index, L2_gnn_ln_gamma, L2_gnn_ln_beta, L2_gnn_W1, L2_gnn_b1, L2_gnn_W2, L2_gnn_b2, L2_gnn_Wt, L2_gnn_bt), axis=-1)
    x = _layernorm(x + _L3_gnn_ref(x, L3_gnn_W, L3_gnn_b, L3_gnn_Wres, L3_gnn_bres, edge_weight, src, dst), axis=-1)
    return x

_drawn_inputs = setup_inputs


def setup_inputs(seed=0):
    import zlib

    import numpy as np

    out = dict(_drawn_inputs(seed))
    spreads = {'L0_gnn_b': (0.0, 0.1),
     'L1_gnn_b1': (0.0, 0.1),
     'L1_gnn_b2': (0.0, 0.1),
     'L2_gnn_ln_gamma': (1.0, 0.2),
     'L2_gnn_ln_beta': (0.0, 0.1),
     'L2_gnn_b1': (0.0, 0.1),
     'L2_gnn_b2': (0.0, 0.1),
     'L2_gnn_bt': (0.0, 0.8)}
    factors = {'L1_gnn_att_r1': 4.708,
     'L1_gnn_att_l2': 8.0,
     'L1_gnn_att_r2': 34.273,
     'L3_gnn_b': 4.949,
     'L3_gnn_bres': 35.829}
    for name, (base, spread) in spreads.items():
        noise = np.random.default_rng([zlib.crc32(name.encode()), seed]).standard_normal(out[name].shape)
        drawn = base * np.exp(spread * noise) if base else spread * noise
        out[name] = jnp.asarray(drawn.astype(out[name].dtype))
    for name, factor in factors.items():
        out[name] = (out[name] * factor).astype(out[name].dtype)
    return out
```

```python
from contextlib import ExitStack

import concourse.bass as bass
from concourse import mybir

ALU = mybir.AluOpType
ACT = mybir.ActivationFunctionType
AX = mybir.AxisListType
F32 = mybir.dt.float32
BF16 = mybir.dt.bfloat16
I32 = mybir.dt.int32
U32 = mybir.dt.uint32

P = 128
N = 12500
E = 200000
D = 128
NT = -(-N // P)
NPAD = NT * P
SPARE = NPAD - 1
HEADS = 4
HID = D // HEADS
LN_EPS = 1e-5
NEG = -3.0e38
LOW = -1.0e30

ROWCH = 16
ROWE = ROWCH * P
EROWS = E // ROWE
ECH = -(-E // P)
TAILCH = ECH - EROWS * ROWCH
TAILE = E - EROWS * ROWE
R = EROWS + 1

CBLK = -(-((ECH * P + NT * (P - 1)) // P) // P)
C = CBLK * P
Q = C * P
U = 4
ITERS = C // (4 * U)
REC = D + 4
ROW = D + HEADS
BASE = 8


def wait_again(eng, sem, value):
    if not (isinstance(value, int) and value <= 0):
        eng.wait_ge(sem, value)


class Sems:

    def __init__(self, nc, ctx, phase):
        self.nc, self.ctx, self.phase, self.all = nc, ctx, phase, []

    def __call__(self, name):
        s = self.ctx.enter_context(self.nc.semaphore(f"{self.phase}_{name}"))
        self.all.append(s)
        return s

    def clear(self):
        with self.nc.Block() as block:
            @block.sync
            def _(sp):
                for s in self.all:
                    sp.sem_clear(s)


class Moves:

    def __init__(self, nc, ctx):
        self.sems = [[ctx.enter_context(nc.semaphore(f"moved{g}_{j}")) for j in range(U)] for g in range(4)]
        self.before = [[0] * U for _ in range(4)]

    def wait(self, eng, i, g, chunks=range(U)):
        for j in chunks:
            eng.wait_ge(self.sems[g][j], i * 16 + (self.before[g][j] + 16))

    def wait_last(self, eng, i, g):
        if not (isinstance(i, int) and i == 0):
            for j in range(U):
                eng.wait_ge(self.sems[g][j], i * 16 + self.before[g][j])

    def close(self, count):
        for g in range(4):
            for j in range(U):
                self.before[g][j] += 16 * count(g, j)


def chain(eng, sem):
    count = [0]

    def link(ins):
        count[0] += 1
        ins.then_inc(sem, 1)
        eng.wait_ge(sem, count[0])
    return link


def spread(ap, n):
    return ap.unsqueeze(2).broadcast_to([ap.shape[0], ap.shape[1], n])


def repeat(ap, n):
    return ap.unsqueeze(1).broadcast_to([ap.shape[0], n, ap.shape[1]])


def build_constants(nc, T):
    with ExitStack() as ctx:
        S = Sems(nc, ctx, "const")
        filled, cut, copied = S("filled"), S("cut"), S("copied")
        with nc.Block() as block:
            @block.gpsimd
            def _(pool):
                pool.memset(T.ident[:, :], 0.0).then_inc(filled, 1)
                pool.memset(T.before[:, :], 1.0).then_inc(filled, 1)
                pool.memset(T.upto[:, :], 1.0).then_inc(filled, 1)
                pool.memset(T.ones[:, :], 1.0).then_inc(filled, 1)
                pool.memset(T.ones_b[:, :], 1.0).then_inc(filled, 1)
                pool.memset(T.zero_b[:, :], 0.0).then_inc(filled, 1)
                pool.wait_ge(filled, 6)
                pool.affine_select(out=T.ident[:, :], in_=T.ident[:, :], compare_op=ALU.not_equal, fill=1.0,
                                   base=0, pattern=[[-1, P]], channel_multiplier=1).then_inc(cut, 1)
                pool.affine_select(out=T.before[:, :], in_=T.before[:, :], compare_op=ALU.is_gt, fill=0.0,
                                   base=0, pattern=[[-1, P]], channel_multiplier=1).then_inc(cut, 1)
                pool.affine_select(out=T.upto[:, :], in_=T.upto[:, :], compare_op=ALU.is_gt, fill=0.0,
                                   base=0, pattern=[[1, P]], channel_multiplier=-1).then_inc(cut, 1)
                pool.iota(T.iota_i[:, :], pattern=[[1, P]], base=0, channel_multiplier=0).then_inc(cut, 1)
                pool.iota(T.part_i[:, :], pattern=[[0, 1]], base=0, channel_multiplier=1).then_inc(cut, 1)
                pool.iota(T.chunk_i[:, :], pattern=[[1, C]], base=0, channel_multiplier=0).then_inc(cut, 1)

            @block.vector
            def _(dve):
                dve.wait_ge(cut, 6)
                nc.vector.tensor_copy(T.iota_b[:, :], T.iota_i[:, :]).then_inc(copied, 1)
                nc.vector.tensor_scalar(T.iota1_f[:, :], T.iota_i[:, :], 1.0, None, ALU.add).then_inc(copied, 1)
                nc.vector.tensor_copy(T.part_f[:, :], T.part_i[:, :]).then_inc(copied, 1)
                nc.vector.tensor_copy(T.ident_b[:, :], T.ident[:, :]).then_inc(copied, 1)
                nc.vector.tensor_scalar(T.ident128_b[:, :], T.ident[:, :], float(P), None, ALU.mult)\
                    .then_inc(copied, 1)
                nc.vector.tensor_copy(T.chunk_f[:, :], T.chunk_i[:, :]).then_inc(copied, 1)
        S.clear()


def build_prepare(nc, T, X):
    with ExitStack() as ctx:
        S = Sems(nc, ctx, "prep")
        dummy, loaded, xin, xout = S("dummy"), S("loaded"), S("xin"), S("xout")
        zero_set, zeroed, dve_at, turned, taken = S("zero_set"), S("zeroed"), S("dve_at"), S("turned"), S("taken")
        src_r = ctx.enter_context(nc.sbuf_tensor("src_r", [R, ROWE], I32))
        dst_r = ctx.enter_context(nc.sbuf_tensor("dst_r", [R, ROWE], I32))
        ew_r = ctx.enter_context(nc.sbuf_tensor("ew_r", [R, ROWE], F32))
        key_f = ctx.enter_context(nc.sbuf_tensor("key_f", [R, ROWE], F32))
        part = ctx.enter_context(nc.sbuf_tensor("part", [R, ROWE], I32))
        col_i = ctx.enter_context(nc.sbuf_tensor("col_i", [P, ROWCH * R], I32))
        zeros = ctx.enter_context(nc.sbuf_tensor("zeros", [P, 16 * REC], F32))
        ps = [ctx.enter_context(nc.psum_tensor(f"ps_prep{k}", [P, 512], F32)) for k in range(2)]
        XR = 100
        xb = ctx.enter_context(nc.sbuf_tensor("xb", [125, XR // 4 * D], F32))
        NB = C // 16
        with nc.Block() as block:
            @block.sync
            def _(sp):
                sp.wait_ge(dummy, 4)
                for t, a in ((src_r, X.src), (dst_r, X.dst), (ew_r, X.edge_weight)):
                    sp.dma_start(t[0:EROWS, :], a[0:EROWS * ROWE].rearrange("(r e) -> r e", e=ROWE))\
                        .then_inc(loaded, 16)
                    sp.dma_start(t[EROWS:R, 0:TAILE], a[EROWS * ROWE:E].rearrange("(r e) -> r e", r=1))\
                        .then_inc(loaded, 16)
                xr, xo = X.x.rearrange("(p k) f -> p (k f)", p=125), X.xpad[0:N, :].rearrange("(p k) f -> p (k f)", p=125)
                w = XR // 4 * D
                for k in range(4):
                    sp.dma_start(xb[:, :], xr[:, k * w:(k + 1) * w]).then_inc(xin, 16)
                    sp.wait_ge(xin, 16 * (k + 1))
                    sp.dma_start(xo[:, k * w:(k + 1) * w], xb[:, :]).then_inc(xout, 16)
                    sp.wait_ge(xout, 16 * (k + 1))
                sp.wait_ge(zero_set, 1)
                sp.dma_start(X.xpad[N:NPAD, :], zeros[0:NPAD - N, 0:D]).then_inc(xout, 16)
                sp.wait_ge(xout, 16 * 5)

            @block.scalar
            def _(act):
                act.wait_ge(zero_set, 1)
                act.dma_start(X.rec_dst.rearrange("(p k) f -> p (k f)", p=P)[:, 0:16 * REC * 3],
                              zeros[:, :].unsqueeze(1).broadcast_to([P, 3, 16 * REC])).then_inc(zeroed, 16)
                act.dma_start(X.rec_dst.rearrange("(p k) f -> p (k f)", p=P)[:, 16 * REC * 3:4 * C],
                              zeros[:, 0:4 * C - 16 * REC * 3]).then_inc(zeroed, 16)
                rows = X.rec_src.rearrange("(p b k) f -> b p (k f)", p=P, k=16)
                with act.Fori(0, NB) as b:
                    act.dma_start(rows[bass.ds(b, 1)].squeeze(0), zeros[:, :]).then_inc(zeroed, 16)
                act.wait_ge(zeroed, 16 * (NB + 2))

            @block.vector
            def _(dve):
                nc.vector.memset(src_r[:, :], SPARE).then_inc(dummy, 1)
                nc.vector.memset(dst_r[:, :], SPARE).then_inc(dummy, 1)
                nc.vector.memset(ew_r[:, :], 0.0).then_inc(dummy, 1)
                nc.vector.memset(zeros[:, :], 0.0).then_inc(zero_set, 1)
                nc.vector.memset(T.meta_src[:, :, :, :], 0.0).then_inc(dummy, 1)
                nc.vector.memset(T.meta_dst[:, :, :, :], 0.0).then_inc(dve_at, 1)
                link_n = [1]

                def link(ins):
                    link_n[0] += 1
                    ins.then_inc(dve_at, 1)
                    dve.wait_ge(dve_at, link_n[0])
                dve.wait_ge(loaded, 16 * 6)
                dve.wait_ge(dummy, 4)
                dve.wait_ge(dve_at, 1)
                for k_r, lo_b, hi_b, col, hicol, mine, other in (
                        (src_r, T.slo_b, T.shi_b, T.scol, T.shicol, T.meta_src, T.meta_dst),
                        (dst_r, T.dlo_b, T.dhi_b, T.dcol, T.dhicol, T.meta_dst, T.meta_src)):
                    n = 0 if k_r is src_r else 1
                    link(nc.vector.tensor_scalar(part[:, :], k_r[:, :], P - 1, None, ALU.bitwise_and))
                    link(nc.vector.tensor_copy(lo_b[:, :], part[:, :]))
                    link(nc.vector.tensor_scalar(part[:, :], k_r[:, :], 7, None, ALU.logical_shift_right))
                    link(nc.vector.tensor_copy(hi_b[:, :], part[:, :]))
                    if n:
                        dve.wait_ge(turned, 4)
                    link(nc.vector.tensor_copy(key_f[:, :], k_r[:, :]))
                    for g in range(4):
                        dve.wait_ge(turned, 4 * n + g + 1)
                        nc.vector.tensor_copy(col[:, g * 4 * R:(g + 1) * 4 * R], ps[g % 2][:, 0:4 * R])\
                            .then_inc(taken, 1)
                    dve.wait_ge(taken, 4 * n + 4)
                    link(nc.vector.tensor_copy(col_i[:, :], col[:, :]))
                    flat = mine[:, :, :, :].rearrange("p b r f -> p (b r) f")
                    link(nc.vector.tensor_scalar(flat[:, :, 3], col[:, :], 1.0, None, ALU.add))
                    link(nc.vector.tensor_copy(other[:, :, :, :].rearrange("p b r f -> p (b r) f")[:, :, 0],
                                               col[:, :]))
                    link(nc.vector.tensor_scalar(part2 := T.colp[:, :], col_i[:, :], P - 1, None, ALU.bitwise_and))
                    link(nc.vector.tensor_scalar(flat[:, :, 2], part2, 1.0, None, ALU.add))
                    link(nc.vector.tensor_scalar(part2, col_i[:, :], 7, None, ALU.logical_shift_right))
                    link(nc.vector.tensor_copy(hicol[:, :], part2))
                for g in range(4):
                    dve.wait_ge(turned, 8 + g + 1)
                    for m, meta in enumerate((T.meta_src, T.meta_dst)):
                        ins = nc.vector.tensor_copy(meta[:, 4 * g:4 * g + 4, :, 1],
                                                    ps[g % 2][:, 0:4 * R].rearrange("p (b r) -> p b r", r=R))
                    ins.then_inc(taken, 1)

            @block.tensor
            def _(pe):
                pe.wait_ge(loaded, 16 * 6)
                for n, rows in enumerate((key_f, key_f, ew_r)):
                    if n < 2:
                        pe.wait_ge(dve_at, (6, 6 + 7 + 5)[n])
                    for g in range(4):
                        u = 4 * n + g
                        if u >= 2:
                            pe.wait_ge(taken, u - 1)
                        for j in range(4):
                            b = 4 * g + j
                            ins = nc.tensor.transpose(ps[g % 2][:, j * R:(j + 1) * R], rows[:, b * P:(b + 1) * P],
                                                      T.ident[0:R, 0:R])
                        ins.then_inc(turned, 1)
        S.clear()


def build_histogram(nc, T):
    with ExitStack() as ctx:
        S = Sems(nc, ctx, "hist")
        hot_ready, counted, stored = S("hot_ready"), S("counted"), S("stored")
        hot_lo = [ctx.enter_context(nc.sbuf_tensor(f"hist_lo{k}", [P, U, P], BF16)) for k in range(2)]
        hot_hi = [ctx.enter_context(nc.sbuf_tensor(f"hist_hi{k}", [P, U, NT], BF16)) for k in range(2)]
        ps = [ctx.enter_context(nc.psum_tensor(f"ps_hist{k}", [P, 512], F32)) for k in range(2)]
        metas, hicols = (T.meta_src, T.meta_dst), (T.shicol, T.dhicol)

        def units(eng, unit):
            with eng.Fori(0, EROWS) as i:
                for g in range(4):
                    for k in range(2):
                        unit(k, i, g, U, i * 8 + (2 * g + k))
            for g in range(-(-TAILCH // U)):
                for k in range(2):
                    unit(k, EROWS, g, min(U, TAILCH - U * g), EROWS * 8 + 2 * g + k)
        NU = EROWS * 8 + 2 * -(-TAILCH // U)

        with nc.Block() as block:
            @block.vector
            def _(dve):
                def unit(k, i, g, m, n):
                    dve.wait_ge(counted, n + 1)
                    lo = metas[k][:, 4 * g:4 * g + m, bass.ds(i, 1), 2].squeeze(2)
                    hi = hicols[k][:, :].rearrange("p (b r) -> p b r", r=R)[:, 4 * g:4 * g + m, bass.ds(i, 1)].squeeze(2)
                    nc.vector.tensor_tensor(hot_lo[k][:, 0:m, :], repeat(T.iota1_f[:, :], m), spread(lo, P),
                                            ALU.is_equal)
                    nc.vector.tensor_tensor(hot_hi[k][:, 0:m, :], repeat(T.iota_b[:, 0:NT], m), spread(hi, NT),
                                            ALU.is_equal).then_inc(hot_ready, 1)
                units(dve, unit)
                for k, h in enumerate((T.hist_s, T.hist_d)):
                    dve.wait_ge(counted, NU + 2)
                    nc.vector.tensor_copy(h[:, :], ps[k][:, 0:NT]).then_inc(stored, 1)

            @block.tensor
            def _(pe):
                pe.sem_inc(counted, 2)
                for k in range(2):
                    nc.tensor.matmul(ps[k][:, 0:NT], T.ident_b[:, :], T.zero_b[:, 0:NT], start=True, stop=False,
                                     skip_group_check=True)

                def unit(k, i, g, m, n):
                    pe.wait_ge(hot_ready, n + 1)
                    for j in range(m):
                        ins = nc.tensor.matmul(ps[k][:, 0:NT], hot_lo[k][:, j, :], hot_hi[k][:, j, :],
                                               start=False, stop=False, skip_group_check=True)
                    ins.then_inc(counted, 1)
                units(pe, unit)
        S.clear()


def build_offsets(nc, T):
    with ExitStack() as ctx:
        S = Sems(nc, ctx, "offs")
        dve_at, pe_at = S("dve_at"), S("pe_at")
        cnt_i = ctx.enter_context(nc.sbuf_tensor("cnt_i", [P, NT], I32))
        cnt_j = ctx.enter_context(nc.sbuf_tensor("cnt_j", [P, NT], I32))
        ch = ctx.enter_context(nc.sbuf_tensor("ch", [P, NT + 1], F32))
        upto_ch = ctx.enter_context(nc.sbuf_tensor("upto_ch", [P, NT + 1], F32))
        first_ch = ctx.enter_context(nc.sbuf_tensor("first_ch", [P, 1], F32))
        reached = ctx.enter_context(nc.sbuf_tensor("reached", [P, C], BF16))
        tile_f = ctx.enter_context(nc.sbuf_tensor("tile_f", [1, C], F32))
        pc = ctx.enter_context(nc.psum_tensor("ps_cnt", [P, 512], F32))
        pp = ctx.enter_context(nc.psum_tensor("ps_pre", [P, 512], F32))
        pf = ctx.enter_context(nc.psum_tensor("ps_fst", [P, 512], F32))
        NW = -(-C // 512)
        pt = [ctx.enter_context(nc.psum_tensor(f"ps_til{k}", [P, 512], F32)) for k in range(NW)]
        STEPS = 11 + NW
        with nc.Block() as block:
            @block.vector
            def _(dve):
                link = chain(dve, dve_at)
                for k, (h, first, tiles) in enumerate(((T.hist_s, T.first_s, T.tile_s), (T.hist_d, T.first_d, T.tile_d))):
                    dve.wait_ge(pe_at, 3 * k + 1)
                    link(nc.vector.tensor_scalar(cnt_i[:, :], pc[:, 0:NT], float(P - 1), None, ALU.add))
                    link(nc.vector.tensor_scalar(cnt_j[:, :], cnt_i[:, :], 7, None, ALU.logical_shift_right))
                    link(nc.vector.memset(ch[:, 0:1], 0.0))
                    link(nc.vector.tensor_copy(ch[:, 1:NT + 1], cnt_j[:, :]))
                    link(nc.vector.tensor_tensor_scan(upto_ch[:, :], ch[:, :], ch[:, :], 0.0, ALU.add, ALU.max))
                    link(nc.vector.scalar_tensor_tensor(out=first[:, :], in0=upto_ch[:, 0:NT], scalar=float(P),
                                                        in1=pp[:, 0:NT], op0=ALU.mult, op1=ALU.add))
                    dve.wait_ge(pe_at, 3 * k + 2)
                    link(nc.vector.tensor_copy(first_ch[0:NT, :], pf[0:NT, 0:1]))
                    link(nc.vector.tensor_scalar(reached[0:NT, :], T.chunk_f[0:NT, :], first_ch[0:NT, 0:1], None, ALU.is_ge))
                    dve.wait_ge(pe_at, 3 * k + 3)
                    for w in range(NW):
                        a, b = w * 512, min(C, w * 512 + 512)
                        link(nc.vector.tensor_scalar(tile_f[0:1, a:b], pt[w][0:1, 0:b - a], -1.0, None, ALU.add))
                    link(nc.vector.tensor_copy(tiles[:, :], tile_f[:, :]))

            @block.tensor
            def _(pe):
                for k, h in enumerate((T.hist_s, T.hist_d)):
                    if k:
                        pe.wait_ge(dve_at, 9 + NW)
                    nc.tensor.matmul(pc[:, 0:NT], T.ones[:, :], h[:, :], start=True, stop=True)
                    nc.tensor.matmul(pp[:, 0:NT], T.upto[:, :], h[:, :], start=True, stop=True).then_inc(pe_at, 1)
                    pe.wait_ge(dve_at, (9 + NW) * k + 5)
                    nc.tensor.matmul(pf[0:NT, 0:1], upto_ch[0:1, 0:NT], T.ones[0:1, 0:1], start=True, stop=True)\
                        .then_inc(pe_at, 1)
                    pe.wait_ge(dve_at, (9 + NW) * k + 8)
                    for w in range(NW):
                        a, b = w * 512, min(C, w * 512 + 512)
                        ins = nc.tensor.matmul(pt[w][0:1, 0:b - a], T.ones_b[0:NT, 0:1], reached[0:NT, a:b],
                                               start=True, stop=True)
                    ins.then_inc(pe_at, 1)
        S.clear()


def build_place(nc, T, X, by_src):
    name = "pls" if by_src else "pld"
    lo_b, hi_b = (T.slo_b, T.shi_b) if by_src else (T.dlo_b, T.dhi_b)
    col, hicol = (T.scol, T.shicol) if by_src else (T.dcol, T.dhicol)
    meta, first = (T.meta_src, T.first_s) if by_src else (T.meta_dst, T.first_d)
    width = REC if by_src else 4
    target = X.rec_src if by_src else X.rec_dst
    TAILU = -(-TAILCH // U)
    with ExitStack() as ctx:
        S = Sems(nc, ctx, name)
        rows_ready, rows_free, hot_ready = S("rows_ready"), S("rows_free"), S("hot_ready")
        table_at, table_read, slots_ready = S("table_at"), S("table_read"), S("slots_ready")
        at_read, at_summed = S("at_read"), S("at_summed")
        meta_ready, pool_step = S("meta_ready"), S("pool_step")
        attr_in = [S(f"attr_in{k}") for k in range(4)]

        def sb(n, shape, dt):
            return ctx.enter_context(nc.sbuf_tensor(f"{name}_{n}", shape, dt))

        def pb(n):
            return ctx.enter_context(nc.psum_tensor(f"{name}_{n}", [P, 512], F32))
        lo_hot = [sb(f"lo_hot{k}", [P, U, P], BF16) for k in range(2)]
        hi_hot = [sb(f"hi_hot{k}", [P, U, NT], BF16) for k in range(2)]
        hi_f = [sb(f"hi_f{k}", [P, U, NT], F32) for k in range(2)]
        lo_hot_t = [sb(f"lo_hot_t{k}", [P, U * P], F32) for k in range(2)]
        same = [sb(f"same{k}", [P, U, P], BF16) for k in range(2)]
        rank = [sb(f"rank{k}", [P, U], F32) for k in range(2)]
        at = [sb(f"at{k}", [P, U], F32) for k in range(2)]
        slot = [sb(f"slot{k}", [P, U], U32) for k in range(4)]
        rec = [sb(f"rec{k}", [P, U, width], F32) for k in range(4)]
        table = [sb(f"table{k}", [P, NT], F32) for k in range(2)]
        ps_lo = [pb(f"ps_lo{k}") for k in range(2)]
        ps_key = [pb(f"ps_key{k}") for k in range(2)]
        ps_at = [pb(f"ps_at{k}") for k in range(2)]
        ps_table = pb("ps_table")

        def turns(eng, unit):
            for g in range(4):
                unit(0, g, U)
            with eng.Fori(1, EROWS) as i:
                for g in range(4):
                    unit(i, g, U)
            for g in range(TAILU):
                unit(EROWS, g, min(U, TAILCH - U * g))

        with nc.Block() as block:
            @block.sync
            def _(sp):
                if by_src:
                    def unit(i, g, m):
                        T.moves.wait_last(sp, i, g)
                        rows = X.edge_attr_128[bass.ds(i * ROWE + g * U * P, m * P), :]
                        sp.dma_start(rec[g][:, 0:m, 0:D], rows.rearrange("(j e) f -> e j f", e=P)).then_inc(attr_in[g], 16)
                    for g in range(4):
                        unit(0, g, U)
                    with sp.Fori(1, EROWS) as i:
                        for g in range(4):
                            unit(i, g, U)
                    for g in range(TAILU):
                        m = min(U, TAILCH - U * g)
                        if (EROWS * ROWCH + U * g + m) * P <= E:
                            unit(EROWS, g, m)
                        else:
                            a = EROWS * ROWE + g * U * P
                            full = (E - a) // P
                            T.moves.wait_last(sp, EROWS, g)
                            sp.dma_start(rec[g][:, 0:full, 0:D], X.edge_attr_128[a:a + full * P, :]
                                         .rearrange("(j e) f -> e j f", e=P)).then_inc(attr_in[g], 16)
                            sp.dma_start(rec[g][0:E - a - full * P, full, 0:D], X.edge_attr_128[a + full * P:E, :])\
                                .then_inc(attr_in[g], 16)

            @block.gpsimd
            def _(pool):

                def unit(i, g, m):
                    pool.wait_ge(slots_ready, i * 4 + (g + 1))
                    pool.wait_ge(meta_ready, i * 4 + (g + 1))
                    if by_src:
                        pool.wait_ge(attr_in[g], i * 16 + (16 if m == U else 32))
                    pool.sem_inc(pool_step, 1)
                    for j in range(m):
                        pool.indirect_dma_start(target[:, :], bass.IndirectOffsetOnAxis(ap=slot[g][:, j:j + 1], axis=0),
                                                rec[g][:, j, :], None).then_inc(T.moves.sems[g][j], 16)
                turns(pool, unit)
                for g in range(4):
                    tail = range(max(0, min(U, TAILCH - U * g)))
                    T.moves.wait(pool, EROWS, g, tail)
                    T.moves.wait(pool, EROWS - 1, g, range(len(tail), U))

            @block.scalar
            def _(act):
                def unit(i, g, m):
                    T.moves.wait_last(act, i, g)
                    nc.scalar.copy(rec[g][:, 0:m, width - 4:width],
                                   meta[:, 4 * g:4 * g + m, bass.ds(i, 1), :].squeeze(2)).then_inc(meta_ready, 1)
                    for j in range(m):
                        n = i * ROWCH + (U * g + j)
                        act.wait_ge(table_at, n + BASE)
                        nc.scalar.copy(table[j % 2][:, :], ps_table[:, 0:NT]).then_inc(table_read, 1)
                turns(act, unit)

            @block.vector
            def _(dve):
                dve.sem_inc(rows_free, 2)
                dve.sem_inc(at_read, 2)

                def front(i, g, m):
                    k = g % 2
                    n = i * 4 + g
                    dve.wait_ge(table_at, i * ROWCH + (U * (g - 1) + BASE))
                    lo = meta[:, 4 * g:4 * g + m, bass.ds(i, 1), 2].squeeze(2)
                    hi = hicol[:, :].rearrange("p (b r) -> p b r", r=R)[:, 4 * g:4 * g + m, bass.ds(i, 1)].squeeze(2)
                    nc.vector.tensor_tensor(lo_hot[k][:, 0:m, :], repeat(T.iota1_f[:, :], m), spread(lo, P), ALU.is_equal)
                    nc.vector.tensor_tensor(hi_hot[k][:, 0:m, :], repeat(T.iota_b[:, 0:NT], m), spread(hi, NT), ALU.is_equal)
                    dve.wait_ge(rows_ready, n + 1)
                    nc.vector.tensor_scalar(lo_hot_t[k][:, 0:m * P], ps_lo[k][:, 0:m * P], T.part_f[:, 0:1], None,
                                            ALU.is_equal).then_inc(hot_ready, 1)
                    wait_again(dve, slots_ready, i * 4 + (g - 1))
                    for j in range(m):
                        ins = nc.vector.scalar_tensor_tensor(
                            out=same[k][:, j, :], in0=ps_key[k][:, j * P:(j + 1) * P],
                            scalar=col[:, :].rearrange("p (b r) -> p b r", r=R)[:, 4 * g + j, bass.ds(i, 1)],
                            in1=T.before[:, :], op0=ALU.is_equal, op1=ALU.mult, accum_out=rank[k][:, j:j + 1])
                    ins.then_inc(rows_free, 1)

                def back(i, g, m):
                    k = g % 2
                    dve.wait_ge(table_at, i * ROWCH + (U * g + m + BASE))
                    read = ps_at[k][:, 0:m * NT].rearrange("p (j t) -> p j t", t=NT)
                    nc.vector.tensor_tensor(hi_f[k][:, 0:m, :], hi_hot[k][:, 0:m, :], read, ALU.mult).then_inc(at_read, 1)
                    dve.wait_ge(at_read, i * 4 + (g + 3))
                    nc.vector.tensor_reduce(at[k][:, 0:m], hi_f[k][:, 0:m, :], AX.X, ALU.add).then_inc(at_summed, 1)
                    dve.wait_ge(at_summed, i * 4 + (g + 1))
                    dve.wait_ge(rows_free, i * 4 + (g + 3))
                    T.moves.wait_last(dve, i, g)
                    nc.vector.tensor_tensor(slot[g][:, 0:m], at[k][:, 0:m], rank[k][:, 0:m], ALU.add)\
                        .then_inc(slots_ready, 1)

                front(0, 0, U)
                for g in range(4):
                    front((g + 1) // 4, (g + 1) % 4, U)
                    back(0, g, U)
                with dve.Fori(1, EROWS) as i:
                    for g in range(4):
                        front(i + (g + 1) // 4, (g + 1) % 4, U)
                        back(i, g, U)
                for g in range(TAILU):
                    if g + 1 < TAILU:
                        front(EROWS, g + 1, min(U, TAILCH - U * (g + 1)))
                    back(EROWS, g, min(U, TAILCH - U * g))

            @block.tensor
            def _(pe):
                pe.sem_inc(table_at, BASE - 1)
                nc.tensor.matmul(ps_table[:, 0:NT], T.ident[:, :], first[:, :], start=True, stop=False,
                                 skip_group_check=True).then_inc(table_at, 1)

                def rows(i, g, m):
                    k = g % 2
                    pe.wait_ge(rows_free, i * 4 + (g + 1))
                    pick = T.ident_b[0:R, bass.ds(i, 1)].broadcast_to([R, P])
                    pick128 = T.ident128_b[0:R, bass.ds(i, 1)].broadcast_to([R, P])
                    a, b = g * U * P, (g * U + m) * P
                    nc.tensor.matmul(ps_lo[k][:, 0:m * P], pick, lo_b[:, a:b], start=True, stop=True)
                    nc.tensor.matmul(ps_key[k][:, 0:m * P], pick, lo_b[:, a:b], start=True, stop=False)
                    nc.tensor.matmul(ps_key[k][:, 0:m * P], pick128, hi_b[:, a:b], start=False, stop=True)\
                        .then_inc(rows_ready, 1)

                def unit(i, g, m):
                    k = g % 2
                    pe.wait_ge(hot_ready, i * 4 + (g + 1))
                    pe.wait_ge(at_read, i * 4 + (g + 1))
                    for j in range(m):
                        pe.wait_ge(table_read, i * ROWCH + (U * g + j + 1))
                        nc.tensor.matmul(ps_at[k][:, j * NT:(j + 1) * NT], lo_hot_t[k][:, j * P:(j + 1) * P],
                                         table[j % 2][:, :], start=True, stop=True)
                        nc.tensor.matmul(ps_table[:, 0:NT], lo_hot[k][:, j, :], hi_hot[k][:, j, :], start=False,
                                         stop=False, skip_group_check=True).then_inc(table_at, 1)
                rows(0, 0, U)
                with pe.Fori(0, EROWS) as i:
                    for g in range(4):
                        rows(i + (g + 1) // 4, (g + 1) % 4, U)
                        unit(i, g, U)
                for g in range(TAILU):
                    if g + 1 < TAILU:
                        rows(EROWS, g + 1, min(U, TAILCH - U * (g + 1)))
                    unit(EROWS, g, min(U, TAILCH - U * g))
        T.moves.close(lambda g, j: EROWS + (U * g + j < TAILCH))
        S.clear()


NU = C // U


def turns(eng, unit, depth=4, count=ITERS):
    for g in range(depth):
        unit(0, g)
    with eng.Fori(1, count - 1) as i:
        for g in range(depth):
            unit(i, g)
    for g in range(depth):
        unit(count - 1, g)


def near(i, g, k, depth=4, count=ITERS):
    j, h = i + (g + k) // depth, (g + k) % depth
    return None if isinstance(j, int) and not 0 <= j < count else (j, h)


def tiles_of(nc, eng_type, row, i, g):
    return nc.values_load_multi_w_load_instructions(row[0:1, bass.ds(i * 4 * U + g * U, U)], engines=[eng_type],
                                                    min_val=0, max_val=NT - 1,
                                                    skip_runtime_bounds_check_because="tiles are counted below NT")[1]


def build_flags(nc, T, X, by_src):
    name = "fls" if by_src else "fld"
    m, last, rec, keys, reset = ((T.m_src, T.last_src, X.rec_src, X.keys_src, X.reset_src) if by_src else
                                 (T.m_dst, T.last_dst, X.rec_dst, X.keys_dst, X.reset_dst))
    at = D if by_src else 0
    with ExitStack() as ctx:
        S = Sems(nc, ctx, name)
        loaded, turned, taken, stored, shifted, done, dve_at, guard = (
            S("loaded"), S("turned"), S("taken"), S("stored"), S("shifted"), S("done"), S("dve_at"), S("guard"))
        kt = ctx.enter_context(nc.sbuf_tensor(name + "_kt", [P, CBLK, P], F32))
        prev = ctx.enter_context(nc.sbuf_tensor(name + "_prev", [P, CBLK, P], F32))
        nxt = ctx.enter_context(nc.sbuf_tensor(name + "_next", [P, CBLK, P], F32))
        rs = ctx.enter_context(nc.sbuf_tensor(name + "_rs", [P, CBLK, P], BF16))
        edge = ctx.enter_context(nc.sbuf_tensor(name + "_edge", [1, 2], F32))
        ps = [ctx.enter_context(nc.psum_tensor(f"{name}_ps{k}", [P, 512], F32)) for k in range(4)]
        groups = [range(a, min(a + 4, CBLK)) for a in range(0, CBLK, 4)]
        with nc.Block() as block:
            @block.sync
            def _(sp):
                sp.dma_start(m[:, :, :], rec.rearrange("(c p) f -> p c f", p=P)[:, :, at:at + 4]).then_inc(loaded, 16)
                sp.wait_ge(guard, 1)
                sp.dma_start(keys[0:1].unsqueeze(0), edge[:, 0:1]).then_inc(stored, 16)
                sp.dma_start(keys[Q + 1:Q + 2].unsqueeze(0), edge[:, 1:2]).then_inc(stored, 16)
                sp.wait_ge(taken, len(groups))
                view = "(b c p) -> c b p"
                sp.dma_start(keys[1:Q + 1].rearrange(view, b=CBLK, c=P), kt[:, :, :]).then_inc(stored, 16)
                sp.wait_ge(stored, 48)
                sp.dma_start(prev[:, :, :], keys[0:Q].rearrange(view, b=CBLK, c=P)).then_inc(shifted, 16)
                sp.dma_start(nxt[:, :, :], keys[2:Q + 2].rearrange(view, b=CBLK, c=P)).then_inc(shifted, 16)
                sp.wait_ge(dve_at, 3)
                sp.dma_start(reset.rearrange(view, b=CBLK, c=P), rs[:, :, :]).then_inc(done, 16)
                sp.wait_ge(done, 16)

            @block.vector
            def _(dve):
                nc.vector.memset(edge[:, :], -1.0).then_inc(guard, 1)
                for n, blocks in enumerate(groups):
                    dve.wait_ge(turned, n + 1)
                    w = len(blocks) * P
                    nc.vector.tensor_copy(kt[:, blocks[0]:blocks[0] + len(blocks), :],
                                          ps[n][:, 0:w].rearrange("c (b p) -> c b p", p=P)).then_inc(taken, 1)
                dve.wait_ge(taken, len(groups))
                dve.wait_ge(shifted, 32)
                link = chain(dve, dve_at)
                link(nc.vector.tensor_tensor(prev[:, :, :], prev[:, :, :], kt[:, :, :], ALU.not_equal))
                if by_src:
                    link(nc.vector.tensor_scalar(rs[:, :, :], prev[:, :, :], NEG, None, ALU.mult))
                    link(nc.vector.tensor_tensor(nxt[:, :, :], nxt[:, :, :], kt[:, :, :], ALU.not_equal))
                    link(nc.vector.tensor_copy(kt[:, :, :], nxt[:, :, :]))
                else:
                    link(nc.vector.tensor_scalar(rs[:, :, :], prev[:, :, :], NEG, None, ALU.mult))
                    link(nc.vector.memset(rs[:, :, 0:1], NEG))
                    link(nc.vector.tensor_tensor(nxt[:, :, :], nxt[:, :, :], kt[:, :, :], ALU.not_equal))
                    link(nc.vector.memset(nxt[:, :, P - 1:P], 1.0))
                for n, blocks in enumerate(groups):
                    dve.wait_ge(turned, len(groups) + n + 1)
                    a, b = blocks[0] * P, (blocks[-1] + 1) * P
                    link(nc.vector.tensor_tensor(last[:, a:b], ps[n][:, 0:b - a], m[:, a:b, 2], ALU.mult))

            @block.tensor
            def _(pe):
                pe.wait_ge(loaded, 16)
                for n, blocks in enumerate(groups):
                    for j, b in enumerate(blocks):
                        ins = nc.tensor.transpose(ps[n][:, j * P:(j + 1) * P], m[:, b * P:(b + 1) * P, 3], T.ident[:, :])
                    ins.then_inc(turned, 1)
                pe.wait_ge(dve_at, 4 if by_src else 5)
                for n, blocks in enumerate(groups):
                    for j, b in enumerate(blocks):
                        ins = nc.tensor.transpose(ps[n][:, j * P:(j + 1) * P], nxt[:, b, :], T.ident[:, :])
                    ins.then_inc(turned, 1)
        S.clear()


def build_max_edges(nc, T, X):
    with ExitStack() as ctx:
        S = Sems(nc, ctx, "mx")
        idx_ready, turned, scanned, back, vals_ready = S("idx_ready"), S("turned"), S("scanned"), S("back"), S("vals_ready")
        hot_ready, picked, added, pool_step = S("hot_ready"), S("picked"), S("added"), S("pool_step")
        cleared = S("cleared")
        reset_in = [S(f"reset_in{k}") for k in range(4)]

        def sb(n, shape, dt=F32):
            return ctx.enter_context(nc.sbuf_tensor("mx_" + n, shape, dt))

        def pb(n):
            return ctx.enter_context(nc.psum_tensor("mx_" + n, [P, 512], F32))
        idx = [sb(f"idx{k}", [P, U], U32) for k in range(4)]
        rows = [sb(f"rows{k}", [P, U, D]) for k in range(4)]
        reset = [sb(f"reset{k}", [P, U * P], BF16) for k in range(4)]
        run = [sb(f"run{k}", [P, U * P]) for k in range(2)]
        vals = [sb(f"vals{k}", [P, U * D]) for k in range(2)]
        hot = [sb(f"hot{k}", [P, U, P]) for k in range(2)]
        ps_x, ps_b, ps_n = ([pb(f"ps_{n}{k}") for k in range(2)] for n in "xbn")

        with nc.Block() as block:
            @block.gpsimd
            def _(pool):
                def unit(i, g):
                    pool.wait_ge(idx_ready, i * 4 + (g + 1))
                    wait_again(pool, turned, i * 4 + (g - 3))
                    pool.sem_inc(pool_step, 1)
                    for j in range(U):
                        pool.indirect_dma_start(rows[g][:, j, :], None, X.xpad[:, :],
                                                bass.IndirectOffsetOnAxis(ap=idx[g][:, j:j + 1], axis=0))\
                            .then_inc(T.moves.sems[g][j], 16)
                turns(pool, unit)

            @block.sync
            def _(sp):
                def unit(i, g):
                    wait_again(sp, scanned, i * 4 + (g - 3))
                    sp.dma_start(reset[g][:, :], X.reset_src[bass.ds(i * 4 * U * P + g * U * P, U * P)]
                                 .partition_broadcast(P)).then_inc(reset_in[g], 16)
                turns(sp, unit)

            @block.vector
            def _(dve):
                nc.vector.memset(T.acc[:, :], 0.0).then_inc(cleared, 1)

                def take_index(i, g):
                    T.moves.wait_last(dve, i, g)
                    nc.vector.tensor_copy(idx[g][:, :], T.m_src[:, bass.ds(i * 4 * U + g * U, U), 0]).then_inc(idx_ready, 1)

                def add(i, g):
                    tiles = tiles_of(nc, mybir.EngineType.DVE, T.tile_s, i, g)
                    dve.wait_ge(picked, i * 4 + (g + 1))
                    for j in range(U):
                        wait_again(dve, added, i * 16 + (U * g + j))
                        to = T.acc[:, bass.ds(tiles[j] * ROW, D)]
                        nc.vector.tensor_tensor(to, to, ps_n[g % 2][:, j * D:(j + 1) * D], ALU.add).then_inc(added, 1)

                for g in range(3):
                    take_index(0, g)
                dve.wait_ge(cleared, 1)

                def unit(i, g):
                    if then := near(i, g, 3):
                        take_index(*then)
                    n = i * 4 + g
                    dve.wait_ge(reset_in[g], i * 16 + 16)
                    dve.wait_ge(turned, n + 1)
                    wait_again(dve, back, n - 1)
                    wait_again(dve, scanned, n)
                    first = 0.0 if isinstance(i, int) and n == 0 else run[(g - 1) % 2][:, U * P - 1:U * P]
                    nc.vector.tensor_tensor_scan(run[g % 2][:, :], reset[g][:, :], ps_x[g % 2][:, :], first,
                                                 ALU.add, ALU.max).then_inc(scanned, 1)
                    wait_again(dve, picked, n - 1)
                    nc.vector.tensor_tensor(hot[g % 2][:, :, :], repeat(T.iota1_f[:, :], U),
                                            spread(T.last_src[:, bass.ds(i * 4 * U + g * U, U)], P),
                                            ALU.is_equal).then_inc(hot_ready, 1)
                    if past := near(i, g, -2):
                        add(*past)
                turns(dve, unit)
                add(ITERS - 1, 2)
                add(ITERS - 1, 3)

            @block.scalar
            def _(act):
                def unit(i, g):
                    n = i * 4 + g
                    act.wait_ge(back, n + 1)
                    wait_again(act, picked, n - 1)
                    nc.scalar.copy(vals[g % 2][:, :], ps_b[g % 2][:, :]).then_inc(vals_ready, 1)
                turns(act, unit)

            @block.tensor
            def _(pe):
                def turn(i, g):
                    wait_again(pe, scanned, i * 4 + (g - 1))
                    for j in range(U):
                        T.moves.wait(pe, i, g, [j])
                        ins = nc.tensor.transpose(ps_x[g % 2][:, j * P:(j + 1) * P], rows[g][:, j, :], T.ident[:, :])
                    ins.then_inc(turned, 1)

                def turn_back(i, g):
                    pe.wait_ge(scanned, i * 4 + (g + 1))
                    wait_again(pe, vals_ready, i * 4 + (g - 1))
                    for j in range(U):
                        ins = nc.tensor.transpose(ps_b[g % 2][:, j * D:(j + 1) * D], run[g % 2][:, j * P:(j + 1) * P],
                                                  T.ident[:, :])
                    ins.then_inc(back, 1)

                def pick(i, g):
                    pe.wait_ge(vals_ready, i * 4 + (g + 1))
                    pe.wait_ge(hot_ready, i * 4 + (g + 1))
                    wait_again(pe, added, i * 16 + (U * (g - 1)))
                    for j in range(U):
                        ins = nc.tensor.matmul(ps_n[g % 2][:, j * D:(j + 1) * D], hot[g % 2][:, j, :],
                                               vals[g % 2][:, j * D:(j + 1) * D], start=True, stop=True)
                    ins.then_inc(picked, 1)

                turn(0, 0)

                def unit(i, g):
                    if then := near(i, g, 1):
                        turn(*then)
                    turn_back(i, g)
                    if past := near(i, g, -1):
                        pick(*past)
                turns(pe, unit)
                pick(ITERS - 1, 3)
        T.moves.close(lambda g, j: ITERS)
        S.clear()


def build_gat_edges(nc, T, X, name):
    with ExitStack() as ctx:
        S = Sems(nc, ctx, name)
        (idx_ready, hot_ready, hot_turned, hot_copied, ar_read, z_ready, leaky_ready, logit_ready, turned, scanned,
         back, peaks_ready, peaks_picked, mask_ready, mask_used, m_ready, m_step, scale_ready, m_read, w_ready, ex_ready, hx_ready,
         summed, scaled, added, pool_step, cleared) = (S(n) for n in (
             "idx_ready", "hot_ready", "hot_turned", "hot_copied", "ar_read", "z_ready", "leaky_ready", "logit_ready",
             "turned", "scanned", "back", "peaks_ready", "peaks_picked", "mask_ready", "mask_used", "m_ready", "m_step",
             "scale_ready", "m_read", "w_ready", "ex_ready", "hx_ready", "summed", "scaled", "added", "pool_step",
             "cleared"))
        reset_in = [S(f"reset_in{k}") for k in range(4)]

        def sb(n, shape, dt=F32):
            return ctx.enter_context(nc.sbuf_tensor(f"{name}_{n}", shape, dt))

        def pb(n):
            return ctx.enter_context(nc.psum_tensor(f"{name}_{n}", [P, 512], F32))
        UH = U * HEADS
        idx = [sb(f"idx{k}", [P, U], U32) for k in range(4)]
        rows = [sb(f"rows{k}", [P, U, HEADS, HID + 1]) for k in range(4)]
        reset = [sb(f"reset{k}", [UH, P], BF16) for k in range(4)]
        hot = [sb(f"hot{k}", [P, U, P]) for k in range(2)]
        ends = [sb(f"ends{k}", [P, U, P]) for k in range(2)]
        hot_t = [sb(f"hot_t{k}", [P, U * P]) for k in range(2)]
        z = [sb(f"z{k}", [P, U, HEADS]) for k in range(2)]
        leaky = [sb(f"leaky{k}", [P, U, HEADS]) for k in range(2)]
        logit = [sb(f"logit{k}", [P, U, HEADS]) for k in range(2)]
        run = [sb(f"run{k}", [UH, P]) for k in range(2)]
        peaks = [sb(f"peaks{k}", [P, U, HEADS + 1]) for k in range(2)]
        absent = [sb(f"absent{k}", [P, U]) for k in range(2)]
        chunk_m = [sb(f"chunk_m{k}", [P, U, HEADS]) for k in range(2)]
        new_m = [sb(f"new_m{k}", [P, U, HEADS]) for k in range(2)]
        drop = [sb(f"drop{k}", [P, U, HEADS]) for k in range(2)]
        scale = [sb(f"scale{k}", [P, U, HEADS]) for k in range(2)]
        under = [sb(f"under{k}", [P, U, HEADS]) for k in range(2)]
        hx = [sb(f"hx{k}", [P, U, HEADS, HID + 1]) for k in range(2)]
        ps_t = [pb(f"ps_t{k}") for k in range(2)]
        ps_s = [pb(f"ps_s{k}") for k in range(2)]
        ps_n = [[pb(f"ps_n{k}{h}") for h in range(2)] for k in range(2)]
        AR, MT, MB, MN, MS = (slice(0, 16), slice(64, 192), slice(192, 208), slice(256, 276), slice(320, 336))
        PE_T, DVE_T = mybir.EngineType.PE, mybir.EngineType.DVE

        def heads(ap):
            return ap.rearrange("p (u h) -> p u h", h=HEADS)

        with nc.Block() as block:
            @block.gpsimd
            def _(pool):
                def unit(i, g):
                    pool.wait_ge(idx_ready, i * 4 + (g + 1))
                    wait_again(pool, hx_ready, i * 4 + (g - 3))
                    pool.sem_inc(pool_step, 1)
                    for j in range(U):
                        pool.indirect_dma_start(rows[g][:, j, :, :].rearrange("p h c -> p (h c)"), None, X.hrow[:, :],
                                                bass.IndirectOffsetOnAxis(ap=idx[g][:, j:j + 1], axis=0))\
                            .then_inc(T.moves.sems[g][j], 16)
                turns(pool, unit)

            @block.sync
            def _(sp):
                def unit(i, g):
                    wait_again(sp, scanned, i * 4 + (g - 3))
                    for j in range(U):
                        src = X.reset_dst[bass.ds(i * 4 * U * P + (g * U + j) * P, P)].partition_broadcast(HEADS)
                        sp.dma_start(reset[g][j * HEADS:(j + 1) * HEADS, :], src).then_inc(reset_in[g], 16)
                turns(sp, unit)

            @block.vector
            def _(dve):
                nc.vector.memset(T.acc[:, :], 0.0).then_inc(cleared, 1)
                nc.vector.memset(T.top[:, :], LOW).then_inc(cleared, 1)
                for k in range(2):
                    nc.vector.memset(peaks[k][:, :, :], 1.0).then_inc(cleared, 1)

                def take_index(i, g):
                    T.moves.wait_last(dve, i, g)
                    nc.vector.tensor_copy(idx[g][:, :], T.m_dst[:, bass.ds(i * 4 * U + g * U, U), 0]).then_inc(idx_ready, 1)

                def make_hot(i, g):
                    k = g % 2
                    here = bass.ds(i * 4 * U + g * U, U)
                    wait_again(dve, summed, i * 4 + (g - 1))
                    nc.vector.tensor_tensor(hot[k][:, :, :], repeat(T.iota1_f[:, :], U), spread(T.m_dst[:, here, 2], P),
                                            ALU.is_equal).then_inc(hot_ready, 1)
                    wait_again(dve, peaks_picked, i * 4 + (g - 1))
                    nc.vector.tensor_tensor(ends[k][:, :, :], repeat(T.iota1_f[:, :], U), spread(T.last_dst[:, here], P),
                                            ALU.is_equal).then_inc(mask_ready, 1)

                def logits(i, g):
                    n, k = i * 4 + g, g % 2
                    T.moves.wait(dve, i, g)
                    dve.wait_ge(ar_read, n + 1)
                    wait_again(dve, leaky_ready, n - 1)
                    nc.vector.tensor_tensor(z[k][:, :, :], rows[g][:, :, :, HID], heads(ps_s[k][:, AR]), ALU.add)\
                        .then_inc(z_ready, 1)
                    dve.wait_ge(z_ready, n + 1)
                    wait_again(dve, logit_ready, n - 1)
                    nc.vector.scalar_tensor_tensor(out=leaky[k][:, :, :], in0=z[k][:, :, :], scalar=0.2, in1=z[k][:, :, :],
                                                   op0=ALU.mult, op1=ALU.max).then_inc(leaky_ready, 1)
                    dve.wait_ge(leaky_ready, n + 1)
                    wait_again(dve, w_ready, n - 1)
                    wait_again(dve, turned, n - 1)
                    nc.vector.tensor_tensor(logit[k][:, :, :], leaky[k][:, :, :],
                                            spread(T.m_dst[:, bass.ds(i * 4 * U + g * U, U), 1], HEADS), ALU.mult)\
                        .then_inc(logit_ready, 1)

                def scan(i, g):
                    n, k = i * 4 + g, g % 2
                    dve.wait_ge(turned, n + 1)
                    dve.wait_ge(reset_in[g], i * 64 + 64)
                    wait_again(dve, back, n - 1)
                    nc.vector.tensor_tensor_scan(run[k][:, :], reset[g][:, :], ps_s[k][0:UH, MT], 0.0, ALU.add, ALU.max)\
                        .then_inc(scanned, 1)

                def raise_maxima(i, g, tiles):
                    n, k = i * 4 + g, g % 2
                    dve.wait_ge(peaks_picked, n + 1)
                    pk = ps_s[k][:, MN].rearrange("p (u h) -> p u h", h=HEADS + 1)
                    nc.vector.tensor_scalar(absent[k][:, :], pk[:, :, HEADS], -LOW, LOW, ALU.mult, ALU.add)\
                        .then_inc(m_step, 1)
                    dve.wait_ge(m_step, i * 40 + (10 * g + 1))
                    nc.vector.tensor_tensor(chunk_m[k][:, :, :], pk[:, :, 0:HEADS], spread(absent[k][:, :], HEADS), ALU.add)\
                        .then_inc(m_step, 1)
                    wait_again(dve, scale_ready, n - 1)
                    wait_again(dve, m_read, n - 1)
                    for j in range(U):
                        top = T.top[:, bass.ds(tiles[j] * HEADS, HEADS)]
                        dve.wait_ge(m_step, i * 40 + (10 * g + 2 + 2 * j))
                        nc.vector.tensor_tensor(new_m[k][:, j, :], top, chunk_m[k][:, j, :], ALU.max).then_inc(m_step, 1)
                        dve.wait_ge(m_step, i * 40 + (10 * g + 3 + 2 * j))
                        nc.vector.tensor_tensor(drop[k][:, j, :], top, new_m[k][:, j, :], ALU.subtract).then_inc(m_ready, 1)
                        dve.wait_ge(m_ready, i * 16 + (4 * g + j + 1))
                        nc.vector.tensor_scalar(top, new_m[k][:, j, :], 0.0, None, ALU.add).then_inc(m_step, 1)

                def under_max(i, g):
                    n, k = i * 4 + g, g % 2
                    dve.wait_ge(m_read, n + 1)
                    wait_again(dve, ex_ready, n - 1)
                    nc.vector.tensor_tensor(under[k][:, :, :], logit[k][:, :, :], heads(ps_s[k][:, MS]), ALU.subtract)\
                        .then_inc(w_ready, 1)

                def weigh(i, g):
                    n, k = i * 4 + g, g % 2
                    dve.wait_ge(ex_ready, n + 1)
                    for j in range(U):
                        ins = nc.vector.tensor_tensor(hx[k][:, j, :, 0:HID], rows[g][:, j, :, 0:HID],
                                                      hx[k][:, j, :, HID:HID + 1].broadcast_to([P, HEADS, HID]), ALU.mult)
                    ins.then_inc(hx_ready, 1)

                def add(i, g, j, tiles):
                    n, k = i * 4 + g, g % 2
                    if j == 0:
                        dve.wait_ge(summed, n + 1)
                        dve.wait_ge(scale_ready, n + 1)
                    acc = T.acc[:, bass.ds(tiles[j] * ROW, ROW)]
                    wait_again(dve, added, i * 16 + (U * g + j))
                    nc.vector.tensor_tensor(acc.rearrange("p (h c) -> p h c", h=HEADS),
                                            acc.rearrange("p (h c) -> p h c", h=HEADS),
                                            spread(scale[k][:, j, :], HID + 1), ALU.mult).then_inc(scaled, 1)
                    dve.wait_ge(scaled, i * 16 + (U * g + j + 1))
                    nc.vector.tensor_tensor(acc, acc, ps_n[k][j // 2][:, (j % 2) * ROW:(j % 2 + 1) * ROW], ALU.add)\
                        .then_inc(added, 1)

                for g in range(3):
                    take_index(0, g)
                dve.wait_ge(cleared, 4)
                make_hot(0, 0)

                def unit(i, g):
                    if then := near(i, g, 3):
                        take_index(*then)
                    logits(i, g)
                    if then := near(i, g, 1):
                        make_hot(*then)
                    scan(i, g)
                    past = near(i, g, -1)
                    if past:
                        tp = tiles_of(nc, DVE_T, T.tile_d, *past)
                        add(*past, 0, tp)
                        add(*past, 1, tp)
                    raise_maxima(i, g, tiles_of(nc, DVE_T, T.tile_d, i, g))
                    if past:
                        add(*past, 2, tp)
                    under_max(i, g)
                    if past:
                        add(*past, 3, tp)
                    weigh(i, g)
                turns(dve, unit)
                tp = tiles_of(nc, DVE_T, T.tile_d, ITERS - 1, 3)
                for j in range(U):
                    add(ITERS - 1, 3, j, tp)

            @block.scalar
            def _(act):
                def copy_hot(i, g):
                    act.wait_ge(hot_turned, i * 4 + (g + 1))
                    wait_again(act, m_read, i * 4 + (g - 1))
                    nc.scalar.copy(hot_t[g % 2][:, :], ps_t[g % 2][:, :]).then_inc(hot_copied, 1)
                act.wait_ge(cleared, 4)
                copy_hot(0, 0)

                def unit(i, g):
                    n, k = i * 4 + g, g % 2
                    if then := near(i, g, 1):
                        copy_hot(*then)
                    act.wait_ge(back, n + 1)
                    wait_again(act, peaks_picked, n - 1)
                    nc.scalar.copy(peaks[k][:, :, 0:HEADS], heads(ps_s[k][:, MB])).then_inc(peaks_ready, 1)
                    act.wait_ge(m_ready, i * 16 + (4 * g + 4))
                    wait_again(act, added, i * 16 + (4 * (g - 1)))
                    nc.scalar.activation(scale[k][:, :, :], drop[k][:, :, :], ACT.Exp).then_inc(scale_ready, 1)
                    act.wait_ge(w_ready, n + 1)
                    wait_again(act, summed, n - 1)
                    nc.scalar.activation(hx[k][:, :, :, HID], under[k][:, :, :], ACT.Exp).then_inc(ex_ready, 1)
                turns(act, unit)

            @block.tensor
            def _(pe):
                def turn_hot(i, g):
                    pe.wait_ge(hot_ready, i * 4 + (g + 1))
                    wait_again(pe, hot_copied, i * 4 + (g - 1))
                    for j in range(U):
                        ins = nc.tensor.transpose(ps_t[g % 2][:, j * P:(j + 1) * P], hot[g % 2][:, j, :], T.ident[:, :])
                    ins.then_inc(hot_turned, 1)
                turn_hot(0, 0)

                def unit(i, g):
                    n, k = i * 4 + g, g % 2
                    tiles = tiles_of(nc, PE_T, T.tile_d, i, g)
                    pe.wait_ge(hot_copied, n + 1)
                    wait_again(pe, z_ready, n - 1)
                    for j in range(U):
                        ins = nc.tensor.matmul(ps_s[k][:, j * HEADS:(j + 1) * HEADS], hot_t[k][:, j * P:(j + 1) * P],
                                               T.ar[:, bass.ds(tiles[j] * HEADS, HEADS)], start=True, stop=True)
                    ins.then_inc(ar_read, 1)
                    pe.wait_ge(logit_ready, n + 1)
                    wait_again(pe, scanned, n - 1)
                    nc.tensor.transpose(ps_s[k][0:UH, MT], logit[k][:, :, :].rearrange("p u h -> p (u h)"), T.ident[:, :])\
                        .then_inc(turned, 1)
                    if then := near(i, g, 1):
                        turn_hot(*then)
                    pe.wait_ge(scanned, n + 1)
                    wait_again(pe, peaks_ready, n - 1)
                    nc.tensor.matmul(ps_s[k][:, MB], run[k][:, :], T.ident[0:UH, 0:UH], start=True, stop=True).then_inc(back, 1)
                    pe.wait_ge(peaks_ready, n + 1)
                    pe.wait_ge(mask_ready, n + 1)
                    wait_again(pe, m_step, i * 40 + (10 * (g - 1)))
                    for j in range(U):
                        a = MN.start + j * (HEADS + 1)
                        ins = nc.tensor.matmul(ps_s[k][:, a:a + HEADS + 1], ends[k][:, j, :], peaks[k][:, j, :],
                                               start=True, stop=True)
                    ins.then_inc(peaks_picked, 1)
                    pe.wait_ge(m_ready, i * 16 + (4 * g + 4))
                    wait_again(pe, w_ready, n - 1)
                    for j in range(U):
                        a = MS.start + j * HEADS
                        ins = nc.tensor.matmul(ps_s[k][:, a:a + HEADS], hot_t[k][:, j * P:(j + 1) * P], new_m[k][:, j, :],
                                               start=True, stop=True)
                    ins.then_inc(m_read, 1)
                    pe.wait_ge(hx_ready, n + 1)
                    wait_again(pe, added, i * 16 + (4 * (g - 1)))
                    for j in range(U):
                        ins = nc.tensor.matmul(ps_n[k][j // 2][:, (j % 2) * ROW:(j % 2 + 1) * ROW], hot[k][:, j, :],
                                               hx[k][:, j, :, :].rearrange("p h c -> p (h c)"), start=True, stop=True)
                    ins.then_inc(summed, 1)
                turns(pe, unit)
        T.moves.close(lambda g, j: ITERS)
        S.clear()


def build_mlp_edges(nc, T, X):
    with ExitStack() as ctx:
        S = Sems(nc, ctx, "ml")
        (idx_ready, hot_ready, hot_turned, hot_copied, own_read, part_ready, in_ready, turned, act_in, hid_ready,
         act_hid, theta_ready, msg_ready, summed, added, pool_step, cleared) = (S(n) for n in (
             "idx_ready", "hot_ready", "hot_turned", "hot_copied", "own_read", "part_ready", "in_ready", "turned",
             "act_in", "hid_ready", "act_hid", "theta_ready", "msg_ready", "summed", "added", "pool_step", "cleared"))
        attr_in = [S(f"attr_in{k}") for k in range(4)]

        def sb(n, shape, dt=F32):
            return ctx.enter_context(nc.sbuf_tensor("ml_" + n, shape, dt))

        def pb(n):
            return ctx.enter_context(nc.psum_tensor("ml_" + n, [P, 512], F32))
        idx = [sb(f"idx{k}", [P, U], U32) for k in range(4)]
        rows = [sb(f"rows{k}", [P, U, D]) for k in range(4)]
        attr = [sb(f"attr{k}", [P, U, D]) for k in range(4)]
        hot = [sb(f"hot{k}", [P, U, P]) for k in range(4)]
        hot_t = sb("hot_t", [P, U * P])
        sin = sb("sin", [P, U * P])
        hid = [sb(f"hid{k}", [P, U * P]) for k in range(2)]
        msg = sb("msg", [P, U, D])
        ps_t, ps_o, ps_x, ps_f, ps_s = pb("ps_t"), pb("ps_o"), pb("ps_x"), pb("ps_f"), pb("ps_s")
        ps_h = [pb(f"ps_h{k}") for k in range(2)]
        PE_T, DVE_T = mybir.EngineType.PE, mybir.EngineType.DVE

        with nc.Block() as block:
            @block.gpsimd
            def _(pool):
                def unit(i, g):
                    pool.wait_ge(idx_ready, i * 4 + (g + 1))
                    wait_again(pool, msg_ready, i * 4 + (g - 3))
                    pool.sem_inc(pool_step, 1)
                    for j in range(U):
                        pool.indirect_dma_start(rows[g][:, j, :], None, X.h2row[:, :],
                                                bass.IndirectOffsetOnAxis(ap=idx[g][:, j:j + 1], axis=0))\
                            .then_inc(T.moves.sems[g][j], 16)
                turns(pool, unit)

            @block.sync
            def _(sp):
                def unit(i, g):
                    wait_again(sp, turned, i * 4 + (g - 3))
                    a = X.rec_src[bass.ds(i * 4 * U * P + g * U * P, U * P), :]
                    sp.dma_start(attr[g][:, :, :], a.rearrange("(j e) f -> e j f", e=P)[:, :, 0:D]).then_inc(attr_in[g], 16)
                turns(sp, unit)

            @block.vector
            def _(dve):
                nc.vector.memset(T.acc[:, :], 0.0).then_inc(cleared, 1)

                def take_index(i, g):
                    T.moves.wait_last(dve, i, g)
                    nc.vector.tensor_copy(idx[g][:, :], T.m_src[:, bass.ds(i * 4 * U + g * U, U), 0]).then_inc(idx_ready, 1)

                def make_hot(i, g):
                    wait_again(dve, summed, i * 4 + (g - 3))
                    nc.vector.tensor_tensor(hot[g][:, :, :], repeat(T.iota1_f[:, :], U),
                                            spread(T.m_src[:, bass.ds(i * 4 * U + g * U, U), 2], P),
                                            ALU.is_equal).then_inc(hot_ready, 1)

                def sum_input(i, g):
                    T.moves.wait(dve, i, g)
                    dve.wait_ge(attr_in[g], i * 16 + 16)
                    nc.vector.tensor_tensor(attr[g][:, :, :], attr[g][:, :, :], rows[g][:, :, :], ALU.add)\
                        .then_inc(part_ready, 1)
                    dve.wait_ge(own_read, i * 4 + (g + 1))
                    dve.wait_ge(part_ready, i * 4 + (g + 1))
                    nc.vector.tensor_tensor(attr[g][:, :, :], attr[g][:, :, :],
                                            ps_o[:, :].rearrange("p (j f) -> p j f", f=D), ALU.add).then_inc(in_ready, 1)

                def message(i, g):
                    dve.wait_ge(theta_ready, i * 4 + (g + 1))
                    wait_again(dve, summed, i * 4 + g)
                    nc.vector.tensor_tensor(msg[:, :, :], rows[g][:, :, :],
                                            ps_f[:, :].rearrange("p (j f) -> p j f", f=D), ALU.mult).then_inc(msg_ready, 1)

                def add(i, g):
                    tiles = tiles_of(nc, DVE_T, T.tile_s, i, g)
                    dve.wait_ge(summed, i * 4 + (g + 1))
                    for j in range(U):
                        wait_again(dve, added, i * 16 + (U * g + j))
                        to = T.acc[:, bass.ds(tiles[j] * ROW, D)]
                        nc.vector.tensor_tensor(to, to, ps_s[:, j * D:(j + 1) * D], ALU.add).then_inc(added, 1)

                for g in range(3):
                    take_index(0, g)
                dve.wait_ge(cleared, 1)
                make_hot(0, 0)
                sum_input(0, 0)

                def unit(i, g):
                    if then := near(i, g, 3):
                        take_index(*then)
                    then = near(i, g, 1)
                    if then:
                        make_hot(*then)
                    if past := near(i, g, -1):
                        add(*past)
                    if then:
                        sum_input(*then)
                    message(i, g)
                turns(dve, unit)
                add(ITERS - 1, 3)

            @block.scalar
            def _(act):
                def copy_hot(i, g):
                    act.wait_ge(hot_turned, i * 4 + (g + 1))
                    wait_again(act, own_read, i * 4 + g)
                    nc.scalar.copy(hot_t[:, :], ps_t[:, :]).then_inc(hot_copied, 1)
                copy_hot(0, 0)

                def unit(i, g):
                    n = i * 4 + g
                    act.wait_ge(turned, n + 1)
                    wait_again(act, hid_ready, 2 * n)
                    nc.scalar.activation(sin[:, :], ps_x[:, :], ACT.Silu).then_inc(act_in, 1)
                    if then := near(i, g, 1):
                        copy_hot(*then)
                    for h in range(2):
                        act.wait_ge(hid_ready, 2 * n + (h + 1))
                        wait_again(act, theta_ready, n)
                        nc.scalar.activation(hid[h][:, :], ps_h[h][:, :], ACT.Silu, bias=T.b1c[:, h:h + 1])\
                            .then_inc(act_hid, 1)
                turns(act, unit)

            @block.tensor
            def _(pe):
                def turn_hot(i, g):
                    pe.wait_ge(hot_ready, i * 4 + (g + 1))
                    wait_again(pe, hot_copied, i * 4 + g)
                    for j in range(U):
                        ins = nc.tensor.transpose(ps_t[:, j * P:(j + 1) * P], hot[g][:, j, :], T.ident[:, :])
                    ins.then_inc(hot_turned, 1)

                def read_own(i, g):
                    tiles = tiles_of(nc, PE_T, T.tile_s, i, g)
                    pe.wait_ge(hot_copied, i * 4 + (g + 1))
                    wait_again(pe, in_ready, i * 4 + g)
                    for j in range(U):
                        ins = nc.tensor.matmul(ps_o[:, j * D:(j + 1) * D], hot_t[:, j * P:(j + 1) * P],
                                               T.nodes[:, bass.ds(tiles[j] * D, D)], start=True, stop=True)
                    ins.then_inc(own_read, 1)

                def turn_input(i, g):
                    pe.wait_ge(in_ready, i * 4 + (g + 1))
                    wait_again(pe, act_in, i * 4 + g)
                    for j in range(U):
                        ins = nc.tensor.transpose(ps_x[:, j * P:(j + 1) * P], attr[g][:, j, :], T.ident[:, :])
                    ins.then_inc(turned, 1)

                def hidden(i, g):
                    pe.wait_ge(act_in, i * 4 + (g + 1))
                    for h in range(2):
                        wait_again(pe, act_hid, 2 * (i * 4 + g) + (h - 1))
                        nc.tensor.matmul(ps_h[h][:, :], T.w1[:, h * P:(h + 1) * P], sin[:, :], start=True, stop=True)\
                            .then_inc(hid_ready, 1)

                def theta(i, g):
                    pe.wait_ge(act_hid, 2 * (i * 4 + g) + 2)
                    wait_again(pe, msg_ready, i * 4 + g)
                    for j in range(U):
                        part = ps_f[:, j * D:(j + 1) * D]
                        nc.tensor.matmul(part, T.ones[0:1, :], T.b2r[0:1, :], start=True, stop=False)
                        for h in range(2):
                            ins = nc.tensor.matmul(part, hid[h][:, j * P:(j + 1) * P], T.w2[:, h, :], start=False, stop=(h == 1))
                    ins.then_inc(theta_ready, 1)

                def sum_up(i, g):
                    pe.wait_ge(msg_ready, i * 4 + (g + 1))
                    wait_again(pe, added, i * 16 + U * g)
                    for j in range(U):
                        ins = nc.tensor.matmul(ps_s[:, j * D:(j + 1) * D], hot[g][:, j, :], msg[:, j, :], start=True, stop=True)
                    ins.then_inc(summed, 1)
                turn_hot(0, 0)
                read_own(0, 0)

                def unit(i, g):
                    turn_input(i, g)
                    then = near(i, g, 1)
                    if then:
                        turn_hot(*then)
                    if past := near(i, g, -1):
                        sum_up(*past)
                    hidden(i, g)
                    if then:
                        read_own(*then)
                    theta(i, g)
                turns(pe, unit)
                sum_up(ITERS - 1, 3)
        T.moves.close(lambda g, j: ITERS)
        S.clear()


def build_gcn_edges(nc, T, X):
    with ExitStack() as ctx:
        S = Sems(nc, ctx, "gc")
        idx_ready, hot_ready, summed, added, pool_step, cleared = (
            S("idx_ready"), S("hot_ready"), S("summed"), S("added"), S("pool_step"), S("cleared"))
        idx = [ctx.enter_context(nc.sbuf_tensor(f"gc_idx{k}", [P, U], U32)) for k in range(4)]
        rows = [ctx.enter_context(nc.sbuf_tensor(f"gc_rows{k}", [P, U, D], F32)) for k in range(4)]
        hot = [ctx.enter_context(nc.sbuf_tensor(f"gc_hot{k}", [P, U, P], F32)) for k in range(2)]
        ps = [ctx.enter_context(nc.psum_tensor(f"gc_ps{k}", [P, 512], F32)) for k in range(2)]

        with nc.Block() as block:
            @block.gpsimd
            def _(pool):
                def unit(i, g):
                    pool.wait_ge(idx_ready, i * 4 + (g + 1))
                    wait_again(pool, summed, i * 4 + (g - 3))
                    pool.sem_inc(pool_step, 1)
                    for j in range(U):
                        pool.indirect_dma_start(rows[g][:, j, :], None, X.h3row[:, :],
                                                bass.IndirectOffsetOnAxis(ap=idx[g][:, j:j + 1], axis=0))\
                            .then_inc(T.moves.sems[g][j], 16)
                turns(pool, unit)

            @block.vector
            def _(dve):
                nc.vector.memset(T.acc[:, :], 0.0).then_inc(cleared, 1)

                def take_index(i, g):
                    T.moves.wait_last(dve, i, g)
                    nc.vector.tensor_copy(idx[g][:, :], T.m_src[:, bass.ds(i * 4 * U + g * U, U), 0]).then_inc(idx_ready, 1)

                def add(i, g):
                    tiles = tiles_of(nc, mybir.EngineType.DVE, T.tile_s, i, g)
                    dve.wait_ge(summed, i * 4 + (g + 1))
                    for j in range(U):
                        wait_again(dve, added, i * 16 + (U * g + j))
                        to = T.acc[:, bass.ds(tiles[j] * ROW, D)]
                        nc.vector.tensor_tensor(to, to, ps[g % 2][:, j * D:(j + 1) * D], ALU.add).then_inc(added, 1)

                for g in range(3):
                    take_index(0, g)
                dve.wait_ge(cleared, 1)

                def unit(i, g):
                    if then := near(i, g, 3):
                        take_index(*then)
                    wait_again(dve, summed, i * 4 + (g - 1))
                    for j in range(U):
                        c = i * 4 * U + (g * U + j)
                        ins = nc.vector.tensor_scalar(hot[g % 2][:, j, :], T.iota1_f[:, :], T.m_src[:, bass.ds(c, 1), 2],
                                                      T.m_src[:, bass.ds(c, 1), 1], ALU.is_equal, ALU.mult)
                    ins.then_inc(hot_ready, 1)
                    if past := near(i, g, -1):
                        add(*past)
                turns(dve, unit)
                add(ITERS - 1, 3)

            @block.tensor
            def _(pe):
                def unit(i, g):
                    pe.wait_ge(hot_ready, i * 4 + (g + 1))
                    wait_again(pe, added, i * 16 + U * (g - 1))
                    for j in range(U):
                        T.moves.wait(pe, i, g, [j])
                        ins = nc.tensor.matmul(ps[g % 2][:, j * D:(j + 1) * D], hot[g % 2][:, j, :], rows[g][:, j, :],
                                               start=True, stop=True)
                    ins.then_inc(summed, 1)
                turns(pe, unit)
        T.moves.close(lambda g, j: ITERS)
        S.clear()


NTURN = NT // 2
WROW = HEADS * (HID + 1)
WCAT = WROW + HEADS


def build_weights(nc, T, X):
    with ExitStack() as ctx:
        S = Sems(nc, ctx, "wt")
        loaded, turned, dve_at = S("loaded"), S("turned"), S("dve_at")
        w0 = ctx.enter_context(nc.sbuf_tensor("wt_w0", [P, 2 * D], F32))
        w = [ctx.enter_context(nc.sbuf_tensor(f"wt_gat{k}", [P, D], F32)) for k in range(2)]
        att = [ctx.enter_context(nc.sbuf_tensor(f"wt_att{k}", [P, D], F32)) for k in range(4)]
        prod = ctx.enter_context(nc.sbuf_tensor("wt_prod", [P, D], F32))
        dots = ctx.enter_context(nc.sbuf_tensor("wt_dots", [P, HEADS], F32))
        ps = ctx.enter_context(nc.psum_tensor("wt_ps", [P, 512], F32))
        loads = [(w0[:, :], X.L0_gnn_W), (w[0][:, :], X.L1_gnn_W1), (w[1][:, :], X.L1_gnn_W2),
                 (T.w1[:, :], X.L2_gnn_W1), (T.w2[:, :, :], X.L2_gnn_W2.rearrange("(h k) n -> k h n", h=2)),
                 (T.wt[:, :], X.L2_gnn_Wt), (T.w3[:, :], X.L3_gnn_W), (T.wres[:, :], X.L3_gnn_Wres),
                 (T.b1c[:, :], X.L2_gnn_b1.rearrange("(h k) -> k h", h=2))]
        loads += [(t[0:1, :], a.unsqueeze(0)) for t, a in (
            (T.b0r, X.L0_gnn_b), (T.b2r, X.L2_gnn_b2), (T.btr, X.L2_gnn_bt), (T.b3r, X.L3_gnn_b), (T.bresr, X.L3_gnn_bres))]
        loads += [(t[:, :], a.partition_broadcast(P)) for t, a in (
            (T.bg1, X.L1_gnn_b1), (T.bg2, X.L1_gnn_b2), (T.gamma, X.L2_gnn_ln_gamma), (T.beta, X.L2_gnn_ln_beta))]
        loads += [(t[:, :], a.rearrange("h c -> (h c)").partition_broadcast(P)) for t, a in zip(
            att, (X.L1_gnn_att_l1, X.L1_gnn_att_r1, X.L1_gnn_att_l2, X.L1_gnn_att_r2))]
        with nc.Block() as block:
            @block.sync
            def _(sp):
                with nc.allow_non_contiguous_dma(reason="256 biases, once"):
                    for to, frm in loads:
                        sp.dma_start(to, frm).then_inc(loaded, 16)

            @block.vector
            def _(dve):
                dve.wait_ge(loaded, 16 * len(loads))
                link = chain(dve, dve_at)
                link(nc.vector.memset(T.acc[:, 0:1], 0.0))
                for k, cat in enumerate((T.cat1, T.cat2)):
                    wide = cat[:, 0:WROW].rearrange("p (h c) -> p h c", h=HEADS)
                    link(nc.vector.tensor_copy(wide[:, :, 0:HID], w[k][:, :].rearrange("p (h c) -> p h c", h=HEADS)))
                    for side in range(2):
                        link(nc.vector.tensor_tensor(prod[:, :], w[k][:, :], att[2 * k + side][:, :], ALU.mult))
                        link(nc.vector.tensor_reduce(dots[:, :], prod[:, :].rearrange("p (h c) -> p h c", h=HEADS),
                                                     AX.X, ALU.add))
                        to = wide[:, :, HID] if side == 0 else cat[:, WROW:WCAT]
                        link(nc.vector.tensor_copy(to, dots[:, :]))
                dve.wait_ge(turned, 1)
                link(nc.vector.tensor_copy(T.w0t[:, :], ps[:, 0:2 * D]))

            @block.tensor
            def _(pe):
                pe.wait_ge(loaded, 16 * len(loads))
                for h in range(2):
                    ins = nc.tensor.transpose(ps[:, h * D:(h + 1) * D], w0[:, h * D:(h + 1) * D], T.ident[:, :])
                ins.then_inc(turned, 1)
        S.clear()


def build_nodes(nc, T, X, kind):
    resid = {"sage": X.xpad, "gat_mid": None, "gat_end": X.x1, "mlp": X.x2, "gcn": X.x3}[kind]
    weight, bias = {"sage": (T.w0t, T.b0r), "gat_mid": (T.cat2, None), "gat_end": (None, None),
                    "mlp": (T.wt, T.btr), "gcn": (T.wres, T.bresr)}[kind]
    gat = kind.startswith("gat")
    width = WCAT if kind == "gat_mid" else D
    with ExitStack() as ctx:
        S = Sems(nc, ctx, "n" + kind)
        taken, scaled, turned, copied, multiplied, plus, noted, told, silued, inv, joined = (S(n) for n in (
            "taken", "scaled", "turned", "copied", "multiplied", "plus", "noted", "told", "silued", "inv", "joined"))
        resid_in = [S(f"resid_in{k}") for k in range(2)]
        stored = [S(f"stored{k}") for k in range(2)]

        def sb(n, shape, dt=F32):
            return ctx.enter_context(nc.sbuf_tensor(f"n{kind}_{n}", shape, dt))
        xr = [sb(f"xr{k}", [P, D]) for k in range(2)]
        pre = [sb(f"pre{k}", [P, D]) for k in range(2)]
        v = [sb(f"v{k}", [P, D]) for k in range(2)]
        vt = [sb(f"vt{k}", [P, 2 * P]) for k in range(2)]
        mid = [sb(f"mid{k}", [P, D]) for k in range(2)]
        hb = [sb(f"hb{k}", [P, WROW]) for k in range(2)]
        rs = sb("rs", [P, NT * HEADS])
        pa = [ctx.enter_context(nc.psum_tensor(f"n{kind}_pa{k}", [P, 512], F32)) for k in range(2)]
        py = [ctx.enter_context(nc.psum_tensor(f"n{kind}_py{k}", [P, 512], F32)) for k in range(2)]

        def loop(eng, step):
            turns(eng, step, depth=2, count=NTURN)

        with nc.Block() as block:
            @block.sync
            def _(sp):
                if resid is not None:
                    def load(i, k):
                        wait_again(sp, noted if width == D else taken, i * 2 + (k - 1))
                        sp.dma_start(xr[k][:, :], resid[bass.ds(i * 2 * P + k * P, P), :]).then_inc(resid_in[k], 16)
                    loop(sp, load)
                if kind == "gat_mid":
                    def store(i, k):
                        sp.wait_ge(plus, i * 2 + (k + 1))
                        sp.dma_start(X.hrow[bass.ds(i * 2 * P + k * P, P), :], hb[k][:, :]).then_inc(stored[k], 16)
                    loop(sp, store)
                    for k in range(2):
                        sp.wait_ge(stored[k], 16 * NTURN)

            @block.vector
            def _(dve):
                if gat:
                    sums = T.acc[:, :].rearrange("p (t c) -> p t c", c=HID + 1)[:, :, HID]
                    nc.vector.tensor_scalar(rs[:, :], sums, 1e-16, None, ALU.add).then_inc(inv, 1)
                    dve.wait_ge(inv, 1)
                    nc.vector.reciprocal(rs[:, :], rs[:, :]).then_inc(inv, 1)
                    dve.wait_ge(inv, 2)

                def before(i, k):
                    n = i * 2 + k
                    acc = T.acc[:, bass.ds(i * 2 * ROW + k * ROW, ROW)]
                    if gat:
                        wait_again(dve, taken, n - 1)
                        nc.vector.tensor_tensor(pre[k][:, :].rearrange("p (h c) -> p h c", h=HEADS),
                                                acc.rearrange("p (h c) -> p h c", h=HEADS)[:, :, 0:HID],
                                                spread(rs[:, bass.ds(i * 2 * HEADS + k * HEADS, HEADS)], HID), ALU.mult)\
                            .then_inc(scaled, 1)
                        dve.wait_ge(scaled, n + 1)
                        wait_again(dve, turned if weight is not None else joined, n - 1)
                        nc.vector.tensor_tensor(v[k][:, :], pre[k][:, :], (T.bg1 if kind == "gat_mid" else T.bg2)[:, :],
                                                ALU.add).then_inc(taken, 1)
                    elif kind == "sage":
                        wait_again(dve, turned, n - 1)
                        nc.vector.tensor_copy(v[k][:, :], acc[:, 0:D]).then_inc(taken, 1)
                    elif kind == "mlp":
                        wait_again(dve, silued, n - 1)
                        nc.vector.tensor_tensor(pre[k][:, :], acc[:, 0:D], T.nodes[:, bass.ds(i * 2 * D + k * D, D)], ALU.add)\
                            .then_inc(taken, 1)
                    else:
                        wait_again(dve, turned, n - 1)
                        wait_again(dve, plus, n - 1)
                        nc.vector.tensor_scalar(v[k][:, :], acc[:, 0:D], 0.0, None, ALU.max).then_inc(taken, 1)

                def after(i, k):
                    n = i * 2 + k
                    if weight is not None:
                        dve.wait_ge(multiplied, n + 1)
                    if kind == "gat_mid":
                        wait_again(dve, stored[k], 16 * i)
                        nc.vector.tensor_copy(hb[k][:, :], py[k][:, 0:WROW]).then_inc(plus, 1)
                        nc.vector.tensor_copy(T.ar[:, bass.ds(i * 2 * HEADS + k * HEADS, HEADS)], py[k][:, WROW:WCAT])\
                            .then_inc(noted, 1)
                        return
                    dve.wait_ge(resid_in[k], i * 16 + 16)
                    to = T.nodes[:, bass.ds(i * 2 * D + k * D, D)]
                    if kind == "gcn":
                        wait_again(dve, joined, n - 1)
                        nc.vector.tensor_tensor(mid[k][:, :], v[k][:, :], py[k][:, 0:D], ALU.add).then_inc(plus, 1)
                        dve.wait_ge(plus, n + 1)
                        nc.vector.tensor_tensor(to, mid[k][:, :], xr[k][:, :], ALU.add).then_inc(joined, 1)
                    elif kind == "gat_end":
                        dve.wait_ge(taken, n + 1)
                        nc.vector.tensor_tensor(to, v[k][:, :], xr[k][:, :], ALU.add).then_inc(joined, 1)
                    else:
                        nc.vector.tensor_tensor(to, xr[k][:, :], py[k][:, 0:D], ALU.add).then_inc(joined, 1)
                    dve.wait_ge(joined, n + 1)
                    dve.sem_inc(told, 1)
                    nc.vector.bn_stats(T.stats[:, bass.ds(i * 12 + 6 * k, 6)], to).then_inc(noted, 1)

                before(0, 0)

                def step(i, k):
                    if then := near(i, k, 1, 2, NTURN):
                        before(*then)
                    after(i, k)
                loop(dve, step)

            @block.scalar
            def _(act):
                if weight is None:
                    return

                def step(i, k):
                    n = i * 2 + k
                    if kind == "mlp":
                        act.wait_ge(taken, n + 1)
                        wait_again(act, turned, n - 1)
                        nc.scalar.activation(v[k][:, :], pre[k][:, :], ACT.Silu).then_inc(silued, 1)
                    act.wait_ge(turned, n + 1)
                    wait_again(act, multiplied, n - 1)
                    w = 2 * P if kind == "sage" else P
                    nc.scalar.copy(vt[k][:, 0:w], pa[k][:, 0:w]).then_inc(copied, 1)
                loop(act, step)

            @block.tensor
            def _(pe):
                if weight is None:
                    return

                def step(i, k):
                    n = i * 2 + k
                    pe.wait_ge(silued if kind == "mlp" else taken, n + 1)
                    wait_again(pe, copied, n - 1)
                    if kind == "sage":
                        pe.wait_ge(resid_in[k], i * 16 + 16)
                        nc.tensor.transpose(pa[k][:, P:2 * P], xr[k][:, :], T.ident[:, :])
                    nc.tensor.transpose(pa[k][:, 0:P], v[k][:, :], T.ident[:, :]).then_inc(turned, 1)
                    pe.wait_ge(copied, n + 1)
                    wait_again(pe, noted, n - 1)
                    y = py[k][:, 0:width]
                    if bias is not None:
                        nc.tensor.matmul(y, T.ones[0:1, :], bias[0:1, :], start=True, stop=False)
                    if kind == "sage":
                        nc.tensor.matmul(y, vt[k][:, P:2 * P], weight[:, 0:D], start=False, stop=False)
                        ins = nc.tensor.matmul(y, vt[k][:, 0:P], weight[:, D:2 * D], start=False, stop=True)
                    else:
                        ins = nc.tensor.matmul(y, vt[k][:, 0:P], weight[:, 0:width], start=bias is None, stop=True)
                    ins.then_inc(multiplied, 1)
                loop(pe, step)
        S.clear()


def build_norm(nc, T, X, kind):
    store = {"x1": X.x1, "x2": X.x2, "h2": X.h2row, "x3": X.x3, "out": X.out}[kind]
    weight, bias, width, rows = {"x1": (T.cat1, None, WCAT, X.hrow), "x3": (T.w3, T.b3r, D, X.h3row)}\
        .get(kind, (None, None, 0, None))
    wrow = min(width, WROW)
    with ExitStack() as ctx:
        S = Sems(nc, ctx, "m" + kind)
        step_at, rooted, normed, turned, copied, multiplied, out_ready, noted, told, times, plus = (S(n) for n in (
            "step_at", "rooted", "normed", "turned", "copied", "multiplied", "out_ready", "noted", "told", "times", "plus"))
        stored = [S(f"stored{k}") for k in range(2)]
        sent = [S(f"sent{k}") for k in range(2)]

        def sb(n, shape, dt=F32):
            return ctx.enter_context(nc.sbuf_tensor(f"m{kind}_{n}", shape, dt))
        dev = sb("dev", [P, NT])
        std = sb("std", [P, NT])
        mean = sb("mean", [P, NT])
        apart = sb("apart", [P, NT])
        ob = [sb(f"ob{k}", [P, D]) for k in range(2)]
        raw = [sb(f"raw{k}", [P, D]) for k in range(2)]
        mul = [sb(f"mul{k}", [P, D]) for k in range(2)]
        vt = [sb(f"vt{k}", [P, P]) for k in range(2)]
        hb = [sb(f"hb{k}", [P, WROW]) for k in range(2)]
        pa = [ctx.enter_context(nc.psum_tensor(f"m{kind}_pa{k}", [P, 512], F32)) for k in range(2)]
        py = [ctx.enter_context(nc.psum_tensor(f"m{kind}_py{k}", [P, 512], F32)) for k in range(2)]
        LAST = N - (NT - 1) * P

        def loop(eng, step):
            turns(eng, step, depth=2, count=NTURN)

        with nc.Block() as block:
            @block.sync
            def _(sp):
                def save(i, k):
                    sp.wait_ge(normed, i * 2 + (k + 1))
                    if kind == "out" and isinstance(i, int) and i == NTURN - 1 and k == 1:
                        sp.dma_start(store[N - LAST:N, :], ob[k][0:LAST, :]).then_inc(stored[k], 16)
                    else:
                        sp.dma_start(store[bass.ds(i * 2 * P + k * P, P), :], ob[k][:, :]).then_inc(stored[k], 16)
                loop(sp, save)
                for k in range(2):
                    sp.wait_ge(stored[k], 16 * NTURN)

            @block.scalar
            def _(act):
                act.wait_ge(step_at, 7)
                nc.scalar.activation(std[:, :], dev[:, :], ACT.Sqrt).then_inc(rooted, 1)
                if weight is None:
                    return

                def step(i, k):
                    n = i * 2 + k
                    act.wait_ge(turned, n + 1)
                    wait_again(act, multiplied, n - 1)
                    nc.scalar.copy(vt[k][:, :], pa[k][:, 0:P]).then_inc(copied, 1)
                    if past := near(i, k, -1, 2, NTURN):
                        send(*past)

                def send(i, k):
                    act.wait_ge(out_ready, i * 2 + (k + 1))
                    act.dma_start(rows[bass.ds(i * 2 * P + k * P, P), :], hb[k][:, 0:wrow]).then_inc(sent[k], 16)
                loop(act, step)
                send(NTURN - 1, 1)
                for k in range(2):
                    act.wait_ge(sent[k], 16 * NTURN)

            @block.vector
            def _(dve):
                st = T.stats[:, :].rearrange("p (t s) -> p t s", s=6)
                link = chain(dve, step_at)
                link(nc.vector.tensor_tensor(mean[:, :], st[:, :, 1], st[:, :, 4], ALU.add))
                link(nc.vector.tensor_scalar(mean[:, :], mean[:, :], 0.5, None, ALU.mult))
                link(nc.vector.tensor_tensor(apart[:, :], st[:, :, 1], st[:, :, 4], ALU.subtract))
                link(nc.vector.tensor_tensor(apart[:, :], apart[:, :], apart[:, :], ALU.mult))
                link(nc.vector.tensor_scalar(apart[:, :], apart[:, :], 0.25, LN_EPS, ALU.mult, ALU.add))
                link(nc.vector.tensor_tensor(dev[:, :], st[:, :, 2], st[:, :, 5], ALU.add))
                link(nc.vector.scalar_tensor_tensor(out=dev[:, :], in0=dev[:, :], scalar=1.0 / D, in1=apart[:, :],
                                                    op0=ALU.mult, op1=ALU.add))
                dve.wait_ge(rooted, 1)
                link(nc.vector.reciprocal(dev[:, :], std[:, :]))

                def norm(i, k):
                    n = i * 2 + k
                    here = T.nodes[:, bass.ds(i * 2 * D + k * D, D)]
                    m, d = mean[:, bass.ds(i * 2 + k, 1)], dev[:, bass.ds(i * 2 + k, 1)]
                    wait_again(dve, stored[k], 16 * i)
                    if kind == "h2":
                        wait_again(dve, times, n - 1)
                        nc.vector.tensor_scalar(raw[k][:, :], here, m, d, ALU.subtract, ALU.mult).then_inc(out_ready, 1)
                        dve.wait_ge(out_ready, n + 1)
                        wait_again(dve, plus, n - 1)
                        nc.vector.tensor_tensor(mul[k][:, :], raw[k][:, :], T.gamma[:, :], ALU.mult).then_inc(times, 1)
                        dve.wait_ge(times, n + 1)
                        nc.vector.tensor_tensor(ob[k][:, :], mul[k][:, :], T.beta[:, :], ALU.add).then_inc(normed, 1)
                    else:
                        if weight is not None:
                            wait_again(dve, turned, n - 1)
                        if kind == "x2":
                            wait_again(dve, plus, n - 1)
                            wait_again(dve, noted, n - 1)
                        nc.vector.tensor_scalar(ob[k][:, :], here, m, d, ALU.subtract, ALU.mult).then_inc(normed, 1)
                    if kind in ("x2", "h2"):
                        dve.wait_ge(normed, n + 1)
                        nc.vector.tensor_scalar(here, ob[k][:, :], 0.0, None, ALU.add).then_inc(plus, 1)
                    if kind == "x2":
                        dve.sem_inc(told, 1)
                        nc.vector.bn_stats(T.stats[:, bass.ds(i * 12 + 6 * k, 6)], ob[k][:, :]).then_inc(noted, 1)

                def give(i, k):
                    n = i * 2 + k
                    dve.wait_ge(multiplied, n + 1)
                    wait_again(dve, sent[k], 16 * i)
                    nc.vector.tensor_copy(hb[k][:, 0:wrow], py[k][:, 0:wrow]).then_inc(out_ready, 1)
                    if kind == "x1":
                        nc.vector.tensor_copy(T.ar[:, bass.ds(i * 2 * HEADS + k * HEADS, HEADS)], py[k][:, WROW:WCAT])\
                            .then_inc(noted, 1)

                def step(i, k):
                    norm(i, k)
                    if weight is not None:
                        if past := near(i, k, -1, 2, NTURN):
                            give(*past)
                loop(dve, step)
                if weight is not None:
                    give(NTURN - 1, 1)

            @block.tensor
            def _(pe):
                if weight is None:
                    return

                def step(i, k):
                    n = i * 2 + k
                    pe.wait_ge(normed, n + 1)
                    wait_again(pe, copied, n - 1)
                    nc.tensor.transpose(pa[k][:, 0:P], ob[k][:, :], T.ident[:, :]).then_inc(turned, 1)
                    pe.wait_ge(copied, n + 1)
                    wait_again(pe, noted if kind == "x1" else out_ready, n - 1)
                    y = py[k][:, 0:width]
                    if bias is not None:
                        nc.tensor.matmul(y, T.ones[0:1, :], bias[0:1, :], start=True, stop=False)
                    nc.tensor.matmul(y, vt[k][:, :], weight[:, 0:width], start=bias is None, stop=True)\
                        .then_inc(multiplied, 1)
                loop(pe, step)
        S.clear()


class Bag:
    pass




def build(nc, X):
    with ExitStack() as ctx:
        T = Bag()
        T.moves = Moves(nc, ctx)

        def sb(c, name, shape, dt):
            t = c.enter_context(nc.sbuf_tensor(name, shape, dt))
            return t
        T.ident = sb(ctx, "ident", [P, P], F32)
        T.ident_b = sb(ctx, "ident_b", [P, P], BF16)
        T.ones = sb(ctx, "ones", [P, P], F32)
        T.ones_b = sb(ctx, "ones_b", [P, P], BF16)
        T.iota1_f = sb(ctx, "iota1_f", [P, P], F32)
        T.tile_s = sb(ctx, "tile_s", [1, C], I32)
        T.tile_d = sb(ctx, "tile_d", [1, C], I32)
        with ExitStack() as sort:
            T.before = sb(sort, "before", [P, P], F32)
            T.upto = sb(sort, "upto", [P, P], F32)
            T.zero_b = sb(sort, "zero_b", [P, P], BF16)
            T.iota_i = sb(sort, "iota_i", [P, P], I32)
            T.iota_b = sb(sort, "iota_b", [P, P], BF16)
            T.part_i = sb(sort, "part_i", [P, 1], I32)
            T.part_f = sb(sort, "part_f", [P, 1], F32)
            T.ident128_b = sb(sort, "ident128_b", [P, P], BF16)
            T.chunk_i = sb(sort, "chunk_i", [P, C], I32)
            T.chunk_f = sb(sort, "chunk_f", [P, C], F32)
            T.slo_b = sb(sort, "slo_b", [R, ROWE], BF16)
            T.shi_b = sb(sort, "shi_b", [R, ROWE], BF16)
            T.dlo_b = sb(sort, "dlo_b", [R, ROWE], BF16)
            T.dhi_b = sb(sort, "dhi_b", [R, ROWE], BF16)
            T.scol = sb(sort, "scol", [P, ROWCH * R], F32)
            T.dcol = sb(sort, "dcol", [P, ROWCH * R], F32)
            T.shicol = sb(sort, "shicol", [P, ROWCH * R], F32)
            T.dhicol = sb(sort, "dhicol", [P, ROWCH * R], F32)
            T.colp = sb(sort, "colp", [P, ROWCH * R], I32)
            T.meta_src = sb(sort, "meta_src", [P, ROWCH, R, 4], F32)
            T.meta_dst = sb(sort, "meta_dst", [P, ROWCH, R, 4], F32)
            T.hist_s = sb(sort, "hist_s", [P, NT], F32)
            T.hist_d = sb(sort, "hist_d", [P, NT], F32)
            T.first_s = sb(sort, "first_s", [P, NT], F32)
            T.first_d = sb(sort, "first_d", [P, NT], F32)
            build_constants(nc, T)
            build_prepare(nc, T, X)
            build_histogram(nc, T)
            build_offsets(nc, T)
            build_place(nc, T, X, True)
            build_place(nc, T, X, False)
        T.m_src = sb(ctx, "m_src", [P, C, 4], F32)
        T.last_src = sb(ctx, "last_src", [P, C], F32)
        T.acc = sb(ctx, "acc", [P, NT * ROW], F32)
        T.cat1 = sb(ctx, "cat1", [P, WCAT], F32)
        T.cat2 = sb(ctx, "cat2", [P, WCAT], F32)
        T.w0t = sb(ctx, "w0t", [P, 2 * D], F32)
        T.w1 = sb(ctx, "w1", [P, 2 * D], F32)
        T.w2 = sb(ctx, "w2", [P, 2, D], F32)
        T.wt = sb(ctx, "wt", [P, D], F32)
        T.w3 = sb(ctx, "w3", [P, D], F32)
        T.wres = sb(ctx, "wres", [P, D], F32)
        T.b1c = sb(ctx, "b1c", [P, 2], F32)
        T.b0r = sb(ctx, "b0r", [1, D], F32)
        T.b2r = sb(ctx, "b2r", [1, D], F32)
        T.btr = sb(ctx, "btr", [1, D], F32)
        T.b3r = sb(ctx, "b3r", [1, D], F32)
        T.bresr = sb(ctx, "bresr", [1, D], F32)
        T.bg1 = sb(ctx, "bg1", [P, D], F32)
        T.bg2 = sb(ctx, "bg2", [P, D], F32)
        T.gamma = sb(ctx, "gamma", [P, D], F32)
        T.beta = sb(ctx, "beta", [P, D], F32)
        T.stats = sb(ctx, "stats", [P, NT * 6], F32)
        build_weights(nc, T, X)
        build_flags(nc, T, X, True)
        build_max_edges(nc, T, X)
        with ExitStack() as gat:
            T.m_dst = sb(gat, "m_dst", [P, C, 4], F32)
            T.last_dst = sb(gat, "last_dst", [P, C], F32)
            build_flags(nc, T, X, False)
            T.ar = sb(gat, "ar", [P, NT * HEADS], F32)
            with ExitStack() as table:
                T.nodes = sb(table, "nodes_a", [P, NT * D], F32)
                build_nodes(nc, T, X, "sage")
                build_norm(nc, T, X, "x1")
            with ExitStack() as table:
                T.top = sb(table, "top", [P, NT * HEADS], F32)
                build_gat_edges(nc, T, X, "ga")
            build_nodes(nc, T, X, "gat_mid")
            with ExitStack() as table:
                T.top = sb(table, "top_b", [P, NT * HEADS], F32)
                build_gat_edges(nc, T, X, "gb")
        T.nodes = sb(ctx, "nodes_b", [P, NT * D], F32)
        build_nodes(nc, T, X, "gat_end")
        build_norm(nc, T, X, "x2")
        build_norm(nc, T, X, "h2")
        build_mlp_edges(nc, T, X)
        build_nodes(nc, T, X, "mlp")
        build_norm(nc, T, X, "x3")
        build_gcn_edges(nc, T, X)
        build_nodes(nc, T, X, "gcn")
        build_norm(nc, T, X, "out")


_INS = ['x', 'src', 'dst', 'edge_attr_128', 'edge_weight', 'L0_gnn_W', 'L0_gnn_b', 'L1_gnn_W1', 'L1_gnn_att_l1', 'L1_gnn_att_r1', 'L1_gnn_b1', 'L1_gnn_W2', 'L1_gnn_att_l2', 'L1_gnn_att_r2', 'L1_gnn_b2', 'L2_gnn_ln_gamma', 'L2_gnn_ln_beta', 'L2_gnn_W1', 'L2_gnn_b1', 'L2_gnn_W2', 'L2_gnn_b2', 'L2_gnn_Wt', 'L2_gnn_bt', 'L3_gnn_W', 'L3_gnn_b', 'L3_gnn_Wres', 'L3_gnn_bres']


def kernel(**inputs):
    import numpy as _np
    import concourse.bacc as _bacc
    from concourse import mybir as _mybir
    from concourse.bass_utils import run_bass_kernel_spmd as _run

    nc = _bacc.Bacc("TRN2", target_bir_lowering=False, num_devices=1)
    X = Bag()
    arrays = {}
    for name in _INS:
        a = _np.ascontiguousarray(inputs[name])
        arrays[f"in_{name}_dram"] = a
        X.__dict__[name] = nc.dram_tensor(f"in_{name}_dram", a.shape, _mybir.dt.from_np(a.dtype), kind="ExternalInput").ap()
    X.out = nc.dram_tensor("out_0_dram", (N, D), F32, kind="ExternalOutput").ap()
    for name, shape, dt in (("xpad", (NPAD, D), F32), ("rec_src", (Q, REC), F32), ("rec_dst", (Q, 4), F32),
                            ("keys_src", (Q + 2,), F32), ("keys_dst", (Q + 2,), F32),
                            ("reset_src", (Q,), BF16), ("reset_dst", (Q,), BF16),
                            ("hrow", (NPAD, WROW), F32), ("x1", (NPAD, D), F32), ("x2", (NPAD, D), F32),
                            ("h2row", (NPAD, D), F32), ("x3", (NPAD, D), F32), ("h3row", (NPAD, D), F32)):
        X.__dict__[name] = nc.dram_tensor(f"s_{name}", shape, dt, kind="Internal").ap()
    build(nc, X)
    r = _run(nc, [arrays], core_ids=[0])
    return r.results[0]["out_0_dram"]
```

```python
from contextlib import ExitStack

import concourse.bass as bass
from concourse import mybir

ALU = mybir.AluOpType
ACT = mybir.ActivationFunctionType
AX = mybir.AxisListType
F32 = mybir.dt.float32
BF16 = mybir.dt.bfloat16
I32 = mybir.dt.int32
U32 = mybir.dt.uint32

P = 128
N = 12500
E = 200000
D = 128
NT = -(-N // P)
NPAD = NT * P
SPARE = NPAD - 1
HEADS = 4
HID = D // HEADS
LN_EPS = 1e-5
NEG = -3.0e38
LOW = -1.0e30

ROWCH = 16
ROWE = ROWCH * P
EROWS = E // ROWE
ECH = -(-E // P)
TAILCH = ECH - EROWS * ROWCH
TAILE = E - EROWS * ROWE
R = EROWS + 1

CBLK = -(-((ECH * P + NT * (P - 1)) // P) // P)
C = CBLK * P
Q = C * P
U = 4
ITERS = C // (4 * U)
REC = D + 4
ROW = D + HEADS
BASE = 8


def wait_again(eng, sem, value):
    if not (isinstance(value, int) and value <= 0):
        eng.wait_ge(sem, value)


class Sems:

    def __init__(self, nc, ctx, phase):
        self.nc, self.ctx, self.phase, self.all = nc, ctx, phase, []

    def __call__(self, name):
        s = self.ctx.enter_context(self.nc.semaphore(f"{self.phase}_{name}"))
        self.all.append(s)
        return s

    def clear(self):
        with self.nc.Block() as block:
            @block.sync
            def _(sp):
                for s in self.all:
                    sp.sem_clear(s)


class Moves:

    def __init__(self, nc, ctx):
        self.sems = [[ctx.enter_context(nc.semaphore(f"moved{g}_{j}")) for j in range(U)] for g in range(4)]
        self.before = [[0] * U for _ in range(4)]

    def wait(self, eng, i, g, chunks=range(U)):
        for j in chunks:
            eng.wait_ge(self.sems[g][j], i * 16 + (self.before[g][j] + 16))

    def wait_last(self, eng, i, g):
        if not (isinstance(i, int) and i == 0):
            for j in range(U):
                eng.wait_ge(self.sems[g][j], i * 16 + self.before[g][j])

    def close(self, count):
        for g in range(4):
            for j in range(U):
                self.before[g][j] += 16 * count(g, j)


def chain(eng, sem):
    count = [0]

    def link(ins):
        count[0] += 1
        ins.then_inc(sem, 1)
        eng.wait_ge(sem, count[0])
    return link


def spread(ap, n):
    return ap.unsqueeze(2).broadcast_to([ap.shape[0], ap.shape[1], n])


def repeat(ap, n):
    return ap.unsqueeze(1).broadcast_to([ap.shape[0], n, ap.shape[1]])


def build_constants(nc, T):
    with ExitStack() as ctx:
        S = Sems(nc, ctx, "const")
        filled, cut, copied = S("filled"), S("cut"), S("copied")
        with nc.Block() as block:
            @block.gpsimd
            def _(pool):
                pool.memset(T.ident[:, :], 0.0).then_inc(filled, 1)
                pool.memset(T.before[:, :], 1.0).then_inc(filled, 1)
                pool.memset(T.upto[:, :], 1.0).then_inc(filled, 1)
                pool.memset(T.ones[:, :], 1.0).then_inc(filled, 1)
                pool.memset(T.ones_b[:, :], 1.0).then_inc(filled, 1)
                pool.memset(T.zero_b[:, :], 0.0).then_inc(filled, 1)
                pool.wait_ge(filled, 6)
                pool.affine_select(out=T.ident[:, :], in_=T.ident[:, :], compare_op=ALU.not_equal, fill=1.0,
                                   base=0, pattern=[[-1, P]], channel_multiplier=1).then_inc(cut, 1)
                pool.affine_select(out=T.before[:, :], in_=T.before[:, :], compare_op=ALU.is_gt, fill=0.0,
                                   base=0, pattern=[[-1, P]], channel_multiplier=1).then_inc(cut, 1)
                pool.affine_select(out=T.upto[:, :], in_=T.upto[:, :], compare_op=ALU.is_gt, fill=0.0,
                                   base=0, pattern=[[1, P]], channel_multiplier=-1).then_inc(cut, 1)
                pool.iota(T.iota_i[:, :], pattern=[[1, P]], base=0, channel_multiplier=0).then_inc(cut, 1)
                pool.iota(T.part_i[:, :], pattern=[[0, 1]], base=0, channel_multiplier=1).then_inc(cut, 1)
                pool.iota(T.chunk_i[:, :], pattern=[[1, C]], base=0, channel_multiplier=0).then_inc(cut, 1)

            @block.vector
            def _(dve):
                dve.wait_ge(cut, 6)
                nc.vector.tensor_copy(T.iota_b[:, :], T.iota_i[:, :]).then_inc(copied, 1)
                nc.vector.tensor_scalar(T.iota1_f[:, :], T.iota_i[:, :], 1.0, None, ALU.add).then_inc(copied, 1)
                nc.vector.tensor_copy(T.part_f[:, :], T.part_i[:, :]).then_inc(copied, 1)
                nc.vector.tensor_copy(T.ident_b[:, :], T.ident[:, :]).then_inc(copied, 1)
                nc.vector.tensor_scalar(T.ident128_b[:, :], T.ident[:, :], float(P), None, ALU.mult)\
                    .then_inc(copied, 1)
                nc.vector.tensor_copy(T.chunk_f[:, :], T.chunk_i[:, :]).then_inc(copied, 1)
        S.clear()


def build_prepare(nc, T, X):
    with ExitStack() as ctx:
        S = Sems(nc, ctx, "prep")
        dummy, loaded, xin, xout = S("dummy"), S("loaded"), S("xin"), S("xout")
        zero_set, zeroed, dve_at, turned, taken = S("zero_set"), S("zeroed"), S("dve_at"), S("turned"), S("taken")
        src_r = ctx.enter_context(nc.sbuf_tensor("src_r", [R, ROWE], I32))
        dst_r = ctx.enter_context(nc.sbuf_tensor("dst_r", [R, ROWE], I32))
        ew_r = ctx.enter_context(nc.sbuf_tensor("ew_r", [R, ROWE], F32))
        key_f = ctx.enter_context(nc.sbuf_tensor("key_f", [R, ROWE], F32))
        part = ctx.enter_context(nc.sbuf_tensor("part", [R, ROWE], I32))
        col_i = ctx.enter_context(nc.sbuf_tensor("col_i", [P, ROWCH * R], I32))
        zeros = ctx.enter_context(nc.sbuf_tensor("zeros", [P, 16 * REC], F32))
        ps = [ctx.enter_context(nc.psum_tensor(f"ps_prep{k}", [P, 512], F32)) for k in range(2)]
        XR = 100
        xb = ctx.enter_context(nc.sbuf_tensor("xb", [125, XR // 4 * D], F32))
        NB = C // 16
        with nc.Block() as block:
            @block.sync
            def _(sp):
                sp.wait_ge(dummy, 4)
                for t, a in ((src_r, X.src), (dst_r, X.dst), (ew_r, X.edge_weight)):
                    sp.dma_start(t[0:EROWS, :], a[0:EROWS * ROWE].rearrange("(r e) -> r e", e=ROWE))\
                        .then_inc(loaded, 16)
                    sp.dma_start(t[EROWS:R, 0:TAILE], a[EROWS * ROWE:E].rearrange("(r e) -> r e", r=1))\
                        .then_inc(loaded, 16)
                xr, xo = X.x.rearrange("(p k) f -> p (k f)", p=125), X.xpad[0:N, :].rearrange("(p k) f -> p (k f)", p=125)
                w = XR // 4 * D
                for k in range(4):
                    sp.dma_start(xb[:, :], xr[:, k * w:(k + 1) * w]).then_inc(xin, 16)
                    sp.wait_ge(xin, 16 * (k + 1))
                    sp.dma_start(xo[:, k * w:(k + 1) * w], xb[:, :]).then_inc(xout, 16)
                    sp.wait_ge(xout, 16 * (k + 1))
                sp.wait_ge(zero_set, 1)
                sp.dma_start(X.xpad[N:NPAD, :], zeros[0:NPAD - N, 0:D]).then_inc(xout, 16)
                sp.wait_ge(xout, 16 * 5)

            @block.scalar
            def _(act):
                act.wait_ge(zero_set, 1)
                act.dma_start(X.rec_dst.rearrange("(p k) f -> p (k f)", p=P)[:, 0:16 * REC * 3],
                              zeros[:, :].unsqueeze(1).broadcast_to([P, 3, 16 * REC])).then_inc(zeroed, 16)
                act.dma_start(X.rec_dst.rearrange("(p k) f -> p (k f)", p=P)[:, 16 * REC * 3:4 * C],
                              zeros[:, 0:4 * C - 16 * REC * 3]).then_inc(zeroed, 16)
                rows = X.rec_src.rearrange("(p b k) f -> b p (k f)", p=P, k=16)
                with act.Fori(0, NB) as b:
                    act.dma_start(rows[bass.ds(b, 1)].squeeze(0), zeros[:, :]).then_inc(zeroed, 16)
                act.wait_ge(zeroed, 16 * (NB + 2))

            @block.vector
            def _(dve):
                nc.vector.memset(src_r[:, :], SPARE).then_inc(dummy, 1)
                nc.vector.memset(dst_r[:, :], SPARE).then_inc(dummy, 1)
                nc.vector.memset(ew_r[:, :], 0.0).then_inc(dummy, 1)
                nc.vector.memset(zeros[:, :], 0.0).then_inc(zero_set, 1)
                nc.vector.memset(T.meta_src[:, :, :, :], 0.0).then_inc(dummy, 1)
                nc.vector.memset(T.meta_dst[:, :, :, :], 0.0).then_inc(dve_at, 1)
                link_n = [1]

                def link(ins):
                    link_n[0] += 1
                    ins.then_inc(dve_at, 1)
                    dve.wait_ge(dve_at, link_n[0])
                dve.wait_ge(loaded, 16 * 6)
                dve.wait_ge(dummy, 4)
                dve.wait_ge(dve_at, 1)
                for k_r, lo_b, hi_b, col, hicol, mine, other in (
                        (src_r, T.slo_b, T.shi_b, T.scol, T.shicol, T.meta_src, T.meta_dst),
                        (dst_r, T.dlo_b, T.dhi_b, T.dcol, T.dhicol, T.meta_dst, T.meta_src)):
                    n = 0 if k_r is src_r else 1
                    link(nc.vector.tensor_scalar(part[:, :], k_r[:, :], P - 1, None, ALU.bitwise_and))
                    link(nc.vector.tensor_copy(lo_b[:, :], part[:, :]))
                    link(nc.vector.tensor_scalar(part[:, :], k_r[:, :], 7, None, ALU.logical_shift_right))
                    link(nc.vector.tensor_copy(hi_b[:, :], part[:, :]))
                    if n:
                        dve.wait_ge(turned, 4)
                    link(nc.vector.tensor_copy(key_f[:, :], k_r[:, :]))
                    for g in range(4):
                        dve.wait_ge(turned, 4 * n + g + 1)
                        nc.vector.tensor_copy(col[:, g * 4 * R:(g + 1) * 4 * R], ps[g % 2][:, 0:4 * R])\
                            .then_inc(taken, 1)
                    dve.wait_ge(taken, 4 * n + 4)
                    link(nc.vector.tensor_copy(col_i[:, :], col[:, :]))
                    flat = mine[:, :, :, :].rearrange("p b r f -> p (b r) f")
                    link(nc.vector.tensor_scalar(flat[:, :, 3], col[:, :], 1.0, None, ALU.add))
                    link(nc.vector.tensor_copy(other[:, :, :, :].rearrange("p b r f -> p (b r) f")[:, :, 0],
                                               col[:, :]))
                    link(nc.vector.tensor_scalar(part2 := T.colp[:, :], col_i[:, :], P - 1, None, ALU.bitwise_and))
                    link(nc.vector.tensor_scalar(flat[:, :, 2], part2, 1.0, None, ALU.add))
                    link(nc.vector.tensor_scalar(part2, col_i[:, :], 7, None, ALU.logical_shift_right))
                    link(nc.vector.tensor_copy(hicol[:, :], part2))
                for g in range(4):
                    dve.wait_ge(turned, 8 + g + 1)
                    for m, meta in enumerate((T.meta_src, T.meta_dst)):
                        ins = nc.vector.tensor_copy(meta[:, 4 * g:4 * g + 4, :, 1],
                                                    ps[g % 2][:, 0:4 * R].rearrange("p (b r) -> p b r", r=R))
                    ins.then_inc(taken, 1)

            @block.tensor
            def _(pe):
                pe.wait_ge(loaded, 16 * 6)
                for n, rows in enumerate((key_f, key_f, ew_r)):
                    if n < 2:
                        pe.wait_ge(dve_at, (6, 6 + 7 + 5)[n])
                    for g in range(4):
                        u = 4 * n + g
                        if u >= 2:
                            pe.wait_ge(taken, u - 1)
                        for j in range(4):
                            b = 4 * g + j
                            ins = nc.tensor.transpose(ps[g % 2][:, j * R:(j + 1) * R], rows[:, b * P:(b + 1) * P],
                                                      T.ident[0:R, 0:R])
                        ins.then_inc(turned, 1)
        S.clear()


def build_histogram(nc, T):
    with ExitStack() as ctx:
        S = Sems(nc, ctx, "hist")
        hot_ready, counted, stored = S("hot_ready"), S("counted"), S("stored")
        hot_lo = [ctx.enter_context(nc.sbuf_tensor(f"hist_lo{k}", [P, U, P], BF16)) for k in range(2)]
        hot_hi = [ctx.enter_context(nc.sbuf_tensor(f"hist_hi{k}", [P, U, NT], BF16)) for k in range(2)]
        ps = [ctx.enter_context(nc.psum_tensor(f"ps_hist{k}", [P, 512], F32)) for k in range(2)]
        metas, hicols = (T.meta_src, T.meta_dst), (T.shicol, T.dhicol)

        def units(eng, unit):
            with eng.Fori(0, EROWS) as i:
                for g in range(4):
                    for k in range(2):
                        unit(k, i, g, U, i * 8 + (2 * g + k))
            for g in range(-(-TAILCH // U)):
                for k in range(2):
                    unit(k, EROWS, g, min(U, TAILCH - U * g), EROWS * 8 + 2 * g + k)
        NU = EROWS * 8 + 2 * -(-TAILCH // U)

        with nc.Block() as block:
            @block.vector
            def _(dve):
                def unit(k, i, g, m, n):
                    dve.wait_ge(counted, n + 1)
                    lo = metas[k][:, 4 * g:4 * g + m, bass.ds(i, 1), 2].squeeze(2)
                    hi = hicols[k][:, :].rearrange("p (b r) -> p b r", r=R)[:, 4 * g:4 * g + m, bass.ds(i, 1)].squeeze(2)
                    nc.vector.tensor_tensor(hot_lo[k][:, 0:m, :], repeat(T.iota1_f[:, :], m), spread(lo, P),
                                            ALU.is_equal)
                    nc.vector.tensor_tensor(hot_hi[k][:, 0:m, :], repeat(T.iota_b[:, 0:NT], m), spread(hi, NT),
                                            ALU.is_equal).then_inc(hot_ready, 1)
                units(dve, unit)
                for k, h in enumerate((T.hist_s, T.hist_d)):
                    dve.wait_ge(counted, NU + 2)
                    nc.vector.tensor_copy(h[:, :], ps[k][:, 0:NT]).then_inc(stored, 1)

            @block.tensor
            def _(pe):
                pe.sem_inc(counted, 2)
                for k in range(2):
                    nc.tensor.matmul(ps[k][:, 0:NT], T.ident_b[:, :], T.zero_b[:, 0:NT], start=True, stop=False,
                                     skip_group_check=True)

                def unit(k, i, g, m, n):
                    pe.wait_ge(hot_ready, n + 1)
                    for j in range(m):
                        ins = nc.tensor.matmul(ps[k][:, 0:NT], hot_lo[k][:, j, :], hot_hi[k][:, j, :],
                                               start=False, stop=False, skip_group_check=True)
                    ins.then_inc(counted, 1)
                units(pe, unit)
        S.clear()


def build_offsets(nc, T):
    with ExitStack() as ctx:
        S = Sems(nc, ctx, "offs")
        dve_at, pe_at = S("dve_at"), S("pe_at")
        cnt_i = ctx.enter_context(nc.sbuf_tensor("cnt_i", [P, NT], I32))
        cnt_j = ctx.enter_context(nc.sbuf_tensor("cnt_j", [P, NT], I32))
        ch = ctx.enter_context(nc.sbuf_tensor("ch", [P, NT + 1], F32))
        upto_ch = ctx.enter_context(nc.sbuf_tensor("upto_ch", [P, NT + 1], F32))
        first_ch = ctx.enter_context(nc.sbuf_tensor("first_ch", [P, 1], F32))
        reached = ctx.enter_context(nc.sbuf_tensor("reached", [P, C], BF16))
        tile_f = ctx.enter_context(nc.sbuf_tensor("tile_f", [1, C], F32))
        pc = ctx.enter_context(nc.psum_tensor("ps_cnt", [P, 512], F32))
        pp = ctx.enter_context(nc.psum_tensor("ps_pre", [P, 512], F32))
        pf = ctx.enter_context(nc.psum_tensor("ps_fst", [P, 512], F32))
        NW = -(-C // 512)
        pt = [ctx.enter_context(nc.psum_tensor(f"ps_til{k}", [P, 512], F32)) for k in range(NW)]
        STEPS = 11 + NW
        with nc.Block() as block:
            @block.vector
            def _(dve):
                link = chain(dve, dve_at)
                for k, (h, first, tiles) in enumerate(((T.hist_s, T.first_s, T.tile_s), (T.hist_d, T.first_d, T.tile_d))):
                    dve.wait_ge(pe_at, 3 * k + 1)
                    link(nc.vector.tensor_scalar(cnt_i[:, :], pc[:, 0:NT], float(P - 1), None, ALU.add))
                    link(nc.vector.tensor_scalar(cnt_j[:, :], cnt_i[:, :], 7, None, ALU.logical_shift_right))
                    link(nc.vector.memset(ch[:, 0:1], 0.0))
                    link(nc.vector.tensor_copy(ch[:, 1:NT + 1], cnt_j[:, :]))
                    link(nc.vector.tensor_tensor_scan(upto_ch[:, :], ch[:, :], ch[:, :], 0.0, ALU.add, ALU.max))
                    link(nc.vector.scalar_tensor_tensor(out=first[:, :], in0=upto_ch[:, 0:NT], scalar=float(P),
                                                        in1=pp[:, 0:NT], op0=ALU.mult, op1=ALU.add))
                    dve.wait_ge(pe_at, 3 * k + 2)
                    link(nc.vector.tensor_copy(first_ch[0:NT, :], pf[0:NT, 0:1]))
                    link(nc.vector.tensor_scalar(reached[0:NT, :], T.chunk_f[0:NT, :], first_ch[0:NT, 0:1], None, ALU.is_ge))
                    dve.wait_ge(pe_at, 3 * k + 3)
                    for w in range(NW):
                        a, b = w * 512, min(C, w * 512 + 512)
                        link(nc.vector.tensor_scalar(tile_f[0:1, a:b], pt[w][0:1, 0:b - a], -1.0, None, ALU.add))
                    link(nc.vector.tensor_copy(tiles[:, :], tile_f[:, :]))

            @block.tensor
            def _(pe):
                for k, h in enumerate((T.hist_s, T.hist_d)):
                    if k:
                        pe.wait_ge(dve_at, 9 + NW)
                    nc.tensor.matmul(pc[:, 0:NT], T.ones[:, :], h[:, :], start=True, stop=True)
                    nc.tensor.matmul(pp[:, 0:NT], T.upto[:, :], h[:, :], start=True, stop=True).then_inc(pe_at, 1)
                    pe.wait_ge(dve_at, (9 + NW) * k + 5)
                    nc.tensor.matmul(pf[0:NT, 0:1], upto_ch[0:1, 0:NT], T.ones[0:1, 0:1], start=True, stop=True)\
                        .then_inc(pe_at, 1)
                    pe.wait_ge(dve_at, (9 + NW) * k + 8)
                    for w in range(NW):
                        a, b = w * 512, min(C, w * 512 + 512)
                        ins = nc.tensor.matmul(pt[w][0:1, 0:b - a], T.ones_b[0:NT, 0:1], reached[0:NT, a:b],
                                               start=True, stop=True)
                    ins.then_inc(pe_at, 1)
        S.clear()


def build_place(nc, T, X, by_src):
    name = "pls" if by_src else "pld"
    lo_b, hi_b = (T.slo_b, T.shi_b) if by_src else (T.dlo_b, T.dhi_b)
    col, hicol = (T.scol, T.shicol) if by_src else (T.dcol, T.dhicol)
    meta, first = (T.meta_src, T.first_s) if by_src else (T.meta_dst, T.first_d)
    width = REC if by_src else 4
    target = X.rec_src if by_src else X.rec_dst
    TAILU = -(-TAILCH // U)
    with ExitStack() as ctx:
        S = Sems(nc, ctx, name)
        rows_ready, rows_free, hot_ready = S("rows_ready"), S("rows_free"), S("hot_ready")
        table_at, table_read, slots_ready = S("table_at"), S("table_read"), S("slots_ready")
        at_read, at_summed = S("at_read"), S("at_summed")
        meta_ready, pool_step = S("meta_ready"), S("pool_step")
        attr_in = [S(f"attr_in{k}") for k in range(4)]

        def sb(n, shape, dt):
            return ctx.enter_context(nc.sbuf_tensor(f"{name}_{n}", shape, dt))

        def pb(n):
            return ctx.enter_context(nc.psum_tensor(f"{name}_{n}", [P, 512], F32))
        lo_hot = [sb(f"lo_hot{k}", [P, U, P], BF16) for k in range(2)]
        hi_hot = [sb(f"hi_hot{k}", [P, U, NT], BF16) for k in range(2)]
        hi_f = [sb(f"hi_f{k}", [P, U, NT], F32) for k in range(2)]
        lo_hot_t = [sb(f"lo_hot_t{k}", [P, U * P], F32) for k in range(2)]
        same = [sb(f"same{k}", [P, U, P], BF16) for k in range(2)]
        rank = [sb(f"rank{k}", [P, U], F32) for k in range(2)]
        at = [sb(f"at{k}", [P, U], F32) for k in range(2)]
        slot = [sb(f"slot{k}", [P, U], U32) for k in range(4)]
        rec = [sb(f"rec{k}", [P, U, width], F32) for k in range(4)]
        table = [sb(f"table{k}", [P, NT], F32) for k in range(2)]
        ps_lo = [pb(f"ps_lo{k}") for k in range(2)]
        ps_key = [pb(f"ps_key{k}") for k in range(2)]
        ps_at = [pb(f"ps_at{k}") for k in range(2)]
        ps_table = pb("ps_table")

        def turns(eng, unit):
            for g in range(4):
                unit(0, g, U)
            with eng.Fori(1, EROWS) as i:
                for g in range(4):
                    unit(i, g, U)
            for g in range(TAILU):
                unit(EROWS, g, min(U, TAILCH - U * g))

        with nc.Block() as block:
            @block.sync
            def _(sp):
                if by_src:
                    def unit(i, g, m):
                        T.moves.wait_last(sp, i, g)
                        rows = X.edge_attr_128[bass.ds(i * ROWE + g * U * P, m * P), :]
                        sp.dma_start(rec[g][:, 0:m, 0:D], rows.rearrange("(j e) f -> e j f", e=P)).then_inc(attr_in[g], 16)
                    for g in range(4):
                        unit(0, g, U)
                    with sp.Fori(1, EROWS) as i:
                        for g in range(4):
                            unit(i, g, U)
                    for g in range(TAILU):
                        m = min(U, TAILCH - U * g)
                        if (EROWS * ROWCH + U * g + m) * P <= E:
                            unit(EROWS, g, m)
                        else:
                            a = EROWS * ROWE + g * U * P
                            full = (E - a) // P
                            T.moves.wait_last(sp, EROWS, g)
                            sp.dma_start(rec[g][:, 0:full, 0:D], X.edge_attr_128[a:a + full * P, :]
                                         .rearrange("(j e) f -> e j f", e=P)).then_inc(attr_in[g], 16)
                            sp.dma_start(rec[g][0:E - a - full * P, full, 0:D], X.edge_attr_128[a + full * P:E, :])\
                                .then_inc(attr_in[g], 16)

            @block.gpsimd
            def _(pool):

                def unit(i, g, m):
                    pool.wait_ge(slots_ready, i * 4 + (g + 1))
                    pool.wait_ge(meta_ready, i * 4 + (g + 1))
                    if by_src:
                        pool.wait_ge(attr_in[g], i * 16 + (16 if m == U else 32))
                    pool.sem_inc(pool_step, 1)
                    for j in range(m):
                        pool.indirect_dma_start(target[:, :], bass.IndirectOffsetOnAxis(ap=slot[g][:, j:j + 1], axis=0),
                                                rec[g][:, j, :], None).then_inc(T.moves.sems[g][j], 16)
                turns(pool, unit)
                for g in range(4):
                    tail = range(max(0, min(U, TAILCH - U * g)))
                    T.moves.wait(pool, EROWS, g, tail)
                    T.moves.wait(pool, EROWS - 1, g, range(len(tail), U))

            @block.scalar
            def _(act):
                def unit(i, g, m):
                    T.moves.wait_last(act, i, g)
                    nc.scalar.copy(rec[g][:, 0:m, width - 4:width],
                                   meta[:, 4 * g:4 * g + m, bass.ds(i, 1), :].squeeze(2)).then_inc(meta_ready, 1)
                    for j in range(m):
                        n = i * ROWCH + (U * g + j)
                        act.wait_ge(table_at, n + BASE)
                        nc.scalar.copy(table[j % 2][:, :], ps_table[:, 0:NT]).then_inc(table_read, 1)
                turns(act, unit)

            @block.vector
            def _(dve):
                dve.sem_inc(rows_free, 2)
                dve.sem_inc(at_read, 2)

                def front(i, g, m):
                    k = g % 2
                    n = i * 4 + g
                    dve.wait_ge(table_at, i * ROWCH + (U * (g - 1) + BASE))
                    lo = meta[:, 4 * g:4 * g + m, bass.ds(i, 1), 2].squeeze(2)
                    hi = hicol[:, :].rearrange("p (b r) -> p b r", r=R)[:, 4 * g:4 * g + m, bass.ds(i, 1)].squeeze(2)
                    nc.vector.tensor_tensor(lo_hot[k][:, 0:m, :], repeat(T.iota1_f[:, :], m), spread(lo, P), ALU.is_equal)
                    nc.vector.tensor_tensor(hi_hot[k][:, 0:m, :], repeat(T.iota_b[:, 0:NT], m), spread(hi, NT), ALU.is_equal)
                    dve.wait_ge(rows_ready, n + 1)
                    nc.vector.tensor_scalar(lo_hot_t[k][:, 0:m * P], ps_lo[k][:, 0:m * P], T.part_f[:, 0:1], None,
                                            ALU.is_equal).then_inc(hot_ready, 1)
                    wait_again(dve, slots_ready, i * 4 + (g - 1))
                    for j in range(m):
                        ins = nc.vector.scalar_tensor_tensor(
                            out=same[k][:, j, :], in0=ps_key[k][:, j * P:(j + 1) * P],
                            scalar=col[:, :].rearrange("p (b r) -> p b r", r=R)[:, 4 * g + j, bass.ds(i, 1)],
                            in1=T.before[:, :], op0=ALU.is_equal, op1=ALU.mult, accum_out=rank[k][:, j:j + 1])
                    ins.then_inc(rows_free, 1)

                def back(i, g, m):
                    k = g % 2
                    dve.wait_ge(table_at, i * ROWCH + (U * g + m + BASE))
                    read = ps_at[k][:, 0:m * NT].rearrange("p (j t) -> p j t", t=NT)
                    nc.vector.tensor_tensor(hi_f[k][:, 0:m, :], hi_hot[k][:, 0:m, :], read, ALU.mult).then_inc(at_read, 1)
                    dve.wait_ge(at_read, i * 4 + (g + 3))
                    nc.vector.tensor_reduce(at[k][:, 0:m], hi_f[k][:, 0:m, :], AX.X, ALU.add).then_inc(at_summed, 1)
                    dve.wait_ge(at_summed, i * 4 + (g + 1))
                    dve.wait_ge(rows_free, i * 4 + (g + 3))
                    T.moves.wait_last(dve, i, g)
                    nc.vector.tensor_tensor(slot[g][:, 0:m], at[k][:, 0:m], rank[k][:, 0:m], ALU.add)\
                        .then_inc(slots_ready, 1)

                front(0, 0, U)
                for g in range(4):
                    front((g + 1) // 4, (g + 1) % 4, U)
                    back(0, g, U)
                with dve.Fori(1, EROWS) as i:
                    for g in range(4):
                        front(i + (g + 1) // 4, (g + 1) % 4, U)
                        back(i, g, U)
                for g in range(TAILU):
                    if g + 1 < TAILU:
                        front(EROWS, g + 1, min(U, TAILCH - U * (g + 1)))
                    back(EROWS, g, min(U, TAILCH - U * g))

            @block.tensor
            def _(pe):
                pe.sem_inc(table_at, BASE - 1)
                nc.tensor.matmul(ps_table[:, 0:NT], T.ident[:, :], first[:, :], start=True, stop=False,
                                 skip_group_check=True).then_inc(table_at, 1)

                def rows(i, g, m):
                    k = g % 2
                    pe.wait_ge(rows_free, i * 4 + (g + 1))
                    pick = T.ident_b[0:R, bass.ds(i, 1)].broadcast_to([R, P])
                    pick128 = T.ident128_b[0:R, bass.ds(i, 1)].broadcast_to([R, P])
                    a, b = g * U * P, (g * U + m) * P
                    nc.tensor.matmul(ps_lo[k][:, 0:m * P], pick, lo_b[:, a:b], start=True, stop=True)
                    nc.tensor.matmul(ps_key[k][:, 0:m * P], pick, lo_b[:, a:b], start=True, stop=False)
                    nc.tensor.matmul(ps_key[k][:, 0:m * P], pick128, hi_b[:, a:b], start=False, stop=True)\
                        .then_inc(rows_ready, 1)

                def unit(i, g, m):
                    k = g % 2
                    pe.wait_ge(hot_ready, i * 4 + (g + 1))
                    pe.wait_ge(at_read, i * 4 + (g + 1))
                    for j in range(m):
                        pe.wait_ge(table_read, i * ROWCH + (U * g + j + 1))
                        nc.tensor.matmul(ps_at[k][:, j * NT:(j + 1) * NT], lo_hot_t[k][:, j * P:(j + 1) * P],
                                         table[j % 2][:, :], start=True, stop=True)
                        nc.tensor.matmul(ps_table[:, 0:NT], lo_hot[k][:, j, :], hi_hot[k][:, j, :], start=False,
                                         stop=False, skip_group_check=True).then_inc(table_at, 1)
                rows(0, 0, U)
                with pe.Fori(0, EROWS) as i:
                    for g in range(4):
                        rows(i + (g + 1) // 4, (g + 1) % 4, U)
                        unit(i, g, U)
                for g in range(TAILU):
                    if g + 1 < TAILU:
                        rows(EROWS, g + 1, min(U, TAILCH - U * (g + 1)))
                    unit(EROWS, g, min(U, TAILCH - U * g))
        T.moves.close(lambda g, j: EROWS + (U * g + j < TAILCH))
        S.clear()


NU = C // U
UROW = U * (D + HEADS)
STRIPS = P // HEADS
SLEN = Q // STRIPS


def turns(eng, unit, depth=4, count=ITERS):
    for g in range(depth):
        unit(0, g)
    with eng.Fori(1, count - 1) as i:
        for g in range(depth):
            unit(i, g)
    for g in range(depth):
        unit(count - 1, g)


def near(i, g, k, depth=4, count=ITERS):
    j, h = i + (g + k) // depth, (g + k) % depth
    return None if isinstance(j, int) and not 0 <= j < count else (j, h)


def tiles_of(nc, eng_type, row, i, g):
    return nc.values_load_multi_w_load_instructions(row[0:1, bass.ds(i * 4 * U + g * U, U)], engines=[eng_type],
                                                    min_val=0, max_val=NT - 1,
                                                    skip_runtime_bounds_check_because="tiles are counted below NT")[1]


def build_flags(nc, T, X, by_src):
    name = "fls" if by_src else "fld"
    m, rec, keys, reset = ((T.m_src, X.rec_src, X.keys_src, X.reset_src) if by_src else
                           (T.m_dst, X.rec_dst, X.keys_dst, X.reset_dst))
    at = D if by_src else 0
    with ExitStack() as ctx:
        S = Sems(nc, ctx, name)
        loaded, turned, taken, stored, shifted, done, dve_at, guard = (
            S("loaded"), S("turned"), S("taken"), S("stored"), S("shifted"), S("done"), S("dve_at"), S("guard"))
        kt = ctx.enter_context(nc.sbuf_tensor(name + "_kt", [P, CBLK, P], F32))
        prev = ctx.enter_context(nc.sbuf_tensor(name + "_prev", [P, CBLK, P], F32))
        nxt = ctx.enter_context(nc.sbuf_tensor(name + "_next", [P, CBLK, P], F32))
        rs = ctx.enter_context(nc.sbuf_tensor(name + "_rs", [P, CBLK, P], BF16))
        re = ctx.enter_context(nc.sbuf_tensor(name + "_re", [P, CBLK, P], BF16))
        edge = ctx.enter_context(nc.sbuf_tensor(name + "_edge", [1, 2], F32))
        ps = [ctx.enter_context(nc.psum_tensor(f"{name}_ps{k}", [P, 512], F32)) for k in range(4)]
        groups = [range(a, min(a + 4, CBLK)) for a in range(0, CBLK, 4)]
        with nc.Block() as block:
            @block.sync
            def _(sp):
                sp.dma_start(m[:, :, :], rec.rearrange("(c p) f -> p c f", p=P)[:, :, at:at + 4]).then_inc(loaded, 16)
                sp.wait_ge(guard, 1)
                sp.dma_start(keys[0:1].unsqueeze(0), edge[:, 0:1]).then_inc(stored, 16)
                sp.dma_start(keys[Q + 1:Q + 2].unsqueeze(0), edge[:, 1:2]).then_inc(stored, 16)
                sp.wait_ge(taken, len(groups))
                view = "(b c p) -> c b p"
                sp.dma_start(keys[1:Q + 1].rearrange(view, b=CBLK, c=P), kt[:, :, :]).then_inc(stored, 16)
                sp.wait_ge(stored, 48)
                sp.dma_start(prev[:, :, :], keys[0:Q].rearrange(view, b=CBLK, c=P)).then_inc(shifted, 16)
                sp.dma_start(nxt[:, :, :], keys[2:Q + 2].rearrange(view, b=CBLK, c=P)).then_inc(shifted, 16)
                sp.wait_ge(dve_at, 3)
                sp.dma_start(reset.rearrange(view, b=CBLK, c=P), rs[:, :, :]).then_inc(done, 16)
                if not by_src:
                    sp.wait_ge(dve_at, 4)
                    sp.dma_start(X.ends_dst.rearrange(view, b=CBLK, c=P), re[:, :, :]).then_inc(done, 16)
                sp.wait_ge(done, 16 if by_src else 32)

            @block.vector
            def _(dve):
                nc.vector.memset(edge[:, :], -1.0).then_inc(guard, 1)
                for n, blocks in enumerate(groups):
                    dve.wait_ge(turned, n + 1)
                    w = len(blocks) * P
                    nc.vector.tensor_copy(kt[:, blocks[0]:blocks[0] + len(blocks), :],
                                          ps[n][:, 0:w].rearrange("c (b p) -> c b p", p=P)).then_inc(taken, 1)
                dve.wait_ge(taken, len(groups))
                dve.wait_ge(shifted, 32)
                link = chain(dve, dve_at)
                link(nc.vector.tensor_tensor(prev[:, :, :], prev[:, :, :], kt[:, :, :], ALU.not_equal))
                link(nc.vector.tensor_tensor(nxt[:, :, :], nxt[:, :, :], kt[:, :, :], ALU.not_equal))
                link(nc.vector.tensor_scalar(rs[:, :, :], prev[:, :, :], NEG, None, ALU.mult))
                if not by_src:
                    link(nc.vector.tensor_scalar(re[:, :, :], nxt[:, :, :], NEG, None, ALU.mult))
                    return
                for n, blocks in enumerate(groups):
                    dve.wait_ge(turned, len(groups) + n + 1)
                    a, b = blocks[0] * P, (blocks[-1] + 1) * P
                    link(nc.vector.tensor_tensor(T.last_src[:, a:b], ps[n][:, 0:b - a], m[:, a:b, 2], ALU.mult))

            @block.tensor
            def _(pe):
                pe.wait_ge(loaded, 16)
                for n, blocks in enumerate(groups):
                    for j, b in enumerate(blocks):
                        ins = nc.tensor.transpose(ps[n][:, j * P:(j + 1) * P], m[:, b * P:(b + 1) * P, 3], T.ident[:, :])
                    ins.then_inc(turned, 1)
                if not by_src:
                    return
                pe.wait_ge(dve_at, 2)
                for n, blocks in enumerate(groups):
                    for j, b in enumerate(blocks):
                        ins = nc.tensor.transpose(ps[n][:, j * P:(j + 1) * P], nxt[:, b, :], T.ident[:, :])
                    ins.then_inc(turned, 1)
        S.clear()


def build_max_edges(nc, T, X):
    with ExitStack() as ctx:
        S = Sems(nc, ctx, "mx")
        idx_ready, turned, scanned, back, vals_ready = S("idx_ready"), S("turned"), S("scanned"), S("back"), S("vals_ready")
        hot_ready, picked, added, pool_step = S("hot_ready"), S("picked"), S("added"), S("pool_step")
        cleared = S("cleared")
        reset_in = [S(f"reset_in{k}") for k in range(4)]

        def sb(n, shape, dt=F32):
            return ctx.enter_context(nc.sbuf_tensor("mx_" + n, shape, dt))

        def pb(n):
            return ctx.enter_context(nc.psum_tensor("mx_" + n, [P, 512], F32))
        idx = [sb(f"idx{k}", [P, U], U32) for k in range(4)]
        rows = [sb(f"rows{k}", [P, U, D]) for k in range(4)]
        reset = [sb(f"reset{k}", [P, U * P], BF16) for k in range(4)]
        run = [sb(f"run{k}", [P, U * P]) for k in range(2)]
        vals = [sb(f"vals{k}", [P, U * D]) for k in range(2)]
        hot = [sb(f"hot{k}", [P, U, P]) for k in range(2)]
        ps_x, ps_b, ps_n = ([pb(f"ps_{n}{k}") for k in range(2)] for n in "xbn")

        with nc.Block() as block:
            @block.gpsimd
            def _(pool):
                def unit(i, g):
                    pool.wait_ge(idx_ready, i * 4 + (g + 1))
                    wait_again(pool, turned, i * 4 + (g - 3))
                    pool.sem_inc(pool_step, 1)
                    for j in range(U):
                        pool.indirect_dma_start(rows[g][:, j, :], None, X.xpad[:, :],
                                                bass.IndirectOffsetOnAxis(ap=idx[g][:, j:j + 1], axis=0))\
                            .then_inc(T.moves.sems[g][j], 16)
                turns(pool, unit)

            @block.sync
            def _(sp):
                def unit(i, g):
                    wait_again(sp, scanned, i * 4 + (g - 3))
                    sp.dma_start(reset[g][:, :], X.reset_src[bass.ds(i * 4 * U * P + g * U * P, U * P)]
                                 .partition_broadcast(P)).then_inc(reset_in[g], 16)
                turns(sp, unit)

            @block.vector
            def _(dve):
                nc.vector.memset(T.acc[:, :], 0.0).then_inc(cleared, 1)

                def take_index(i, g):
                    T.moves.wait_last(dve, i, g)
                    nc.vector.tensor_copy(idx[g][:, :], T.m_src[:, bass.ds(i * 4 * U + g * U, U), 0]).then_inc(idx_ready, 1)

                def add(i, g):
                    tiles = tiles_of(nc, mybir.EngineType.DVE, T.tile_s, i, g)
                    dve.wait_ge(picked, i * 4 + (g + 1))
                    for j in range(U):
                        wait_again(dve, added, i * 16 + (U * g + j))
                        to = T.acc[:, bass.ds(tiles[j] * ROW, D)]
                        nc.vector.tensor_tensor(to, to, ps_n[g % 2][:, j * D:(j + 1) * D], ALU.add).then_inc(added, 1)

                for g in range(3):
                    take_index(0, g)
                dve.wait_ge(cleared, 1)

                def unit(i, g):
                    if then := near(i, g, 3):
                        take_index(*then)
                    n = i * 4 + g
                    dve.wait_ge(reset_in[g], i * 16 + 16)
                    dve.wait_ge(turned, n + 1)
                    wait_again(dve, back, n - 1)
                    wait_again(dve, scanned, n)
                    first = 0.0 if isinstance(i, int) and n == 0 else run[(g - 1) % 2][:, U * P - 1:U * P]
                    nc.vector.tensor_tensor_scan(run[g % 2][:, :], reset[g][:, :], ps_x[g % 2][:, :], first,
                                                 ALU.add, ALU.max).then_inc(scanned, 1)
                    wait_again(dve, picked, n - 1)
                    nc.vector.tensor_tensor(hot[g % 2][:, :, :], repeat(T.iota1_f[:, :], U),
                                            spread(T.last_src[:, bass.ds(i * 4 * U + g * U, U)], P),
                                            ALU.is_equal).then_inc(hot_ready, 1)
                    if past := near(i, g, -2):
                        add(*past)
                turns(dve, unit)
                add(ITERS - 1, 2)
                add(ITERS - 1, 3)

            @block.scalar
            def _(act):
                def unit(i, g):
                    n = i * 4 + g
                    act.wait_ge(back, n + 1)
                    wait_again(act, picked, n - 1)
                    nc.scalar.copy(vals[g % 2][:, :], ps_b[g % 2][:, :]).then_inc(vals_ready, 1)
                turns(act, unit)

            @block.tensor
            def _(pe):
                def turn(i, g):
                    wait_again(pe, scanned, i * 4 + (g - 1))
                    for j in range(U):
                        T.moves.wait(pe, i, g, [j])
                        ins = nc.tensor.transpose(ps_x[g % 2][:, j * P:(j + 1) * P], rows[g][:, j, :], T.ident[:, :])
                    ins.then_inc(turned, 1)

                def turn_back(i, g):
                    pe.wait_ge(scanned, i * 4 + (g + 1))
                    wait_again(pe, vals_ready, i * 4 + (g - 1))
                    for j in range(U):
                        ins = nc.tensor.transpose(ps_b[g % 2][:, j * D:(j + 1) * D], run[g % 2][:, j * P:(j + 1) * P],
                                                  T.ident[:, :])
                    ins.then_inc(back, 1)

                def pick(i, g):
                    pe.wait_ge(vals_ready, i * 4 + (g + 1))
                    pe.wait_ge(hot_ready, i * 4 + (g + 1))
                    wait_again(pe, added, i * 16 + (U * (g - 1)))
                    for j in range(U):
                        ins = nc.tensor.matmul(ps_n[g % 2][:, j * D:(j + 1) * D], hot[g % 2][:, j, :],
                                               vals[g % 2][:, j * D:(j + 1) * D], start=True, stop=True)
                    ins.then_inc(picked, 1)

                turn(0, 0)

                def unit(i, g):
                    if then := near(i, g, 1):
                        turn(*then)
                    turn_back(i, g)
                    if past := near(i, g, -1):
                        pick(*past)
                turns(pe, unit)
                pick(ITERS - 1, 3)
        T.moves.close(lambda g, j: ITERS)
        S.clear()


def build_gat_logits(nc, T, X, name):
    with ExitStack() as ctx:
        S = Sems(nc, ctx, name)
        idx_ready, hot_ready, hot_turned, hot_copied, ar_read, z_ready, pool_step = (S(n) for n in (
            "idx_ready", "hot_ready", "hot_turned", "hot_copied", "ar_read", "z_ready", "pool_step"))
        stored = [S(f"stored{k}") for k in range(4)]

        def sb(n, shape, dt=F32):
            return ctx.enter_context(nc.sbuf_tensor(f"{name}_{n}", shape, dt))

        def pb(n):
            return ctx.enter_context(nc.psum_tensor(f"{name}_{n}", [P, 512], F32))
        idx = [sb(f"idx{k}", [P, U], U32) for k in range(4)]
        rows = [sb(f"rows{k}", [P, U, HEADS, HID + 1]) for k in range(4)]
        hot = [sb(f"hot{k}", [P, U, P]) for k in range(2)]
        hot_t = [sb(f"hot_t{k}", [P, U * P]) for k in range(2)]
        ps_t = [pb(f"ps_t{k}") for k in range(2)]
        ps_a = [pb(f"ps_a{k}") for k in range(2)]

        with nc.Block() as block:
            @block.gpsimd
            def _(pool):
                def unit(i, g):
                    pool.wait_ge(idx_ready, i * 4 + (g + 1))
                    wait_again(pool, z_ready, i * 4 + (g - 3))
                    wait_again(pool, stored[g], i * 16)
                    pool.sem_inc(pool_step, 1)
                    for j in range(U):
                        pool.indirect_dma_start(rows[g][:, j, :, :].rearrange("p h c -> p (h c)"), None, X.hrow[:, :],
                                                bass.IndirectOffsetOnAxis(ap=idx[g][:, j:j + 1], axis=0))\
                            .then_inc(T.moves.sems[g][j], 16)
                turns(pool, unit)

            @block.sync
            def _(sp):
                def unit(i, g):
                    sp.wait_ge(z_ready, i * 4 + (g + 1))
                    sp.dma_start(X.gathered[bass.ds(i * 4 * P + g * P, P), :],
                                 rows[g][:, :, :, :].rearrange("p u h c -> p (u h c)")).then_inc(stored[g], 16)
                turns(sp, unit)
                for g in range(4):
                    sp.wait_ge(stored[g], 16 * ITERS)

            @block.vector
            def _(dve):
                def take_index(i, g):
                    T.moves.wait_last(dve, i, g)
                    nc.vector.tensor_copy(idx[g][:, :], T.m_dst[:, bass.ds(i * 4 * U + g * U, U), 0]).then_inc(idx_ready, 1)

                def make_hot(i, g):
                    wait_again(dve, hot_turned, i * 4 + (g - 1))
                    nc.vector.tensor_tensor(hot[g % 2][:, :, :], repeat(T.iota1_f[:, :], U),
                                            spread(T.m_dst[:, bass.ds(i * 4 * U + g * U, U), 2], P),
                                            ALU.is_equal).then_inc(hot_ready, 1)
                for g in range(3):
                    take_index(0, g)
                make_hot(0, 0)

                def unit(i, g):
                    if then := near(i, g, 3):
                        take_index(*then)
                    if then := near(i, g, 1):
                        make_hot(*then)
                    T.moves.wait(dve, i, g)
                    dve.wait_ge(ar_read, i * 4 + (g + 1))
                    nc.vector.tensor_tensor(T.z[:, bass.ds(i * 4 * U + g * U, U), :], rows[g][:, :, :, HID],
                                            ps_a[g % 2][:, 0:U * HEADS].rearrange("p (u h) -> p u h", h=HEADS), ALU.add)\
                        .then_inc(z_ready, 1)
                turns(dve, unit)

            @block.scalar
            def _(act):
                def unit(i, g):
                    act.wait_ge(hot_turned, i * 4 + (g + 1))
                    wait_again(act, ar_read, i * 4 + (g - 1))
                    nc.scalar.copy(hot_t[g % 2][:, :], ps_t[g % 2][:, :]).then_inc(hot_copied, 1)
                turns(act, unit)

            @block.tensor
            def _(pe):
                def turn_hot(i, g):
                    pe.wait_ge(hot_ready, i * 4 + (g + 1))
                    wait_again(pe, hot_copied, i * 4 + (g - 1))
                    for j in range(U):
                        ins = nc.tensor.transpose(ps_t[g % 2][:, j * P:(j + 1) * P], hot[g % 2][:, j, :], T.ident[:, :])
                    ins.then_inc(hot_turned, 1)
                turn_hot(0, 0)

                def unit(i, g):
                    k = g % 2
                    if then := near(i, g, 1):
                        turn_hot(*then)
                    tiles = tiles_of(nc, mybir.EngineType.PE, T.tile_d, i, g)
                    pe.wait_ge(hot_copied, i * 4 + (g + 1))
                    wait_again(pe, z_ready, i * 4 + (g - 1))
                    for j in range(U):
                        ins = nc.tensor.matmul(ps_a[k][:, j * HEADS:(j + 1) * HEADS], hot_t[k][:, j * P:(j + 1) * P],
                                               T.ar[:, bass.ds(tiles[j] * HEADS, HEADS)], start=True, stop=True)
                    ins.then_inc(ar_read, 1)
                turns(pe, unit)
        T.moves.close(lambda g, j: ITERS)
        S.clear()


def build_gat_softmax(nc, T, X, name):
    with ExitStack() as ctx:
        S = Sems(nc, ctx, name)
        (dve_at, act_at, turned, taken, turned_back, taken_back, row_at, flags_in, stored, loaded, ex_stored, ex_in) = (
            S(n) for n in ("dve_at", "act_at", "turned", "taken", "turned_back", "taken_back", "row_at", "flags_in",
                           "stored", "loaded", "ex_stored", "ex_in"))

        def sb(n, shape, dt=F32):
            return ctx.enter_context(nc.sbuf_tensor(f"{name}_{n}", shape, dt))
        one = T.acc[:, 0:SLEN]
        two = T.acc[:, SLEN:2 * SLEN]
        flags = [sb(f"flags{k}", [P, SLEN], BF16) for k in range(2)]
        edge = [sb(f"edge{k}", [P, 2]) for k in range(2)]
        rowed = [sb(f"rowed{k}", [1, 2 * P]) for k in range(2)]
        handed = [sb(f"handed{k}", [1, 2 * P]) for k in range(2)]
        carry = [sb(f"carry{k}", [P, 1]) for k in range(2)]
        ps = [ctx.enter_context(nc.psum_tensor(f"{name}_ps{k}", [P, 512], F32)) for k in range(4)]
        ps_r = ctx.enter_context(nc.psum_tensor(f"{name}_ps_r", [P, 512], F32))
        ps_c = ctx.enter_context(nc.psum_tensor(f"{name}_ps_c", [P, 512], F32))
        groups = [(h, a, min(4, CBLK - a)) for h in range(HEADS) for a in range(0, CBLK, 4)]
        by_chunk = one[:, :].rearrange("p (h b s) -> p h b s", h=HEADS, b=CBLK)

        def chunked(x, h):
            return x[h].rearrange("(b c p) -> c b p", b=CBLK, c=P)

        def strips(x):
            return x.rearrange("h (b s) -> (h b) s", s=SLEN)

        with nc.Block() as block:
            @block.sync
            def _(sp):
                for k, x in enumerate((X.reset_dst, X.ends_dst)):
                    for h in range(HEADS):
                        sp.dma_start(flags[k][h * STRIPS:(h + 1) * STRIPS, :], x.rearrange("(b s) -> b s", s=SLEN))\
                            .then_inc(flags_in, 16)
                for h in range(HEADS):
                    sp.wait_ge(taken, len(groups) // HEADS * (h + 1))
                    sp.dma_start(chunked(X.logits, h), by_chunk[:, h]).then_inc(stored, 16)
                sp.wait_ge(stored, 16 * HEADS)
                sp.dma_start(one[:, :], strips(X.logits)).then_inc(loaded, 16)
                sp.wait_ge(act_at, 1)
                sp.dma_start(strips(X.exps), two[:, :]).then_inc(ex_stored, 16)
                sp.wait_ge(ex_stored, 16)
                for h in range(HEADS):
                    sp.dma_start(by_chunk[:, h], chunked(X.exps, h)).then_inc(ex_in, 16)

            @block.vector
            def _(dve):
                link = chain(dve, dve_at)
                z = T.z[:, :, :]
                link(nc.vector.scalar_tensor_tensor(out=z, in0=z, scalar=0.2, in1=z, op0=ALU.mult, op1=ALU.max))
                link(nc.vector.tensor_tensor(z, z, spread(T.m_dst[:, :, 1], HEADS), ALU.mult))
                for n, (h, a, m) in enumerate(groups):
                    dve.wait_ge(turned, n + 1)
                    nc.vector.tensor_copy(by_chunk[:, h, a:a + m, :], ps[n % 4][:, 0:m * P].rearrange("c (b p) -> c b p", p=P))\
                        .then_inc(taken, 1)
                dve.wait_ge(flags_in, 16 * 2 * HEADS)
                dve.wait_ge(loaded, 16)
                for k in range(2):
                    way = slice(None, None, -1) if k else slice(None)
                    mine, more = (0, SLEN - 1)[1 - k], two if k else one
                    link(nc.vector.tensor_tensor_scan(two[:, way], flags[k][:, way], more[:, way], LOW, ALU.add, ALU.max))
                    link(nc.vector.tensor_scalar(edge[k][:, 0:1], two[:, mine:mine + 1], 0.0, None, ALU.add))
                    link(nc.vector.tensor_reduce(edge[k][:, 1:2], flags[k][:, :], AX.X, ALU.min))
                    link(nc.vector.tensor_scalar(edge[k][:, 1:2], edge[k][:, 1:2], 0.0, None, ALU.is_lt))
                    dve.wait_ge(row_at, 2 * k + 1)
                    link(nc.vector.tensor_copy(rowed[k][:, 0:P], ps_r[0:1, 0:P]))
                    link(nc.vector.tensor_scalar(rowed[k][:, P:2 * P], ps_r[0:1, P:2 * P], NEG, None, ALU.mult))
                    first = STRIPS - 1 if k else 0
                    link(nc.vector.memset(rowed[k][:, P:2 * P].rearrange("o (h b) -> o h b", h=HEADS)[:, :, first:first + 1], NEG))
                    link(nc.vector.tensor_tensor_scan(handed[k][:, 0:P][:, way], rowed[k][:, P:2 * P][:, way],
                                                      rowed[k][:, 0:P][:, way], LOW, ALU.add, ALU.max))
                    to, frm = (slice(P, 2 * P - 1), slice(1, P)) if k else (slice(P + 1, 2 * P), slice(0, P - 1))
                    link(nc.vector.tensor_copy(handed[k][:, to], handed[k][:, frm]))
                    link(nc.vector.memset(handed[k][:, P:2 * P].rearrange("o (h b) -> o h b", h=HEADS)[:, :, first:first + 1], LOW))
                    dve.wait_ge(row_at, 2 * k + 2)
                    link(nc.vector.tensor_copy(carry[k][:, :], ps_c[:, k:k + 1]))
                    link(nc.vector.tensor_tensor_scan(two[:, way], flags[k][:, way], two[:, way], carry[k][:, :],
                                                      ALU.add, ALU.max))
                link(nc.vector.tensor_tensor(two[:, :], one[:, :], two[:, :], ALU.subtract))
                for n, (h, a, m) in enumerate(groups):
                    dve.wait_ge(turned_back, n + 1)
                    nc.vector.tensor_copy(T.z[:, a * P:(a + m) * P, h], ps[n % 4][:, 0:m * P]).then_inc(taken_back, 1)

            @block.scalar
            def _(act):
                act.wait_ge(dve_at, 27)
                nc.scalar.activation(two[:, :], two[:, :], ACT.Exp).then_inc(act_at, 1)

            @block.tensor
            def _(pe):
                pe.wait_ge(dve_at, 2)
                for n, (h, a, m) in enumerate(groups):
                    if n >= 4:
                        pe.wait_ge(taken, n - 3)
                    for j in range(m):
                        ins = nc.tensor.transpose(ps[n % 4][:, j * P:(j + 1) * P], T.z[:, (a + j) * P:(a + j + 1) * P, h],
                                                  T.ident[:, :])
                    ins.then_inc(turned, 1)
                for k in range(2):
                    pe.wait_ge(dve_at, 2 + 12 * k + 4)
                    for j in range(2):
                        ins = nc.tensor.matmul(ps_r[0:1, j * P:(j + 1) * P], edge[k][:, j:j + 1], T.ident[:, :],
                                               start=True, stop=True)
                    ins.then_inc(row_at, 1)
                    pe.wait_ge(dve_at, 2 + 12 * k + 10)
                    nc.tensor.matmul(ps_c[:, k:k + 1], handed[k][:, P:2 * P], T.ones[0:1, 0:1], start=True, stop=True)\
                        .then_inc(row_at, 1)
                for n, (h, a, m) in enumerate(groups):
                    pe.wait_ge(ex_in, 16 * HEADS)
                    if n < 4:
                        pe.wait_ge(taken, len(groups) - 3 + n)
                    else:
                        pe.wait_ge(taken_back, n - 3)
                    for j in range(m):
                        ins = nc.tensor.transpose(ps[n % 4][:, j * P:(j + 1) * P], by_chunk[:, h, a + j, :], T.ident[:, :])
                    ins.then_inc(turned_back, 1)
        S.clear()


def build_gat_sums(nc, T, X, name):
    with ExitStack() as ctx:
        S = Sems(nc, ctx, name)
        hot_ready, ex_ready, hx_ready, summed, added, cleared = (S(n) for n in (
            "hot_ready", "ex_ready", "hx_ready", "summed", "added", "cleared"))
        rows_in = [S(f"rows_in{k}") for k in range(4)]

        def sb(n, shape, dt=F32):
            return ctx.enter_context(nc.sbuf_tensor(f"{name}_{n}", shape, dt))
        rows = [sb(f"rows{k}", [P, U * HEADS, HID + 1]) for k in range(4)]
        hot = [sb(f"hot{k}", [P, U, P]) for k in range(2)]
        hx = [sb(f"hx{k}", [P, U * HEADS, HID + 1]) for k in range(2)]
        ps = [[ctx.enter_context(nc.psum_tensor(f"{name}_ps{k}{h}", [P, 512], F32)) for h in range(2)] for k in range(2)]

        def exps(i, g):
            return T.z[:, bass.ds(i * 4 * U + g * U, U), :]

        with nc.Block() as block:
            @block.sync
            def _(sp):
                def unit(i, g):
                    wait_again(sp, hx_ready, i * 4 + (g - 3))
                    sp.dma_start(rows[g][:, :, :].rearrange("p u c -> p (u c)"),
                                 X.gathered[bass.ds(i * 4 * P + g * P, P), :]).then_inc(rows_in[g], 16)
                turns(sp, unit)

            @block.vector
            def _(dve):
                nc.vector.memset(T.acc[:, :], 0.0).then_inc(cleared, 1)

                def add(i, g):
                    tiles = tiles_of(nc, mybir.EngineType.DVE, T.tile_d, i, g)
                    dve.wait_ge(summed, i * 4 + (g + 1))
                    for j in range(U):
                        wait_again(dve, added, i * 16 + (U * g + j))
                        acc = T.acc[:, bass.ds(tiles[j] * ROW, ROW)]
                        nc.vector.tensor_tensor(acc, acc, ps[g % 2][j // 2][:, (j % 2) * ROW:(j % 2 + 1) * ROW], ALU.add)\
                            .then_inc(added, 1)
                dve.wait_ge(cleared, 1)

                def unit(i, g):
                    n, k = i * 4 + g, g % 2
                    wait_again(dve, summed, n - 1)
                    nc.vector.tensor_tensor(hot[k][:, :, :], repeat(T.iota1_f[:, :], U),
                                            spread(T.m_dst[:, bass.ds(i * 4 * U + g * U, U), 2], P),
                                            ALU.is_equal).then_inc(hot_ready, 1)
                    dve.wait_ge(rows_in[g], i * 16 + 16)
                    nc.vector.tensor_tensor(hx[k][:, :, 0:HID], rows[g][:, :, 0:HID],
                                            spread(exps(i, g).rearrange("p u h -> p (u h)"), HID), ALU.mult)\
                        .then_inc(hx_ready, 1)
                    if past := near(i, g, -1):
                        add(*past)
                turns(dve, unit)
                add(ITERS - 1, 3)

            @block.scalar
            def _(act):
                def unit(i, g):
                    wait_again(act, summed, i * 4 + (g - 1))
                    nc.scalar.copy(hx[g % 2][:, :, HID], exps(i, g).rearrange("p u h -> p (u h)")).then_inc(ex_ready, 1)
                turns(act, unit)

            @block.tensor
            def _(pe):
                def unit(i, g):
                    n, k = i * 4 + g, g % 2
                    pe.wait_ge(hot_ready, n + 1)
                    pe.wait_ge(ex_ready, n + 1)
                    pe.wait_ge(hx_ready, n + 1)
                    wait_again(pe, added, i * 16 + (4 * (g - 1)))
                    for j in range(U):
                        ins = nc.tensor.matmul(ps[k][j // 2][:, (j % 2) * ROW:(j % 2 + 1) * ROW], hot[k][:, j, :],
                                               hx[k][:, j * HEADS:(j + 1) * HEADS, :].rearrange("p h c -> p (h c)"),
                                               start=True, stop=True)
                    ins.then_inc(summed, 1)
                turns(pe, unit)
        S.clear()


def build_mlp_edges(nc, T, X):
    with ExitStack() as ctx:
        S = Sems(nc, ctx, "ml")
        (idx_ready, hot_ready, hot_turned, hot_copied, own_read, part_ready, in_ready, turned, act_in, hid_ready,
         act_hid, theta_ready, msg_ready, summed, added, pool_step, cleared) = (S(n) for n in (
             "idx_ready", "hot_ready", "hot_turned", "hot_copied", "own_read", "part_ready", "in_ready", "turned",
             "act_in", "hid_ready", "act_hid", "theta_ready", "msg_ready", "summed", "added", "pool_step", "cleared"))
        attr_in = [S(f"attr_in{k}") for k in range(4)]

        def sb(n, shape, dt=F32):
            return ctx.enter_context(nc.sbuf_tensor("ml_" + n, shape, dt))

        def pb(n):
            return ctx.enter_context(nc.psum_tensor("ml_" + n, [P, 512], F32))
        idx = [sb(f"idx{k}", [P, U], U32) for k in range(4)]
        rows = [sb(f"rows{k}", [P, U, D]) for k in range(4)]
        attr = [sb(f"attr{k}", [P, U, D]) for k in range(4)]
        hot = [sb(f"hot{k}", [P, U, P]) for k in range(4)]
        hot_t = sb("hot_t", [P, U * P])
        sin = sb("sin", [P, U * P])
        hid = [sb(f"hid{k}", [P, U * P]) for k in range(2)]
        msg = sb("msg", [P, U, D])
        ps_t, ps_o, ps_x, ps_f, ps_s = pb("ps_t"), pb("ps_o"), pb("ps_x"), pb("ps_f"), pb("ps_s")
        ps_h = [pb(f"ps_h{k}") for k in range(2)]
        PE_T, DVE_T = mybir.EngineType.PE, mybir.EngineType.DVE

        with nc.Block() as block:
            @block.gpsimd
            def _(pool):
                def unit(i, g):
                    pool.wait_ge(idx_ready, i * 4 + (g + 1))
                    wait_again(pool, msg_ready, i * 4 + (g - 3))
                    pool.sem_inc(pool_step, 1)
                    for j in range(U):
                        pool.indirect_dma_start(rows[g][:, j, :], None, X.h2row[:, :],
                                                bass.IndirectOffsetOnAxis(ap=idx[g][:, j:j + 1], axis=0))\
                            .then_inc(T.moves.sems[g][j], 16)
                turns(pool, unit)

            @block.sync
            def _(sp):
                def unit(i, g):
                    wait_again(sp, turned, i * 4 + (g - 3))
                    a = X.rec_src[bass.ds(i * 4 * U * P + g * U * P, U * P), :]
                    sp.dma_start(attr[g][:, :, :], a.rearrange("(j e) f -> e j f", e=P)[:, :, 0:D]).then_inc(attr_in[g], 16)
                turns(sp, unit)

            @block.vector
            def _(dve):
                nc.vector.memset(T.acc[:, :], 0.0).then_inc(cleared, 1)

                def take_index(i, g):
                    T.moves.wait_last(dve, i, g)
                    nc.vector.tensor_copy(idx[g][:, :], T.m_src[:, bass.ds(i * 4 * U + g * U, U), 0]).then_inc(idx_ready, 1)

                def make_hot(i, g):
                    wait_again(dve, summed, i * 4 + (g - 3))
                    nc.vector.tensor_tensor(hot[g][:, :, :], repeat(T.iota1_f[:, :], U),
                                            spread(T.m_src[:, bass.ds(i * 4 * U + g * U, U), 2], P),
                                            ALU.is_equal).then_inc(hot_ready, 1)

                def sum_input(i, g):
                    T.moves.wait(dve, i, g)
                    dve.wait_ge(attr_in[g], i * 16 + 16)
                    nc.vector.tensor_tensor(attr[g][:, :, :], attr[g][:, :, :], rows[g][:, :, :], ALU.add)\
                        .then_inc(part_ready, 1)
                    dve.wait_ge(own_read, i * 4 + (g + 1))
                    dve.wait_ge(part_ready, i * 4 + (g + 1))
                    nc.vector.tensor_tensor(attr[g][:, :, :], attr[g][:, :, :],
                                            ps_o[:, :].rearrange("p (j f) -> p j f", f=D), ALU.add).then_inc(in_ready, 1)

                def message(i, g):
                    dve.wait_ge(theta_ready, i * 4 + (g + 1))
                    wait_again(dve, summed, i * 4 + g)
                    nc.vector.tensor_tensor(msg[:, :, :], rows[g][:, :, :],
                                            ps_f[:, :].rearrange("p (j f) -> p j f", f=D), ALU.mult).then_inc(msg_ready, 1)

                def add(i, g):
                    tiles = tiles_of(nc, DVE_T, T.tile_s, i, g)
                    dve.wait_ge(summed, i * 4 + (g + 1))
                    for j in range(U):
                        wait_again(dve, added, i * 16 + (U * g + j))
                        to = T.acc[:, bass.ds(tiles[j] * ROW, D)]
                        nc.vector.tensor_tensor(to, to, ps_s[:, j * D:(j + 1) * D], ALU.add).then_inc(added, 1)

                for g in range(3):
                    take_index(0, g)
                dve.wait_ge(cleared, 1)
                make_hot(0, 0)
                sum_input(0, 0)

                def unit(i, g):
                    if then := near(i, g, 3):
                        take_index(*then)
                    then = near(i, g, 1)
                    if then:
                        make_hot(*then)
                    if past := near(i, g, -1):
                        add(*past)
                    if then:
                        sum_input(*then)
                    message(i, g)
                turns(dve, unit)
                add(ITERS - 1, 3)

            @block.scalar
            def _(act):
                def copy_hot(i, g):
                    act.wait_ge(hot_turned, i * 4 + (g + 1))
                    wait_again(act, own_read, i * 4 + g)
                    nc.scalar.copy(hot_t[:, :], ps_t[:, :]).then_inc(hot_copied, 1)
                copy_hot(0, 0)

                def unit(i, g):
                    n = i * 4 + g
                    act.wait_ge(turned, n + 1)
                    wait_again(act, hid_ready, 2 * n)
                    nc.scalar.activation(sin[:, :], ps_x[:, :], ACT.Silu).then_inc(act_in, 1)
                    if then := near(i, g, 1):
                        copy_hot(*then)
                    for h in range(2):
                        act.wait_ge(hid_ready, 2 * n + (h + 1))
                        wait_again(act, theta_ready, n)
                        nc.scalar.activation(hid[h][:, :], ps_h[h][:, :], ACT.Silu, bias=T.b1c[:, h:h + 1])\
                            .then_inc(act_hid, 1)
                turns(act, unit)

            @block.tensor
            def _(pe):
                def turn_hot(i, g):
                    pe.wait_ge(hot_ready, i * 4 + (g + 1))
                    wait_again(pe, hot_copied, i * 4 + g)
                    for j in range(U):
                        ins = nc.tensor.transpose(ps_t[:, j * P:(j + 1) * P], hot[g][:, j, :], T.ident[:, :])
                    ins.then_inc(hot_turned, 1)

                def read_own(i, g):
                    tiles = tiles_of(nc, PE_T, T.tile_s, i, g)
                    pe.wait_ge(hot_copied, i * 4 + (g + 1))
                    wait_again(pe, in_ready, i * 4 + g)
                    for j in range(U):
                        ins = nc.tensor.matmul(ps_o[:, j * D:(j + 1) * D], hot_t[:, j * P:(j + 1) * P],
                                               T.nodes[:, bass.ds(tiles[j] * D, D)], start=True, stop=True)
                    ins.then_inc(own_read, 1)

                def turn_input(i, g):
                    pe.wait_ge(in_ready, i * 4 + (g + 1))
                    wait_again(pe, act_in, i * 4 + g)
                    for j in range(U):
                        ins = nc.tensor.transpose(ps_x[:, j * P:(j + 1) * P], attr[g][:, j, :], T.ident[:, :])
                    ins.then_inc(turned, 1)

                def hidden(i, g):
                    pe.wait_ge(act_in, i * 4 + (g + 1))
                    for h in range(2):
                        wait_again(pe, act_hid, 2 * (i * 4 + g) + (h - 1))
                        nc.tensor.matmul(ps_h[h][:, :], T.w1[:, h * P:(h + 1) * P], sin[:, :], start=True, stop=True)\
                            .then_inc(hid_ready, 1)

                def theta(i, g):
                    pe.wait_ge(act_hid, 2 * (i * 4 + g) + 2)
                    wait_again(pe, msg_ready, i * 4 + g)
                    for j in range(U):
                        part = ps_f[:, j * D:(j + 1) * D]
                        nc.tensor.matmul(part, T.ones[0:1, :], T.b2r[0:1, :], start=True, stop=False)
                        for h in range(2):
                            ins = nc.tensor.matmul(part, hid[h][:, j * P:(j + 1) * P], T.w2[:, h, :], start=False, stop=(h == 1))
                    ins.then_inc(theta_ready, 1)

                def sum_up(i, g):
                    pe.wait_ge(msg_ready, i * 4 + (g + 1))
                    wait_again(pe, added, i * 16 + U * g)
                    for j in range(U):
                        ins = nc.tensor.matmul(ps_s[:, j * D:(j + 1) * D], hot[g][:, j, :], msg[:, j, :], start=True, stop=True)
                    ins.then_inc(summed, 1)
                turn_hot(0, 0)
                read_own(0, 0)

                def unit(i, g):
                    turn_input(i, g)
                    then = near(i, g, 1)
                    if then:
                        turn_hot(*then)
                    if past := near(i, g, -1):
                        sum_up(*past)
                    hidden(i, g)
                    if then:
                        read_own(*then)
                    theta(i, g)
                turns(pe, unit)
                sum_up(ITERS - 1, 3)
        T.moves.close(lambda g, j: ITERS)
        S.clear()


def build_gcn_edges(nc, T, X):
    with ExitStack() as ctx:
        S = Sems(nc, ctx, "gc")
        idx_ready, hot_ready, summed, added, pool_step, cleared = (
            S("idx_ready"), S("hot_ready"), S("summed"), S("added"), S("pool_step"), S("cleared"))
        idx = [ctx.enter_context(nc.sbuf_tensor(f"gc_idx{k}", [P, U], U32)) for k in range(4)]
        rows = [ctx.enter_context(nc.sbuf_tensor(f"gc_rows{k}", [P, U, D], F32)) for k in range(4)]
        hot = [ctx.enter_context(nc.sbuf_tensor(f"gc_hot{k}", [P, U, P], F32)) for k in range(2)]
        ps = [ctx.enter_context(nc.psum_tensor(f"gc_ps{k}", [P, 512], F32)) for k in range(2)]

        with nc.Block() as block:
            @block.gpsimd
            def _(pool):
                def unit(i, g):
                    pool.wait_ge(idx_ready, i * 4 + (g + 1))
                    wait_again(pool, summed, i * 4 + (g - 3))
                    pool.sem_inc(pool_step, 1)
                    for j in range(U):
                        pool.indirect_dma_start(rows[g][:, j, :], None, X.h3row[:, :],
                                                bass.IndirectOffsetOnAxis(ap=idx[g][:, j:j + 1], axis=0))\
                            .then_inc(T.moves.sems[g][j], 16)
                turns(pool, unit)

            @block.vector
            def _(dve):
                nc.vector.memset(T.acc[:, :], 0.0).then_inc(cleared, 1)

                def take_index(i, g):
                    T.moves.wait_last(dve, i, g)
                    nc.vector.tensor_copy(idx[g][:, :], T.m_src[:, bass.ds(i * 4 * U + g * U, U), 0]).then_inc(idx_ready, 1)

                def add(i, g):
                    tiles = tiles_of(nc, mybir.EngineType.DVE, T.tile_s, i, g)
                    dve.wait_ge(summed, i * 4 + (g + 1))
                    for j in range(U):
                        wait_again(dve, added, i * 16 + (U * g + j))
                        to = T.acc[:, bass.ds(tiles[j] * ROW, D)]
                        nc.vector.tensor_tensor(to, to, ps[g % 2][:, j * D:(j + 1) * D], ALU.add).then_inc(added, 1)

                for g in range(3):
                    take_index(0, g)
                dve.wait_ge(cleared, 1)

                def unit(i, g):
                    if then := near(i, g, 3):
                        take_index(*then)
                    wait_again(dve, summed, i * 4 + (g - 1))
                    for j in range(U):
                        c = i * 4 * U + (g * U + j)
                        ins = nc.vector.tensor_scalar(hot[g % 2][:, j, :], T.iota1_f[:, :], T.m_src[:, bass.ds(c, 1), 2],
                                                      T.m_src[:, bass.ds(c, 1), 1], ALU.is_equal, ALU.mult)
                    ins.then_inc(hot_ready, 1)
                    if past := near(i, g, -1):
                        add(*past)
                turns(dve, unit)
                add(ITERS - 1, 3)

            @block.tensor
            def _(pe):
                def unit(i, g):
                    pe.wait_ge(hot_ready, i * 4 + (g + 1))
                    wait_again(pe, added, i * 16 + U * (g - 1))
                    for j in range(U):
                        T.moves.wait(pe, i, g, [j])
                        ins = nc.tensor.matmul(ps[g % 2][:, j * D:(j + 1) * D], hot[g % 2][:, j, :], rows[g][:, j, :],
                                               start=True, stop=True)
                    ins.then_inc(summed, 1)
                turns(pe, unit)
        T.moves.close(lambda g, j: ITERS)
        S.clear()


NTURN = NT // 2
WROW = HEADS * (HID + 1)
WCAT = WROW + HEADS


def build_weights(nc, T, X):
    with ExitStack() as ctx:
        S = Sems(nc, ctx, "wt")
        loaded, turned, dve_at = S("loaded"), S("turned"), S("dve_at")
        w0 = ctx.enter_context(nc.sbuf_tensor("wt_w0", [P, 2 * D], F32))
        w = [ctx.enter_context(nc.sbuf_tensor(f"wt_gat{k}", [P, D], F32)) for k in range(2)]
        att = [ctx.enter_context(nc.sbuf_tensor(f"wt_att{k}", [P, D], F32)) for k in range(4)]
        prod = ctx.enter_context(nc.sbuf_tensor("wt_prod", [P, D], F32))
        dots = ctx.enter_context(nc.sbuf_tensor("wt_dots", [P, HEADS], F32))
        ps = ctx.enter_context(nc.psum_tensor("wt_ps", [P, 512], F32))
        loads = [(w0[:, :], X.L0_gnn_W), (w[0][:, :], X.L1_gnn_W1), (w[1][:, :], X.L1_gnn_W2),
                 (T.w1[:, :], X.L2_gnn_W1), (T.w2[:, :, :], X.L2_gnn_W2.rearrange("(h k) n -> k h n", h=2)),
                 (T.wt[:, :], X.L2_gnn_Wt), (T.w3[:, :], X.L3_gnn_W), (T.wres[:, :], X.L3_gnn_Wres),
                 (T.b1c[:, :], X.L2_gnn_b1.rearrange("(h k) -> k h", h=2))]
        loads += [(t[0:1, :], a.unsqueeze(0)) for t, a in (
            (T.b0r, X.L0_gnn_b), (T.b2r, X.L2_gnn_b2), (T.btr, X.L2_gnn_bt), (T.b3r, X.L3_gnn_b), (T.bresr, X.L3_gnn_bres))]
        loads += [(t[:, :], a.partition_broadcast(P)) for t, a in (
            (T.bg1, X.L1_gnn_b1), (T.bg2, X.L1_gnn_b2), (T.gamma, X.L2_gnn_ln_gamma), (T.beta, X.L2_gnn_ln_beta))]
        loads += [(t[:, :], a.rearrange("h c -> (h c)").partition_broadcast(P)) for t, a in zip(
            att, (X.L1_gnn_att_l1, X.L1_gnn_att_r1, X.L1_gnn_att_l2, X.L1_gnn_att_r2))]
        with nc.Block() as block:
            @block.sync
            def _(sp):
                with nc.allow_non_contiguous_dma(reason="256 biases, once"):
                    for to, frm in loads:
                        sp.dma_start(to, frm).then_inc(loaded, 16)

            @block.vector
            def _(dve):
                dve.wait_ge(loaded, 16 * len(loads))
                link = chain(dve, dve_at)
                link(nc.vector.memset(T.acc[:, 0:1], 0.0))
                for k, cat in enumerate((T.cat1, T.cat2)):
                    wide = cat[:, 0:WROW].rearrange("p (h c) -> p h c", h=HEADS)
                    link(nc.vector.tensor_copy(wide[:, :, 0:HID], w[k][:, :].rearrange("p (h c) -> p h c", h=HEADS)))
                    for side in range(2):
                        link(nc.vector.tensor_tensor(prod[:, :], w[k][:, :], att[2 * k + side][:, :], ALU.mult))
                        link(nc.vector.tensor_reduce(dots[:, :], prod[:, :].rearrange("p (h c) -> p h c", h=HEADS),
                                                     AX.X, ALU.add))
                        to = wide[:, :, HID] if side == 0 else cat[:, WROW:WCAT]
                        link(nc.vector.tensor_copy(to, dots[:, :]))
                dve.wait_ge(turned, 1)
                link(nc.vector.tensor_copy(T.w0t[:, :], ps[:, 0:2 * D]))

            @block.tensor
            def _(pe):
                pe.wait_ge(loaded, 16 * len(loads))
                for h in range(2):
                    ins = nc.tensor.transpose(ps[:, h * D:(h + 1) * D], w0[:, h * D:(h + 1) * D], T.ident[:, :])
                ins.then_inc(turned, 1)
        S.clear()


def build_nodes(nc, T, X, kind):
    resid = {"sage": X.xpad, "gat_mid": None, "gat_end": X.x1, "mlp": X.x2, "gcn": X.x3}[kind]
    weight, bias = {"sage": (T.w0t, T.b0r), "gat_mid": (T.cat2, None), "gat_end": (None, None),
                    "mlp": (T.wt, T.btr), "gcn": (T.wres, T.bresr)}[kind]
    gat = kind.startswith("gat")
    width = WCAT if kind == "gat_mid" else D
    with ExitStack() as ctx:
        S = Sems(nc, ctx, "n" + kind)
        taken, scaled, turned, copied, multiplied, plus, noted, told, silued, inv, joined = (S(n) for n in (
            "taken", "scaled", "turned", "copied", "multiplied", "plus", "noted", "told", "silued", "inv", "joined"))
        resid_in = [S(f"resid_in{k}") for k in range(2)]
        stored = [S(f"stored{k}") for k in range(2)]

        def sb(n, shape, dt=F32):
            return ctx.enter_context(nc.sbuf_tensor(f"n{kind}_{n}", shape, dt))
        xr = [sb(f"xr{k}", [P, D]) for k in range(2)]
        pre = [sb(f"pre{k}", [P, D]) for k in range(2)]
        v = [sb(f"v{k}", [P, D]) for k in range(2)]
        vt = [sb(f"vt{k}", [P, 2 * P]) for k in range(2)]
        mid = [sb(f"mid{k}", [P, D]) for k in range(2)]
        hb = [sb(f"hb{k}", [P, WROW]) for k in range(2)]
        rs = sb("rs", [P, NT * HEADS])
        pa = [ctx.enter_context(nc.psum_tensor(f"n{kind}_pa{k}", [P, 512], F32)) for k in range(2)]
        py = [ctx.enter_context(nc.psum_tensor(f"n{kind}_py{k}", [P, 512], F32)) for k in range(2)]

        def loop(eng, step):
            turns(eng, step, depth=2, count=NTURN)

        with nc.Block() as block:
            @block.sync
            def _(sp):
                if resid is not None:
                    def load(i, k):
                        wait_again(sp, noted if width == D else taken, i * 2 + (k - 1))
                        sp.dma_start(xr[k][:, :], resid[bass.ds(i * 2 * P + k * P, P), :]).then_inc(resid_in[k], 16)
                    loop(sp, load)
                if kind == "gat_mid":
                    def store(i, k):
                        sp.wait_ge(plus, i * 2 + (k + 1))
                        sp.dma_start(X.hrow[bass.ds(i * 2 * P + k * P, P), :], hb[k][:, :]).then_inc(stored[k], 16)
                    loop(sp, store)
                    for k in range(2):
                        sp.wait_ge(stored[k], 16 * NTURN)

            @block.vector
            def _(dve):
                if gat:
                    sums = T.acc[:, 0:NT * ROW].rearrange("p (t c) -> p t c", c=HID + 1)[:, :, HID]
                    nc.vector.tensor_scalar(rs[:, :], sums, 1e-16, None, ALU.add).then_inc(inv, 1)
                    dve.wait_ge(inv, 1)
                    nc.vector.reciprocal(rs[:, :], rs[:, :]).then_inc(inv, 1)
                    dve.wait_ge(inv, 2)

                def before(i, k):
                    n = i * 2 + k
                    acc = T.acc[:, bass.ds(i * 2 * ROW + k * ROW, ROW)]
                    if gat:
                        wait_again(dve, taken, n - 1)
                        nc.vector.tensor_tensor(pre[k][:, :].rearrange("p (h c) -> p h c", h=HEADS),
                                                acc.rearrange("p (h c) -> p h c", h=HEADS)[:, :, 0:HID],
                                                spread(rs[:, bass.ds(i * 2 * HEADS + k * HEADS, HEADS)], HID), ALU.mult)\
                            .then_inc(scaled, 1)
                        dve.wait_ge(scaled, n + 1)
                        wait_again(dve, turned if weight is not None else joined, n - 1)
                        nc.vector.tensor_tensor(v[k][:, :], pre[k][:, :], (T.bg1 if kind == "gat_mid" else T.bg2)[:, :],
                                                ALU.add).then_inc(taken, 1)
                    elif kind == "sage":
                        wait_again(dve, turned, n - 1)
                        nc.vector.tensor_copy(v[k][:, :], acc[:, 0:D]).then_inc(taken, 1)
                    elif kind == "mlp":
                        wait_again(dve, silued, n - 1)
                        nc.vector.tensor_tensor(pre[k][:, :], acc[:, 0:D], T.nodes[:, bass.ds(i * 2 * D + k * D, D)], ALU.add)\
                            .then_inc(taken, 1)
                    else:
                        wait_again(dve, turned, n - 1)
                        wait_again(dve, plus, n - 1)
                        nc.vector.tensor_scalar(v[k][:, :], acc[:, 0:D], 0.0, None, ALU.max).then_inc(taken, 1)

                def after(i, k):
                    n = i * 2 + k
                    if weight is not None:
                        dve.wait_ge(multiplied, n + 1)
                    if kind == "gat_mid":
                        wait_again(dve, stored[k], 16 * i)
                        nc.vector.tensor_copy(hb[k][:, :], py[k][:, 0:WROW]).then_inc(plus, 1)
                        nc.vector.tensor_copy(T.ar[:, bass.ds(i * 2 * HEADS + k * HEADS, HEADS)], py[k][:, WROW:WCAT])\
                            .then_inc(noted, 1)
                        return
                    dve.wait_ge(resid_in[k], i * 16 + 16)
                    to = T.nodes[:, bass.ds(i * 2 * D + k * D, D)]
                    if kind == "gcn":
                        wait_again(dve, joined, n - 1)
                        nc.vector.tensor_tensor(mid[k][:, :], v[k][:, :], py[k][:, 0:D], ALU.add).then_inc(plus, 1)
                        dve.wait_ge(plus, n + 1)
                        nc.vector.tensor_tensor(to, mid[k][:, :], xr[k][:, :], ALU.add).then_inc(joined, 1)
                    elif kind == "gat_end":
                        dve.wait_ge(taken, n + 1)
                        nc.vector.tensor_tensor(to, v[k][:, :], xr[k][:, :], ALU.add).then_inc(joined, 1)
                    else:
                        nc.vector.tensor_tensor(to, xr[k][:, :], py[k][:, 0:D], ALU.add).then_inc(joined, 1)
                    dve.wait_ge(joined, n + 1)
                    dve.sem_inc(told, 1)
                    nc.vector.bn_stats(T.stats[:, bass.ds(i * 12 + 6 * k, 6)], to).then_inc(noted, 1)

                before(0, 0)

                def step(i, k):
                    if then := near(i, k, 1, 2, NTURN):
                        before(*then)
                    after(i, k)
                loop(dve, step)

            @block.scalar
            def _(act):
                if weight is None:
                    return

                def step(i, k):
                    n = i * 2 + k
                    if kind == "mlp":
                        act.wait_ge(taken, n + 1)
                        wait_again(act, turned, n - 1)
                        nc.scalar.activation(v[k][:, :], pre[k][:, :], ACT.Silu).then_inc(silued, 1)
                    act.wait_ge(turned, n + 1)
                    wait_again(act, multiplied, n - 1)
                    w = 2 * P if kind == "sage" else P
                    nc.scalar.copy(vt[k][:, 0:w], pa[k][:, 0:w]).then_inc(copied, 1)
                loop(act, step)

            @block.tensor
            def _(pe):
                if weight is None:
                    return

                def step(i, k):
                    n = i * 2 + k
                    pe.wait_ge(silued if kind == "mlp" else taken, n + 1)
                    wait_again(pe, copied, n - 1)
                    if kind == "sage":
                        pe.wait_ge(resid_in[k], i * 16 + 16)
                        nc.tensor.transpose(pa[k][:, P:2 * P], xr[k][:, :], T.ident[:, :])
                    nc.tensor.transpose(pa[k][:, 0:P], v[k][:, :], T.ident[:, :]).then_inc(turned, 1)
                    pe.wait_ge(copied, n + 1)
                    wait_again(pe, noted, n - 1)
                    y = py[k][:, 0:width]
                    if bias is not None:
                        nc.tensor.matmul(y, T.ones[0:1, :], bias[0:1, :], start=True, stop=False)
                    if kind == "sage":
                        nc.tensor.matmul(y, vt[k][:, P:2 * P], weight[:, 0:D], start=False, stop=False)
                        ins = nc.tensor.matmul(y, vt[k][:, 0:P], weight[:, D:2 * D], start=False, stop=True)
                    else:
                        ins = nc.tensor.matmul(y, vt[k][:, 0:P], weight[:, 0:width], start=bias is None, stop=True)
                    ins.then_inc(multiplied, 1)
                loop(pe, step)
        S.clear()


def build_norm(nc, T, X, kind):
    store = {"x1": X.x1, "x2": X.x2, "h2": X.h2row, "x3": X.x3, "out": X.out}[kind]
    weight, bias, width, rows = {"x1": (T.cat1, None, WCAT, X.hrow), "x3": (T.w3, T.b3r, D, X.h3row)}\
        .get(kind, (None, None, 0, None))
    wrow = min(width, WROW)
    with ExitStack() as ctx:
        S = Sems(nc, ctx, "m" + kind)
        step_at, rooted, normed, turned, copied, multiplied, out_ready, noted, told, times, plus = (S(n) for n in (
            "step_at", "rooted", "normed", "turned", "copied", "multiplied", "out_ready", "noted", "told", "times", "plus"))
        stored = [S(f"stored{k}") for k in range(2)]
        sent = [S(f"sent{k}") for k in range(2)]

        def sb(n, shape, dt=F32):
            return ctx.enter_context(nc.sbuf_tensor(f"m{kind}_{n}", shape, dt))
        dev = sb("dev", [P, NT])
        std = sb("std", [P, NT])
        mean = sb("mean", [P, NT])
        apart = sb("apart", [P, NT])
        ob = [sb(f"ob{k}", [P, D]) for k in range(2)]
        raw = [sb(f"raw{k}", [P, D]) for k in range(2)]
        mul = [sb(f"mul{k}", [P, D]) for k in range(2)]
        vt = [sb(f"vt{k}", [P, P]) for k in range(2)]
        hb = [sb(f"hb{k}", [P, WROW]) for k in range(2)]
        pa = [ctx.enter_context(nc.psum_tensor(f"m{kind}_pa{k}", [P, 512], F32)) for k in range(2)]
        py = [ctx.enter_context(nc.psum_tensor(f"m{kind}_py{k}", [P, 512], F32)) for k in range(2)]
        LAST = N - (NT - 1) * P

        def loop(eng, step):
            turns(eng, step, depth=2, count=NTURN)

        with nc.Block() as block:
            @block.sync
            def _(sp):
                def save(i, k):
                    sp.wait_ge(normed, i * 2 + (k + 1))
                    if kind == "out" and isinstance(i, int) and i == NTURN - 1 and k == 1:
                        sp.dma_start(store[N - LAST:N, :], ob[k][0:LAST, :]).then_inc(stored[k], 16)
                    else:
                        sp.dma_start(store[bass.ds(i * 2 * P + k * P, P), :], ob[k][:, :]).then_inc(stored[k], 16)
                loop(sp, save)
                for k in range(2):
                    sp.wait_ge(stored[k], 16 * NTURN)

            @block.scalar
            def _(act):
                act.wait_ge(step_at, 7)
                nc.scalar.activation(std[:, :], dev[:, :], ACT.Sqrt).then_inc(rooted, 1)
                if weight is None:
                    return

                def step(i, k):
                    n = i * 2 + k
                    act.wait_ge(turned, n + 1)
                    wait_again(act, multiplied, n - 1)
                    nc.scalar.copy(vt[k][:, :], pa[k][:, 0:P]).then_inc(copied, 1)
                    if past := near(i, k, -1, 2, NTURN):
                        send(*past)

                def send(i, k):
                    act.wait_ge(out_ready, i * 2 + (k + 1))
                    act.dma_start(rows[bass.ds(i * 2 * P + k * P, P), :], hb[k][:, 0:wrow]).then_inc(sent[k], 16)
                loop(act, step)
                send(NTURN - 1, 1)
                for k in range(2):
                    act.wait_ge(sent[k], 16 * NTURN)

            @block.vector
            def _(dve):
                st = T.stats[:, :].rearrange("p (t s) -> p t s", s=6)
                link = chain(dve, step_at)
                link(nc.vector.tensor_tensor(mean[:, :], st[:, :, 1], st[:, :, 4], ALU.add))
                link(nc.vector.tensor_scalar(mean[:, :], mean[:, :], 0.5, None, ALU.mult))
                link(nc.vector.tensor_tensor(apart[:, :], st[:, :, 1], st[:, :, 4], ALU.subtract))
                link(nc.vector.tensor_tensor(apart[:, :], apart[:, :], apart[:, :], ALU.mult))
                link(nc.vector.tensor_scalar(apart[:, :], apart[:, :], 0.25, LN_EPS, ALU.mult, ALU.add))
                link(nc.vector.tensor_tensor(dev[:, :], st[:, :, 2], st[:, :, 5], ALU.add))
                link(nc.vector.scalar_tensor_tensor(out=dev[:, :], in0=dev[:, :], scalar=1.0 / D, in1=apart[:, :],
                                                    op0=ALU.mult, op1=ALU.add))
                dve.wait_ge(rooted, 1)
                link(nc.vector.reciprocal(dev[:, :], std[:, :]))

                def norm(i, k):
                    n = i * 2 + k
                    here = T.nodes[:, bass.ds(i * 2 * D + k * D, D)]
                    m, d = mean[:, bass.ds(i * 2 + k, 1)], dev[:, bass.ds(i * 2 + k, 1)]
                    wait_again(dve, stored[k], 16 * i)
                    if kind == "h2":
                        wait_again(dve, times, n - 1)
                        nc.vector.tensor_scalar(raw[k][:, :], here, m, d, ALU.subtract, ALU.mult).then_inc(out_ready, 1)
                        dve.wait_ge(out_ready, n + 1)
                        wait_again(dve, plus, n - 1)
                        nc.vector.tensor_tensor(mul[k][:, :], raw[k][:, :], T.gamma[:, :], ALU.mult).then_inc(times, 1)
                        dve.wait_ge(times, n + 1)
                        nc.vector.tensor_tensor(ob[k][:, :], mul[k][:, :], T.beta[:, :], ALU.add).then_inc(normed, 1)
                    else:
                        if weight is not None:
                            wait_again(dve, turned, n - 1)
                        if kind == "x2":
                            wait_again(dve, plus, n - 1)
                            wait_again(dve, noted, n - 1)
                        nc.vector.tensor_scalar(ob[k][:, :], here, m, d, ALU.subtract, ALU.mult).then_inc(normed, 1)
                    if kind in ("x2", "h2"):
                        dve.wait_ge(normed, n + 1)
                        nc.vector.tensor_scalar(here, ob[k][:, :], 0.0, None, ALU.add).then_inc(plus, 1)
                    if kind == "x2":
                        dve.sem_inc(told, 1)
                        nc.vector.bn_stats(T.stats[:, bass.ds(i * 12 + 6 * k, 6)], ob[k][:, :]).then_inc(noted, 1)

                def give(i, k):
                    n = i * 2 + k
                    dve.wait_ge(multiplied, n + 1)
                    wait_again(dve, sent[k], 16 * i)
                    nc.vector.tensor_copy(hb[k][:, 0:wrow], py[k][:, 0:wrow]).then_inc(out_ready, 1)
                    if kind == "x1":
                        nc.vector.tensor_copy(T.ar[:, bass.ds(i * 2 * HEADS + k * HEADS, HEADS)], py[k][:, WROW:WCAT])\
                            .then_inc(noted, 1)

                def step(i, k):
                    norm(i, k)
                    if weight is not None:
                        if past := near(i, k, -1, 2, NTURN):
                            give(*past)
                loop(dve, step)
                if weight is not None:
                    give(NTURN - 1, 1)

            @block.tensor
            def _(pe):
                if weight is None:
                    return

                def step(i, k):
                    n = i * 2 + k
                    pe.wait_ge(normed, n + 1)
                    wait_again(pe, copied, n - 1)
                    nc.tensor.transpose(pa[k][:, 0:P], ob[k][:, :], T.ident[:, :]).then_inc(turned, 1)
                    pe.wait_ge(copied, n + 1)
                    wait_again(pe, noted if kind == "x1" else out_ready, n - 1)
                    y = py[k][:, 0:width]
                    if bias is not None:
                        nc.tensor.matmul(y, T.ones[0:1, :], bias[0:1, :], start=True, stop=False)
                    nc.tensor.matmul(y, vt[k][:, :], weight[:, 0:width], start=bias is None, stop=True)\
                        .then_inc(multiplied, 1)
                loop(pe, step)
        S.clear()


class Bag:
    pass




def build(nc, X):
    with ExitStack() as ctx:
        T = Bag()
        T.moves = Moves(nc, ctx)

        def sb(c, name, shape, dt):
            t = c.enter_context(nc.sbuf_tensor(name, shape, dt))
            return t
        T.ident = sb(ctx, "ident", [P, P], F32)
        T.ident_b = sb(ctx, "ident_b", [P, P], BF16)
        T.ones = sb(ctx, "ones", [P, P], F32)
        T.ones_b = sb(ctx, "ones_b", [P, P], BF16)
        T.iota1_f = sb(ctx, "iota1_f", [P, P], F32)
        T.tile_s = sb(ctx, "tile_s", [1, C], I32)
        T.tile_d = sb(ctx, "tile_d", [1, C], I32)
        with ExitStack() as sort:
            T.before = sb(sort, "before", [P, P], F32)
            T.upto = sb(sort, "upto", [P, P], F32)
            T.zero_b = sb(sort, "zero_b", [P, P], BF16)
            T.iota_i = sb(sort, "iota_i", [P, P], I32)
            T.iota_b = sb(sort, "iota_b", [P, P], BF16)
            T.part_i = sb(sort, "part_i", [P, 1], I32)
            T.part_f = sb(sort, "part_f", [P, 1], F32)
            T.ident128_b = sb(sort, "ident128_b", [P, P], BF16)
            T.chunk_i = sb(sort, "chunk_i", [P, C], I32)
            T.chunk_f = sb(sort, "chunk_f", [P, C], F32)
            T.slo_b = sb(sort, "slo_b", [R, ROWE], BF16)
            T.shi_b = sb(sort, "shi_b", [R, ROWE], BF16)
            T.dlo_b = sb(sort, "dlo_b", [R, ROWE], BF16)
            T.dhi_b = sb(sort, "dhi_b", [R, ROWE], BF16)
            T.scol = sb(sort, "scol", [P, ROWCH * R], F32)
            T.dcol = sb(sort, "dcol", [P, ROWCH * R], F32)
            T.shicol = sb(sort, "shicol", [P, ROWCH * R], F32)
            T.dhicol = sb(sort, "dhicol", [P, ROWCH * R], F32)
            T.colp = sb(sort, "colp", [P, ROWCH * R], I32)
            T.meta_src = sb(sort, "meta_src", [P, ROWCH, R, 4], F32)
            T.meta_dst = sb(sort, "meta_dst", [P, ROWCH, R, 4], F32)
            T.hist_s = sb(sort, "hist_s", [P, NT], F32)
            T.hist_d = sb(sort, "hist_d", [P, NT], F32)
            T.first_s = sb(sort, "first_s", [P, NT], F32)
            T.first_d = sb(sort, "first_d", [P, NT], F32)
            build_constants(nc, T)
            build_prepare(nc, T, X)
            build_histogram(nc, T)
            build_offsets(nc, T)
            build_place(nc, T, X, True)
            build_place(nc, T, X, False)
        T.m_src = sb(ctx, "m_src", [P, C, 4], F32)
        T.last_src = sb(ctx, "last_src", [P, C], F32)
        T.acc = sb(ctx, "acc", [P, max(NT * ROW, 2 * SLEN)], F32)
        T.cat1 = sb(ctx, "cat1", [P, WCAT], F32)
        T.cat2 = sb(ctx, "cat2", [P, WCAT], F32)
        T.w0t = sb(ctx, "w0t", [P, 2 * D], F32)
        T.w1 = sb(ctx, "w1", [P, 2 * D], F32)
        T.w2 = sb(ctx, "w2", [P, 2, D], F32)
        T.wt = sb(ctx, "wt", [P, D], F32)
        T.w3 = sb(ctx, "w3", [P, D], F32)
        T.wres = sb(ctx, "wres", [P, D], F32)
        T.b1c = sb(ctx, "b1c", [P, 2], F32)
        T.b0r = sb(ctx, "b0r", [1, D], F32)
        T.b2r = sb(ctx, "b2r", [1, D], F32)
        T.btr = sb(ctx, "btr", [1, D], F32)
        T.b3r = sb(ctx, "b3r", [1, D], F32)
        T.bresr = sb(ctx, "bresr", [1, D], F32)
        T.bg1 = sb(ctx, "bg1", [P, D], F32)
        T.bg2 = sb(ctx, "bg2", [P, D], F32)
        T.gamma = sb(ctx, "gamma", [P, D], F32)
        T.beta = sb(ctx, "beta", [P, D], F32)
        T.stats = sb(ctx, "stats", [P, NT * 6], F32)
        build_weights(nc, T, X)
        build_flags(nc, T, X, True)
        build_max_edges(nc, T, X)
        with ExitStack() as gat:
            T.m_dst = sb(gat, "m_dst", [P, C, 4], F32)
            build_flags(nc, T, X, False)
            T.ar = sb(gat, "ar", [P, NT * HEADS], F32)
            with ExitStack() as table:
                T.nodes = sb(table, "nodes_a", [P, NT * D], F32)
                build_nodes(nc, T, X, "sage")
                build_norm(nc, T, X, "x1")
            T.z = sb(gat, "z", [P, C, HEADS], F32)
            for name in ("ga", "gb"):
                build_gat_logits(nc, T, X, name + "l")
                build_gat_softmax(nc, T, X, name + "m")
                build_gat_sums(nc, T, X, name + "s")
                if name == "ga":
                    build_nodes(nc, T, X, "gat_mid")
        T.nodes = sb(ctx, "nodes_b", [P, NT * D], F32)
        build_nodes(nc, T, X, "gat_end")
        build_norm(nc, T, X, "x2")
        build_norm(nc, T, X, "h2")
        build_mlp_edges(nc, T, X)
        build_nodes(nc, T, X, "mlp")
        build_norm(nc, T, X, "x3")
        build_gcn_edges(nc, T, X)
        build_nodes(nc, T, X, "gcn")
        build_norm(nc, T, X, "out")


_INS = ['x', 'src', 'dst', 'edge_attr_128', 'edge_weight', 'L0_gnn_W', 'L0_gnn_b', 'L1_gnn_W1', 'L1_gnn_att_l1', 'L1_gnn_att_r1', 'L1_gnn_b1', 'L1_gnn_W2', 'L1_gnn_att_l2', 'L1_gnn_att_r2', 'L1_gnn_b2', 'L2_gnn_ln_gamma', 'L2_gnn_ln_beta', 'L2_gnn_W1', 'L2_gnn_b1', 'L2_gnn_W2', 'L2_gnn_b2', 'L2_gnn_Wt', 'L2_gnn_bt', 'L3_gnn_W', 'L3_gnn_b', 'L3_gnn_Wres', 'L3_gnn_bres']


def kernel(**inputs):
    import numpy as _np
    import concourse.bacc as _bacc
    from concourse import mybir as _mybir
    from concourse.bass_utils import run_bass_kernel_spmd as _run

    nc = _bacc.Bacc("TRN2", target_bir_lowering=False, num_devices=1)
    X = Bag()
    arrays = {}
    for name in _INS:
        a = _np.ascontiguousarray(inputs[name])
        arrays[f"in_{name}_dram"] = a
        X.__dict__[name] = nc.dram_tensor(f"in_{name}_dram", a.shape, _mybir.dt.from_np(a.dtype), kind="ExternalInput").ap()
    X.out = nc.dram_tensor("out_0_dram", (N, D), F32, kind="ExternalOutput").ap()
    for name, shape, dt in (("xpad", (NPAD, D), F32), ("rec_src", (Q, REC), F32), ("rec_dst", (Q, 4), F32),
                            ("keys_src", (Q + 2,), F32), ("keys_dst", (Q + 2,), F32),
                            ("reset_src", (Q,), BF16), ("reset_dst", (Q,), BF16),
                            ("ends_dst", (Q,), BF16), ("logits", (HEADS, Q), F32), ("exps", (HEADS, Q), F32),
                            ("gathered", (NU * P, UROW), F32),
                            ("hrow", (NPAD, WROW), F32), ("x1", (NPAD, D), F32), ("x2", (NPAD, D), F32),
                            ("h2row", (NPAD, D), F32), ("x3", (NPAD, D), F32), ("h3row", (NPAD, D), F32)):
        X.__dict__[name] = nc.dram_tensor(f"s_{name}", shape, dt, kind="Internal").ap()
    build(nc, X)
    r = _run(nc, [arrays], core_ids=[0])
    return r.results[0]["out_0_dram"]
```

```python
from contextlib import ExitStack

import concourse.bass as bass
from concourse import mybir

ALU = mybir.AluOpType
ACT = mybir.ActivationFunctionType
AX = mybir.AxisListType
F32 = mybir.dt.float32
BF16 = mybir.dt.bfloat16
I32 = mybir.dt.int32
U32 = mybir.dt.uint32

P = 128
N = 12500
E = 200000
D = 128
NT = -(-N // P)
NPAD = NT * P
SPARE = NPAD - 1
HEADS = 4
HID = D // HEADS
LN_EPS = 1e-5
NEG = -3.0e38
LOW = -1.0e30

ROWCH = 16
ROWE = ROWCH * P
EROWS = E // ROWE
ECH = -(-E // P)
TAILCH = ECH - EROWS * ROWCH
TAILE = E - EROWS * ROWE
R = EROWS + 1

CBLK = -(-((ECH * P + NT * (P - 1)) // P) // P)
C = CBLK * P
Q = C * P
U = 4
ITERS = C // (4 * U)
REC = D + 4
ROW = D + HEADS
BASE = 8


def wait_again(eng, sem, value):
    if not (isinstance(value, int) and value <= 0):
        eng.wait_ge(sem, value)


class Sems:

    def __init__(self, nc, ctx, phase):
        self.nc, self.ctx, self.phase, self.all = nc, ctx, phase, []

    def __call__(self, name):
        s = self.ctx.enter_context(self.nc.semaphore(f"{self.phase}_{name}"))
        self.all.append(s)
        return s

    def clear(self):
        with self.nc.Block() as block:
            @block.sync
            def _(sp):
                for s in self.all:
                    sp.sem_clear(s)


class Moves:

    def __init__(self, nc, ctx):
        self.sems = [[ctx.enter_context(nc.semaphore(f"moved{g}_{j}")) for j in range(U)] for g in range(4)]
        self.before = [[0] * U for _ in range(4)]

    def wait(self, eng, i, g, chunks=range(U)):
        for j in chunks:
            eng.wait_ge(self.sems[g][j], i * 16 + (self.before[g][j] + 16))

    def wait_last(self, eng, i, g):
        if not (isinstance(i, int) and i == 0):
            for j in range(U):
                eng.wait_ge(self.sems[g][j], i * 16 + self.before[g][j])

    def close(self, count):
        for g in range(4):
            for j in range(U):
                self.before[g][j] += 16 * count(g, j)


def chain(eng, sem):
    count = [0]

    def link(ins):
        count[0] += 1
        ins.then_inc(sem, 1)
        eng.wait_ge(sem, count[0])
    return link


def spread(ap, n):
    return ap.unsqueeze(2).broadcast_to([ap.shape[0], ap.shape[1], n])


def repeat(ap, n):
    return ap.unsqueeze(1).broadcast_to([ap.shape[0], n, ap.shape[1]])


def build_constants(nc, T):
    with ExitStack() as ctx:
        S = Sems(nc, ctx, "const")
        filled, cut, copied = S("filled"), S("cut"), S("copied")
        with nc.Block() as block:
            @block.gpsimd
            def _(pool):
                pool.memset(T.ident[:, :], 0.0).then_inc(filled, 1)
                pool.memset(T.before[:, :], 1.0).then_inc(filled, 1)
                pool.memset(T.upto[:, :], 1.0).then_inc(filled, 1)
                pool.memset(T.ones[:, :], 1.0).then_inc(filled, 1)
                pool.memset(T.ones_b[:, :], 1.0).then_inc(filled, 1)
                pool.memset(T.zero_b[:, :], 0.0).then_inc(filled, 1)
                pool.wait_ge(filled, 6)
                pool.affine_select(out=T.ident[:, :], in_=T.ident[:, :], compare_op=ALU.not_equal, fill=1.0,
                                   base=0, pattern=[[-1, P]], channel_multiplier=1).then_inc(cut, 1)
                pool.affine_select(out=T.before[:, :], in_=T.before[:, :], compare_op=ALU.is_gt, fill=0.0,
                                   base=0, pattern=[[-1, P]], channel_multiplier=1).then_inc(cut, 1)
                pool.affine_select(out=T.upto[:, :], in_=T.upto[:, :], compare_op=ALU.is_gt, fill=0.0,
                                   base=0, pattern=[[1, P]], channel_multiplier=-1).then_inc(cut, 1)
                pool.iota(T.iota_i[:, :], pattern=[[1, P]], base=0, channel_multiplier=0).then_inc(cut, 1)
                pool.iota(T.part_i[:, :], pattern=[[0, 1]], base=0, channel_multiplier=1).then_inc(cut, 1)
                pool.iota(T.chunk_i[:, :], pattern=[[1, C]], base=0, channel_multiplier=0).then_inc(cut, 1)

            @block.vector
            def _(dve):
                dve.wait_ge(cut, 6)
                nc.vector.tensor_copy(T.iota_b[:, :], T.iota_i[:, :]).then_inc(copied, 1)
                nc.vector.tensor_scalar(T.iota1_f[:, :], T.iota_i[:, :], 1.0, None, ALU.add).then_inc(copied, 1)
                nc.vector.tensor_copy(T.part_f[:, :], T.part_i[:, :]).then_inc(copied, 1)
                nc.vector.tensor_copy(T.ident_b[:, :], T.ident[:, :]).then_inc(copied, 1)
                nc.vector.tensor_scalar(T.ident128_b[:, :], T.ident[:, :], float(P), None, ALU.mult)\
                    .then_inc(copied, 1)
                nc.vector.tensor_copy(T.chunk_f[:, :], T.chunk_i[:, :]).then_inc(copied, 1)
        S.clear()


def build_prepare(nc, T, X):
    with ExitStack() as ctx:
        S = Sems(nc, ctx, "prep")
        dummy, loaded, xout = S("dummy"), S("loaded"), S("xout")
        zero_set, zeroed, dve_at, turned, taken = S("zero_set"), S("zeroed"), S("dve_at"), S("turned"), S("taken")
        src_r = ctx.enter_context(nc.sbuf_tensor("src_r", [R, ROWE], I32))
        dst_r = ctx.enter_context(nc.sbuf_tensor("dst_r", [R, ROWE], I32))
        ew_r = ctx.enter_context(nc.sbuf_tensor("ew_r", [R, ROWE], F32))
        key_f = ctx.enter_context(nc.sbuf_tensor("key_f", [R, ROWE], F32))
        part = ctx.enter_context(nc.sbuf_tensor("part", [R, ROWE], I32))
        col_i = ctx.enter_context(nc.sbuf_tensor("col_i", [P, ROWCH * R], I32))
        zeros = ctx.enter_context(nc.sbuf_tensor("zeros", [P, C], F32))
        ps = [ctx.enter_context(nc.psum_tensor(f"ps_prep{k}", [P, 512], F32)) for k in range(2)]
        with nc.Block() as block:
            @block.sync
            def _(sp):
                sp.wait_ge(dummy, 4)
                for t, a in ((src_r, X.src), (dst_r, X.dst), (ew_r, X.edge_weight)):
                    sp.dma_start(t[0:EROWS, :], a[0:EROWS * ROWE].rearrange("(r e) -> r e", e=ROWE))\
                        .then_inc(loaded, 16)
                    sp.dma_start(t[EROWS:R, 0:TAILE], a[EROWS * ROWE:E].rearrange("(r e) -> r e", r=1))\
                        .then_inc(loaded, 16)
                rows = "(p k) f -> p (k f)"
                sp.dma_start(X.xpad[0:N, :].rearrange(rows, p=125), X.x.rearrange(rows, p=125)).then_inc(xout, 16)
                sp.wait_ge(zero_set, 1)
                sp.dma_start(X.xpad[N:NPAD, :], zeros[0:NPAD - N, 0:D]).then_inc(xout, 16)
                sp.wait_ge(xout, 32)

            @block.scalar
            def _(act):
                act.wait_ge(zero_set, 1)
                act.dma_start(X.rec_dst.rearrange("(p k) f -> p (k f)", p=P),
                              zeros[:, :].unsqueeze(1).broadcast_to([P, 4, C])).then_inc(zeroed, 16)
                act.wait_ge(zeroed, 16)

            @block.vector
            def _(dve):
                nc.vector.memset(src_r[:, :], SPARE).then_inc(dummy, 1)
                nc.vector.memset(dst_r[:, :], SPARE).then_inc(dummy, 1)
                nc.vector.memset(ew_r[:, :], 0.0).then_inc(dummy, 1)
                nc.vector.memset(zeros[:, :], 0.0).then_inc(zero_set, 1)
                nc.vector.memset(T.meta_src[:, :, :, :], 0.0).then_inc(dummy, 1)
                nc.vector.memset(T.meta_dst[:, :, :, :], 0.0).then_inc(dve_at, 1)
                link_n = [1]

                def link(ins):
                    link_n[0] += 1
                    ins.then_inc(dve_at, 1)
                    dve.wait_ge(dve_at, link_n[0])
                dve.wait_ge(loaded, 16 * 6)
                dve.wait_ge(dummy, 4)
                dve.wait_ge(dve_at, 1)
                for k_r, lo_b, hi_b, col, hicol, mine, other in (
                        (src_r, T.slo_b, T.shi_b, T.scol, T.shicol, T.meta_src, T.meta_dst),
                        (dst_r, T.dlo_b, T.dhi_b, T.dcol, T.dhicol, T.meta_dst, T.meta_src)):
                    n = 0 if k_r is src_r else 1
                    link(nc.vector.tensor_scalar(part[:, :], k_r[:, :], P - 1, None, ALU.bitwise_and))
                    link(nc.vector.tensor_copy(lo_b[:, :], part[:, :]))
                    link(nc.vector.tensor_scalar(part[:, :], k_r[:, :], 7, None, ALU.logical_shift_right))
                    link(nc.vector.tensor_copy(hi_b[:, :], part[:, :]))
                    if n:
                        dve.wait_ge(turned, 4)
                    link(nc.vector.tensor_copy(key_f[:, :], k_r[:, :]))
                    for g in range(4):
                        dve.wait_ge(turned, 4 * n + g + 1)
                        nc.vector.tensor_copy(col[:, g * 4 * R:(g + 1) * 4 * R], ps[g % 2][:, 0:4 * R])\
                            .then_inc(taken, 1)
                    dve.wait_ge(taken, 4 * n + 4)
                    link(nc.vector.tensor_copy(col_i[:, :], col[:, :]))
                    flat = mine[:, :, :, :].rearrange("p b r f -> p (b r) f")
                    link(nc.vector.tensor_scalar(flat[:, :, 3], col[:, :], 1.0, None, ALU.add))
                    link(nc.vector.tensor_copy(other[:, :, :, :].rearrange("p b r f -> p (b r) f")[:, :, 0],
                                               col[:, :]))
                    link(nc.vector.tensor_scalar(part2 := T.colp[:, :], col_i[:, :], P - 1, None, ALU.bitwise_and))
                    link(nc.vector.tensor_scalar(flat[:, :, 2], part2, 1.0, None, ALU.add))
                    link(nc.vector.tensor_scalar(part2, col_i[:, :], 7, None, ALU.logical_shift_right))
                    link(nc.vector.tensor_copy(hicol[:, :], part2))
                for g in range(4):
                    dve.wait_ge(turned, 8 + g + 1)
                    for m, meta in enumerate((T.meta_src, T.meta_dst)):
                        ins = nc.vector.tensor_copy(meta[:, 4 * g:4 * g + 4, :, 1],
                                                    ps[g % 2][:, 0:4 * R].rearrange("p (b r) -> p b r", r=R))
                    ins.then_inc(taken, 1)

            @block.tensor
            def _(pe):
                pe.wait_ge(loaded, 16 * 6)
                for n, rows in enumerate((key_f, key_f, ew_r)):
                    if n < 2:
                        pe.wait_ge(dve_at, (6, 6 + 7 + 5)[n])
                    for g in range(4):
                        u = 4 * n + g
                        if u >= 2:
                            pe.wait_ge(taken, u - 1)
                        for j in range(4):
                            b = 4 * g + j
                            ins = nc.tensor.transpose(ps[g % 2][:, j * R:(j + 1) * R], rows[:, b * P:(b + 1) * P],
                                                      T.ident[0:R, 0:R])
                        ins.then_inc(turned, 1)
        S.clear()


def build_histogram(nc, T, X):
    with ExitStack() as ctx:
        S = Sems(nc, ctx, "hist")
        hot_ready, counted, stored, zero_set, zeroed = (
            S("hot_ready"), S("counted"), S("stored"), S("zero_set"), S("zeroed"))
        zeros = ctx.enter_context(nc.sbuf_tensor("hist_zeros", [P, 16 * REC], F32))
        hot_lo = [ctx.enter_context(nc.sbuf_tensor(f"hist_lo{k}", [P, P, U], BF16)) for k in range(2)]
        hot_hi = [ctx.enter_context(nc.sbuf_tensor(f"hist_hi{k}", [P, NT, U], BF16)) for k in range(2)]
        wide = ctx.enter_context(nc.sbuf_tensor("hist_wide", [P, P, U], BF16))
        wide1 = ctx.enter_context(nc.sbuf_tensor("hist_wide1", [P, P, U], BF16))
        key_lo = [ctx.enter_context(nc.sbuf_tensor(f"hist_klo{k}", [P, R, ROWCH], BF16)) for k in range(2)]
        key_hi = [ctx.enter_context(nc.sbuf_tensor(f"hist_khi{k}", [P, R, ROWCH], BF16)) for k in range(2)]
        written = S("written")
        ps = [ctx.enter_context(nc.psum_tensor(f"ps_hist{k}", [P, 512], F32)) for k in range(2)]
        metas, hicols = (T.meta_src, T.meta_dst), (T.shicol, T.dhicol)

        def units(eng, unit):
            with eng.Fori(0, EROWS) as i:
                for g in range(4):
                    for k in range(2):
                        unit(k, i, g, U, i * 8 + (2 * g + k))
            for g in range(-(-TAILCH // U)):
                for k in range(2):
                    unit(k, EROWS, g, min(U, TAILCH - U * g), EROWS * 8 + 2 * g + k)
        NU = EROWS * 8 + 2 * -(-TAILCH // U)

        with nc.Block() as block:
            @block.vector
            def _(dve):
                def unit(k, i, g, m, n):
                    dve.wait_ge(counted, n + 1)
                    for hot, width, iota, key in ((hot_lo[k], P, wide1, key_lo[k]), (hot_hi[k], NT, wide, key_hi[k])):
                        here = key[:, bass.ds(i, 1), 4 * g:4 * g + m].broadcast_to([P, width, m])
                        ins = nc.vector.tensor_tensor(hot[:, :, 0:m], iota[:, 0:width, 0:m], here, ALU.is_equal)
                    ins.then_inc(hot_ready, 1)
                nc.vector.memset(zeros[:, :], 0.0).then_inc(zero_set, 1)
                nc.vector.tensor_copy(wide[:, :, :], spread(T.iota_b[:, :], U)).then_inc(written, 1)
                nc.vector.tensor_copy(wide1[:, :, :], spread(T.iota1_f[:, :], U)).then_inc(written, 1)
                for k in range(2):
                    nc.vector.tensor_copy(key_lo[k][:, :, :], metas[k][:, :, :, 2].rearrange("p b r -> p r b"))\
                        .then_inc(written, 1)
                    nc.vector.tensor_copy(key_hi[k][:, :, :], hicols[k][:, :].rearrange("p (b r) -> p r b", r=R))\
                        .then_inc(written, 1)
                dve.wait_ge(written, 6)
                units(dve, unit)
                for k, h in enumerate((T.hist_s, T.hist_d)):
                    dve.wait_ge(counted, NU + 2)
                    nc.vector.tensor_copy(h[:, :], ps[k][:, 0:NT]).then_inc(stored, 1)

            @block.sync
            def _(sp):
                sp.wait_ge(zero_set, 1)
                rows = X.rec_src.rearrange("(p b k) f -> b p (k f)", p=P, k=16)
                with sp.Fori(0, C // 16) as b:
                    sp.dma_start(rows[bass.ds(b, 1)].squeeze(0), zeros[:, :]).then_inc(zeroed, 16)
                sp.wait_ge(zeroed, 16 * (C // 16))

            @block.tensor
            def _(pe):
                pe.sem_inc(counted, 2)
                for k in range(2):
                    nc.tensor.matmul(ps[k][:, 0:NT], T.ident_b[:, :], T.zero_b[:, 0:NT], start=True, stop=False,
                                     skip_group_check=True)

                def unit(k, i, g, m, n):
                    pe.wait_ge(hot_ready, n + 1)
                    for j in range(m):
                        ins = nc.tensor.matmul(ps[k][:, 0:NT], hot_lo[k][:, :, j], hot_hi[k][:, :, j],
                                               start=False, stop=False, skip_group_check=True)
                    ins.then_inc(counted, 1)
                units(pe, unit)
        S.clear()


def build_offsets(nc, T):
    with ExitStack() as ctx:
        S = Sems(nc, ctx, "offs")
        dve_at, pe_at = S("dve_at"), S("pe_at")
        cnt_i = ctx.enter_context(nc.sbuf_tensor("cnt_i", [P, NT], I32))
        cnt_j = ctx.enter_context(nc.sbuf_tensor("cnt_j", [P, NT], I32))
        ch = ctx.enter_context(nc.sbuf_tensor("ch", [P, NT + 1], F32))
        upto_ch = ctx.enter_context(nc.sbuf_tensor("upto_ch", [P, NT + 1], F32))
        first_ch = ctx.enter_context(nc.sbuf_tensor("first_ch", [P, 1], F32))
        reached = ctx.enter_context(nc.sbuf_tensor("reached", [P, C], BF16))
        tile_f = ctx.enter_context(nc.sbuf_tensor("tile_f", [1, C], F32))
        pc = ctx.enter_context(nc.psum_tensor("ps_cnt", [P, 512], F32))
        pp = ctx.enter_context(nc.psum_tensor("ps_pre", [P, 512], F32))
        pf = ctx.enter_context(nc.psum_tensor("ps_fst", [P, 512], F32))
        NW = -(-C // 512)
        pt = [ctx.enter_context(nc.psum_tensor(f"ps_til{k}", [P, 512], F32)) for k in range(NW)]
        STEPS = 11 + NW
        with nc.Block() as block:
            @block.vector
            def _(dve):
                link = chain(dve, dve_at)
                for k, (h, first, tiles) in enumerate(((T.hist_s, T.first_s, T.tile_s), (T.hist_d, T.first_d, T.tile_d))):
                    dve.wait_ge(pe_at, 3 * k + 1)
                    link(nc.vector.tensor_scalar(cnt_i[:, :], pc[:, 0:NT], float(P - 1), None, ALU.add))
                    link(nc.vector.tensor_scalar(cnt_j[:, :], cnt_i[:, :], 7, None, ALU.logical_shift_right))
                    link(nc.vector.memset(ch[:, 0:1], 0.0))
                    link(nc.vector.tensor_copy(ch[:, 1:NT + 1], cnt_j[:, :]))
                    link(nc.vector.tensor_tensor_scan(upto_ch[:, :], ch[:, :], ch[:, :], 0.0, ALU.add, ALU.max))
                    link(nc.vector.scalar_tensor_tensor(out=first[:, :], in0=upto_ch[:, 0:NT], scalar=float(P),
                                                        in1=pp[:, 0:NT], op0=ALU.mult, op1=ALU.add))
                    dve.wait_ge(pe_at, 3 * k + 2)
                    link(nc.vector.tensor_copy(first_ch[0:NT, :], pf[0:NT, 0:1]))
                    link(nc.vector.tensor_scalar(reached[0:NT, :], T.chunk_f[0:NT, :], first_ch[0:NT, 0:1], None, ALU.is_ge))
                    dve.wait_ge(pe_at, 3 * k + 3)
                    for w in range(NW):
                        a, b = w * 512, min(C, w * 512 + 512)
                        link(nc.vector.tensor_scalar(tile_f[0:1, a:b], pt[w][0:1, 0:b - a], -1.0, None, ALU.add))
                    link(nc.vector.tensor_copy(tiles[:, :], tile_f[:, :]))

            @block.tensor
            def _(pe):
                for k, h in enumerate((T.hist_s, T.hist_d)):
                    if k:
                        pe.wait_ge(dve_at, 9 + NW)
                    nc.tensor.matmul(pc[:, 0:NT], T.ones[:, :], h[:, :], start=True, stop=True)
                    nc.tensor.matmul(pp[:, 0:NT], T.upto[:, :], h[:, :], start=True, stop=True).then_inc(pe_at, 1)
                    pe.wait_ge(dve_at, (9 + NW) * k + 5)
                    nc.tensor.matmul(pf[0:NT, 0:1], upto_ch[0:1, 0:NT], T.ones[0:1, 0:1], start=True, stop=True)\
                        .then_inc(pe_at, 1)
                    pe.wait_ge(dve_at, (9 + NW) * k + 8)
                    for w in range(NW):
                        a, b = w * 512, min(C, w * 512 + 512)
                        ins = nc.tensor.matmul(pt[w][0:1, 0:b - a], T.ones_b[0:NT, 0:1], reached[0:NT, a:b],
                                               start=True, stop=True)
                    ins.then_inc(pe_at, 1)
        S.clear()


def build_place(nc, T, X, by_src):
    name = "pls" if by_src else "pld"
    lo_b, hi_b = (T.slo_b, T.shi_b) if by_src else (T.dlo_b, T.dhi_b)
    col, hicol = (T.scol, T.shicol) if by_src else (T.dcol, T.dhicol)
    meta, first = (T.meta_src, T.first_s) if by_src else (T.meta_dst, T.first_d)
    width = REC if by_src else 4
    target = X.rec_src if by_src else X.rec_dst
    TAILU = -(-TAILCH // U)
    with ExitStack() as ctx:
        S = Sems(nc, ctx, name)
        rows_ready, rows_free, hot_ready = S("rows_ready"), S("rows_free"), S("hot_ready")
        table_at, table_read, slots_ready = S("table_at"), S("table_read"), S("slots_ready")
        at_done, at_read, at_summed = S("at_done"), S("at_read"), S("at_summed")
        meta_ready, pool_step, m_in = S("meta_ready"), S("pool_step"), S("m_in")
        attr_in = [S(f"attr_in{k}") for k in range(4)]

        def sb(n, shape, dt):
            return ctx.enter_context(nc.sbuf_tensor(f"{name}_{n}", shape, dt))

        def pb(n):
            return ctx.enter_context(nc.psum_tensor(f"{name}_{n}", [P, 512], F32))
        lo_hot = [sb(f"lo_hot{k}", [P, U, P], BF16) for k in range(2)]
        hi_hot = [sb(f"hi_hot{k}", [P, U, NT], BF16) for k in range(2)]
        hi_f = [sb(f"hi_f{k}", [P, U, NT], F32) for k in range(2)]
        lo_hot_t = [sb(f"lo_hot_t{k}", [P, U * P], F32) for k in range(2)]
        same = [sb(f"same{k}", [P, U, P], BF16) for k in range(2)]
        rank = [sb(f"rank{k}", [P, U], F32) for k in range(2)]
        at = [sb(f"at{k}", [P, U], F32) for k in range(2)]
        slot = [sb(f"slot{k}", [P, U], U32) for k in range(4)]
        rec = [sb(f"rec{k}", [P, U, width], F32) for k in range(4)]
        table = [sb(f"table{k}", [P, NT], F32) for k in range(2)]
        ps_lo = [pb(f"ps_lo{k}") for k in range(2)]
        ps_key = [pb(f"ps_key{k}") for k in range(2)]
        ps_at = [pb(f"ps_at{k}") for k in range(2)]
        ps_table = [pb(f"ps_table{k}") for k in range(2)]

        def turns(eng, unit):
            for g in range(4):
                unit(0, g, U)
            with eng.Fori(1, EROWS) as i:
                for g in range(4):
                    unit(i, g, U)
            for g in range(TAILU):
                unit(EROWS, g, min(U, TAILCH - U * g))

        with nc.Block() as block:
            @block.sync
            def _(sp):
                if not by_src:
                    sp.dma_start(T.m_src[:, :, :], X.rec_src.rearrange("(c p) f -> p c f", p=P)[:, :, D:REC])\
                        .then_inc(m_in, 16)
                    sp.wait_ge(m_in, 16)
                if by_src:
                    def unit(i, g, m):
                        T.moves.wait_last(sp, i, g)
                        rows = X.edge_attr_128[bass.ds(i * ROWE + g * U * P, m * P), :]
                        sp.dma_start(rec[g][:, 0:m, 0:D], rows.rearrange("(j e) f -> e j f", e=P)).then_inc(attr_in[g], 16)
                    for g in range(4):
                        unit(0, g, U)
                    with sp.Fori(1, EROWS) as i:
                        for g in range(4):
                            unit(i, g, U)
                    for g in range(TAILU):
                        m = min(U, TAILCH - U * g)
                        if (EROWS * ROWCH + U * g + m) * P <= E:
                            unit(EROWS, g, m)
                        else:
                            a = EROWS * ROWE + g * U * P
                            full = (E - a) // P
                            T.moves.wait_last(sp, EROWS, g)
                            sp.dma_start(rec[g][:, 0:full, 0:D], X.edge_attr_128[a:a + full * P, :]
                                         .rearrange("(j e) f -> e j f", e=P)).then_inc(attr_in[g], 16)
                            sp.dma_start(rec[g][0:E - a - full * P, full, 0:D], X.edge_attr_128[a + full * P:E, :])\
                                .then_inc(attr_in[g], 16)

            @block.gpsimd
            def _(pool):

                def unit(i, g, m):
                    pool.wait_ge(slots_ready, i * 4 + (g + 1))
                    pool.wait_ge(meta_ready, i * 4 + (g + 1))
                    if by_src:
                        pool.wait_ge(attr_in[g], i * 16 + (16 if m == U else 32))
                    pool.sem_inc(pool_step, 1)
                    for j in range(m):
                        pool.indirect_dma_start(target[:, :], bass.IndirectOffsetOnAxis(ap=slot[g][:, j:j + 1], axis=0),
                                                rec[g][:, j, :], None).then_inc(T.moves.sems[g][j], 16)
                turns(pool, unit)
                for g in range(4):
                    tail = range(max(0, min(U, TAILCH - U * g)))
                    T.moves.wait(pool, EROWS, g, tail)
                    T.moves.wait(pool, EROWS - 1, g, range(len(tail), U))

            @block.scalar
            def _(act):
                def unit(i, g, m):
                    T.moves.wait_last(act, i, g)
                    nc.scalar.copy(rec[g][:, 0:m, width - 4:width],
                                   meta[:, 4 * g:4 * g + m, bass.ds(i, 1), :].squeeze(2)).then_inc(meta_ready, 1)
                    for j in range(m):
                        n = i * ROWCH + (U * g + j)
                        act.wait_ge(table_at, n + BASE)
                        wait_again(act, at_done, n - 1)
                        nc.scalar.copy(table[j % 2][:, :], ps_table[j % 2][:, 0:NT]).then_inc(table_read, 1)
                turns(act, unit)

            @block.vector
            def _(dve):
                dve.sem_inc(rows_free, 2)
                dve.sem_inc(at_read, 2)

                def front(i, g, m):
                    k = g % 2
                    n = i * 4 + g
                    dve.wait_ge(table_at, i * ROWCH + (U * (g - 1) + 1 + BASE))
                    lo = meta[:, 4 * g:4 * g + m, bass.ds(i, 1), 2].squeeze(2)
                    hi = hicol[:, :].rearrange("p (b r) -> p b r", r=R)[:, 4 * g:4 * g + m, bass.ds(i, 1)].squeeze(2)
                    nc.vector.tensor_tensor(lo_hot[k][:, 0:m, :], repeat(T.iota1_f[:, :], m), spread(lo, P), ALU.is_equal)
                    nc.vector.tensor_tensor(hi_hot[k][:, 0:m, :], repeat(T.iota_b[:, 0:NT], m), spread(hi, NT), ALU.is_equal)
                    dve.wait_ge(rows_ready, n + 1)
                    nc.vector.tensor_scalar(lo_hot_t[k][:, 0:m * P], ps_lo[k][:, 0:m * P], T.part_f[:, 0:1], None,
                                            ALU.is_equal).then_inc(hot_ready, 1)
                    wait_again(dve, slots_ready, i * 4 + (g - 1))
                    for j in range(m):
                        ins = nc.vector.scalar_tensor_tensor(
                            out=same[k][:, j, :], in0=ps_key[k][:, j * P:(j + 1) * P],
                            scalar=col[:, :].rearrange("p (b r) -> p b r", r=R)[:, 4 * g + j, bass.ds(i, 1)],
                            in1=T.before[:, :], op0=ALU.is_equal, op1=ALU.mult, accum_out=rank[k][:, j:j + 1])
                    ins.then_inc(rows_free, 1)

                def back(i, g, m):
                    k = g % 2
                    dve.wait_ge(at_done, i * ROWCH + (U * g + m))
                    read = ps_at[k][:, 0:m * NT].rearrange("p (j t) -> p j t", t=NT)
                    nc.vector.tensor_tensor(hi_f[k][:, 0:m, :], hi_hot[k][:, 0:m, :], read, ALU.mult).then_inc(at_read, 1)
                    dve.wait_ge(at_read, i * 4 + (g + 3))
                    nc.vector.tensor_reduce(at[k][:, 0:m], hi_f[k][:, 0:m, :], AX.X, ALU.add).then_inc(at_summed, 1)
                    dve.wait_ge(at_summed, i * 4 + (g + 1))
                    dve.wait_ge(rows_free, i * 4 + (g + 3))
                    T.moves.wait_last(dve, i, g)
                    nc.vector.tensor_tensor(slot[g][:, 0:m], at[k][:, 0:m], rank[k][:, 0:m], ALU.add)\
                        .then_inc(slots_ready, 1)

                front(0, 0, U)
                for g in range(4):
                    front((g + 1) // 4, (g + 1) % 4, U)
                    back(0, g, U)
                with dve.Fori(1, EROWS) as i:
                    for g in range(4):
                        front(i + (g + 1) // 4, (g + 1) % 4, U)
                        back(i, g, U)
                for g in range(TAILU):
                    if g + 1 < TAILU:
                        front(EROWS, g + 1, min(U, TAILCH - U * (g + 1)))
                    back(EROWS, g, min(U, TAILCH - U * g))

            @block.tensor
            def _(pe):
                pe.sem_inc(table_at, BASE - 1)
                for k in range(2):
                    ins = nc.tensor.matmul(ps_table[k][:, 0:NT], T.ident[:, :], first[:, :], start=True, stop=False,
                                           skip_group_check=True)
                ins.then_inc(table_at, 1)

                def count(k, h, j):
                    return nc.tensor.matmul(ps_table[k][:, 0:NT], lo_hot[h][:, j, :], hi_hot[h][:, j, :], start=False,
                                            stop=False, skip_group_check=True)

                def rows(i, g, m):
                    k = g % 2
                    pe.wait_ge(rows_free, i * 4 + (g + 1))
                    pick = T.ident_b[0:R, bass.ds(i, 1)].broadcast_to([R, P])
                    pick128 = T.ident128_b[0:R, bass.ds(i, 1)].broadcast_to([R, P])
                    a, b = g * U * P, (g * U + m) * P
                    nc.tensor.matmul(ps_lo[k][:, 0:m * P], pick, lo_b[:, a:b], start=True, stop=True)
                    nc.tensor.matmul(ps_key[k][:, 0:m * P], pick, lo_b[:, a:b], start=True, stop=False)
                    nc.tensor.matmul(ps_key[k][:, 0:m * P], pick128, hi_b[:, a:b], start=False, stop=True)\
                        .then_inc(rows_ready, 1)

                def unit(i, g, m):
                    k = g % 2
                    pe.wait_ge(hot_ready, i * 4 + (g + 1))
                    for j in range(m):
                        if j:
                            count((j + 1) % 2, k, j - 1)
                        elif not (isinstance(i, int) and i == g == 0):
                            count((j + 1) % 2, 1 - k, U - 1)
                        count((j + 1) % 2, k, j).then_inc(table_at, 1)
                        pe.wait_ge(table_read, i * ROWCH + (U * g + j + 1))
                        if j == 0:
                            pe.wait_ge(at_read, i * 4 + (g + 1))
                        nc.tensor.matmul(ps_at[k][:, j * NT:(j + 1) * NT], lo_hot_t[k][:, j * P:(j + 1) * P],
                                         table[j % 2][:, :], start=True, stop=True).then_inc(at_done, 1)
                rows(0, 0, U)
                for g in range(4):
                    rows((g + 1) // 4, (g + 1) % 4, U)
                    unit(0, g, U)
                with pe.Fori(1, EROWS) as i:
                    for g in range(4):
                        rows(i + (g + 1) // 4, (g + 1) % 4, U)
                        unit(i, g, U)
                for g in range(TAILU):
                    if g + 1 < TAILU:
                        rows(EROWS, g + 1, min(U, TAILCH - U * (g + 1)))
                    unit(EROWS, g, min(U, TAILCH - U * g))
        T.moves.close(lambda g, j: EROWS + (U * g + j < TAILCH))
        S.clear()


NU = C // U
UROW = U * (D + HEADS)
STRIPS = P // HEADS
SLEN = Q // STRIPS


def turns(eng, unit, depth=4, count=ITERS):
    for g in range(depth):
        unit(0, g)
    with eng.Fori(1, count - 1) as i:
        for g in range(depth):
            unit(i, g)
    for g in range(depth):
        unit(count - 1, g)


def near(i, g, k, depth=4, count=ITERS):
    j, h = i + (g + k) // depth, (g + k) % depth
    return None if isinstance(j, int) and not 0 <= j < count else (j, h)


def tiles_of(nc, eng_type, row, i, g, units=1):
    return nc.values_load_multi_w_load_instructions(row[0:1, bass.ds(i * 4 * U + g * U, units * U)], engines=[eng_type],
                                                    min_val=0, max_val=NT - 1,
                                                    skip_runtime_bounds_check_because="tiles are counted below NT")[1]


def build_flags(nc, T, X, by_src):
    name = "fls" if by_src else "fld"
    m, keys, reset = (T.m_src, X.keys_src, X.reset_src) if by_src else (T.m_dst, X.keys_dst, X.reset_dst)
    with ExitStack() as ctx:
        S = Sems(nc, ctx, name)
        turned, taken, stored, shifted, done, dve_at, guard = (
            S("turned"), S("taken"), S("stored"), S("shifted"), S("done"), S("dve_at"), S("guard"))
        kt = ctx.enter_context(nc.sbuf_tensor(name + "_kt", [P, CBLK, P], F32))
        prev = ctx.enter_context(nc.sbuf_tensor(name + "_prev", [P, CBLK, P], F32))
        nxt = ctx.enter_context(nc.sbuf_tensor(name + "_next", [P, CBLK, P], F32))
        rs = ctx.enter_context(nc.sbuf_tensor(name + "_rs", [P, CBLK, P], BF16))
        re = ctx.enter_context(nc.sbuf_tensor(name + "_re", [P, CBLK, P], BF16))
        edge = ctx.enter_context(nc.sbuf_tensor(name + "_edge", [1, 2], F32))
        ps = [ctx.enter_context(nc.psum_tensor(f"{name}_ps{k}", [P, 512], F32)) for k in range(4)]
        groups = [range(a, min(a + 4, CBLK)) for a in range(0, CBLK, 4)]
        with nc.Block() as block:
            @block.sync
            def _(sp):
                sp.wait_ge(guard, 1)
                sp.dma_start(keys[0:1].unsqueeze(0), edge[:, 0:1]).then_inc(stored, 16)
                sp.dma_start(keys[Q + 1:Q + 2].unsqueeze(0), edge[:, 1:2]).then_inc(stored, 16)
                sp.wait_ge(taken, len(groups))
                view = "(b c p) -> c b p"
                sp.dma_start(keys[1:Q + 1].rearrange(view, b=CBLK, c=P), kt[:, :, :]).then_inc(stored, 16)
                sp.wait_ge(stored, 48)
                sp.dma_start(prev[:, :, :], keys[0:Q].rearrange(view, b=CBLK, c=P)).then_inc(shifted, 16)
                sp.dma_start(nxt[:, :, :], keys[2:Q + 2].rearrange(view, b=CBLK, c=P)).then_inc(shifted, 16)
                sp.wait_ge(dve_at, 3)
                sp.dma_start(reset.rearrange(view, b=CBLK, c=P), rs[:, :, :]).then_inc(done, 16)
                if not by_src:
                    sp.wait_ge(dve_at, 4)
                    sp.dma_start(X.ends_dst.rearrange(view, b=CBLK, c=P), re[:, :, :]).then_inc(done, 16)
                sp.wait_ge(done, 16 if by_src else 32)

            @block.vector
            def _(dve):
                nc.vector.memset(edge[:, :], -1.0).then_inc(guard, 1)
                for n, blocks in enumerate(groups):
                    dve.wait_ge(turned, n + 1)
                    w = len(blocks) * P
                    nc.vector.tensor_copy(kt[:, blocks[0]:blocks[0] + len(blocks), :],
                                          ps[n][:, 0:w].rearrange("c (b p) -> c b p", p=P)).then_inc(taken, 1)
                dve.wait_ge(taken, len(groups))
                dve.wait_ge(shifted, 32)
                link = chain(dve, dve_at)
                link(nc.vector.tensor_tensor(prev[:, :, :], prev[:, :, :], kt[:, :, :], ALU.not_equal))
                link(nc.vector.tensor_tensor(nxt[:, :, :], nxt[:, :, :], kt[:, :, :], ALU.not_equal))
                link(nc.vector.tensor_scalar(rs[:, :, :], prev[:, :, :], NEG, None, ALU.mult))
                if not by_src:
                    link(nc.vector.tensor_scalar(re[:, :, :], nxt[:, :, :], NEG, None, ALU.mult))
                    return
                for n, blocks in enumerate(groups):
                    dve.wait_ge(turned, len(groups) + n + 1)
                    a, b = blocks[0] * P, (blocks[-1] + 1) * P
                    link(nc.vector.tensor_tensor(T.last_src[:, a:b], ps[n][:, 0:b - a], m[:, a:b, 2], ALU.mult))

            @block.tensor
            def _(pe):
                for n, blocks in enumerate(groups):
                    for j, b in enumerate(blocks):
                        ins = nc.tensor.transpose(ps[n][:, j * P:(j + 1) * P], m[:, b * P:(b + 1) * P, 3], T.ident[:, :])
                    ins.then_inc(turned, 1)
                if not by_src:
                    return
                pe.wait_ge(dve_at, 2)
                for n, blocks in enumerate(groups):
                    for j, b in enumerate(blocks):
                        ins = nc.tensor.transpose(ps[n][:, j * P:(j + 1) * P], nxt[:, b, :], T.ident[:, :])
                    ins.then_inc(turned, 1)
        S.clear()


def build_max_edges(nc, T, X):
    with ExitStack() as ctx:
        S = Sems(nc, ctx, "mx")
        idx_ready, turned, scanned, back, vals_ready = S("idx_ready"), S("turned"), S("scanned"), S("back"), S("vals_ready")
        hot_ready, picked, added, pool_step = S("hot_ready"), S("picked"), S("added"), S("pool_step")
        cleared, m_in = S("cleared"), S("m_in")
        reset_in = [S(f"reset_in{k}") for k in range(4)]

        def sb(n, shape, dt=F32):
            return ctx.enter_context(nc.sbuf_tensor("mx_" + n, shape, dt))

        def pb(n):
            return ctx.enter_context(nc.psum_tensor("mx_" + n, [P, 512], F32))
        idx = [sb(f"idx{k}", [P, U], U32) for k in range(4)]
        rows = [sb(f"rows{k}", [P, U, D]) for k in range(4)]
        reset = [sb(f"reset{k}", [P, U * P], BF16) for k in range(4)]
        run = [sb(f"run{k}", [P, U * P]) for k in range(2)]
        vals = [sb(f"vals{k}", [P, U * D]) for k in range(2)]
        hot = [sb(f"hot{k}", [P, U, P]) for k in range(2)]
        ps_x, ps_b, ps_n = ([pb(f"ps_{n}{k}") for k in range(2)] for n in "xbn")

        with nc.Block() as block:
            @block.gpsimd
            def _(pool):
                def unit(i, g):
                    pool.wait_ge(idx_ready, i * 4 + (g + 1))
                    wait_again(pool, turned, i * 4 + (g - 3))
                    pool.sem_inc(pool_step, 1)
                    for j in range(U):
                        pool.indirect_dma_start(rows[g][:, j, :], None, X.xpad[:, :],
                                                bass.IndirectOffsetOnAxis(ap=idx[g][:, j:j + 1], axis=0))\
                            .then_inc(T.moves.sems[g][j], 16)
                turns(pool, unit)

            @block.sync
            def _(sp):
                def unit(i, g):
                    wait_again(sp, scanned, i * 4 + (g - 3))
                    sp.dma_start(reset[g][:, :], X.reset_src[bass.ds(i * 4 * U * P + g * U * P, U * P)]
                                 .partition_broadcast(P)).then_inc(reset_in[g], 16)
                turns(sp, unit)

            @block.vector
            def _(dve):
                nc.vector.memset(T.acc[:, :], 0.0).then_inc(cleared, 1)

                def take_index(i, g):
                    T.moves.wait_last(dve, i, g)
                    nc.vector.tensor_copy(idx[g][:, :], T.m_src[:, bass.ds(i * 4 * U + g * U, U), 0]).then_inc(idx_ready, 1)

                def add(i, g):
                    tiles = tiles_of(nc, mybir.EngineType.DVE, T.tile_s, i, g)
                    dve.wait_ge(picked, i * 4 + (g + 1))
                    for j in range(U):
                        wait_again(dve, added, i * 16 + (U * g + j))
                        to = T.acc[:, bass.ds(tiles[j] * ROW, D)]
                        nc.vector.tensor_tensor(to, to, ps_n[g % 2][:, j * D:(j + 1) * D], ALU.add).then_inc(added, 1)

                for g in range(3):
                    take_index(0, g)
                dve.wait_ge(cleared, 1)

                def unit(i, g):
                    if then := near(i, g, 3):
                        take_index(*then)
                    n = i * 4 + g
                    dve.wait_ge(reset_in[g], i * 16 + 16)
                    dve.wait_ge(turned, n + 1)
                    wait_again(dve, back, n - 1)
                    wait_again(dve, scanned, n)
                    first = 0.0 if isinstance(i, int) and n == 0 else run[(g - 1) % 2][:, U * P - 1:U * P]
                    nc.vector.tensor_tensor_scan(run[g % 2][:, :], reset[g][:, :], ps_x[g % 2][:, :], first,
                                                 ALU.add, ALU.max).then_inc(scanned, 1)
                    wait_again(dve, picked, n - 1)
                    nc.vector.tensor_tensor(hot[g % 2][:, :, :], repeat(T.iota1_f[:, :], U),
                                            spread(T.last_src[:, bass.ds(i * 4 * U + g * U, U)], P),
                                            ALU.is_equal).then_inc(hot_ready, 1)
                    if past := near(i, g, -2):
                        add(*past)
                turns(dve, unit)
                add(ITERS - 1, 2)
                add(ITERS - 1, 3)

            @block.scalar
            def _(act):
                act.dma_start(T.m_dst[:, :, :], X.rec_dst.rearrange("(c p) f -> p c f", p=P)).then_inc(m_in, 16)

                def unit(i, g):
                    n = i * 4 + g
                    act.wait_ge(back, n + 1)
                    wait_again(act, picked, n - 1)
                    nc.scalar.copy(vals[g % 2][:, :], ps_b[g % 2][:, :]).then_inc(vals_ready, 1)
                turns(act, unit)
                act.wait_ge(m_in, 16)

            @block.tensor
            def _(pe):
                def turn(i, g):
                    wait_again(pe, scanned, i * 4 + (g - 1))
                    for j in range(U):
                        T.moves.wait(pe, i, g, [j])
                        ins = nc.tensor.transpose(ps_x[g % 2][:, j * P:(j + 1) * P], rows[g][:, j, :], T.ident[:, :])
                    ins.then_inc(turned, 1)

                def turn_back(i, g):
                    pe.wait_ge(scanned, i * 4 + (g + 1))
                    wait_again(pe, vals_ready, i * 4 + (g - 1))
                    for j in range(U):
                        ins = nc.tensor.transpose(ps_b[g % 2][:, j * D:(j + 1) * D], run[g % 2][:, j * P:(j + 1) * P],
                                                  T.ident[:, :])
                    ins.then_inc(back, 1)

                def pick(i, g):
                    pe.wait_ge(vals_ready, i * 4 + (g + 1))
                    pe.wait_ge(hot_ready, i * 4 + (g + 1))
                    wait_again(pe, added, i * 16 + (U * (g - 1)))
                    for j in range(U):
                        ins = nc.tensor.matmul(ps_n[g % 2][:, j * D:(j + 1) * D], hot[g % 2][:, j, :],
                                               vals[g % 2][:, j * D:(j + 1) * D], start=True, stop=True)
                    ins.then_inc(picked, 1)

                turn(0, 0)

                def unit(i, g):
                    if then := near(i, g, 1):
                        turn(*then)
                    turn_back(i, g)
                    if past := near(i, g, -1):
                        pick(*past)
                turns(pe, unit)
                pick(ITERS - 1, 3)
        T.moves.close(lambda g, j: ITERS)
        S.clear()


def build_gat_logits(nc, T, X, name):
    with ExitStack() as ctx:
        S = Sems(nc, ctx, name)
        idx_ready, hot_ready, hot_turned, hot_copied, ar_read, z_ready, pool_step = (S(n) for n in (
            "idx_ready", "hot_ready", "hot_turned", "hot_copied", "ar_read", "z_ready", "pool_step"))
        stored = [S(f"stored{k}") for k in range(4)]

        def sb(n, shape, dt=F32):
            return ctx.enter_context(nc.sbuf_tensor(f"{name}_{n}", shape, dt))

        def pb(n):
            return ctx.enter_context(nc.psum_tensor(f"{name}_{n}", [P, 512], F32))
        idx = [sb(f"idx{k}", [P, U], U32) for k in range(4)]
        rows = [sb(f"rows{k}", [P, U, HEADS, HID + 1]) for k in range(4)]
        hot = [sb(f"hot{k}", [P, U, P]) for k in range(2)]
        hot_t = [sb(f"hot_t{k}", [P, U * P]) for k in range(2)]
        ps_t = [pb(f"ps_t{k}") for k in range(2)]
        ps_a = [pb(f"ps_a{k}") for k in range(2)]

        with nc.Block() as block:
            @block.gpsimd
            def _(pool):
                def unit(i, g):
                    pool.wait_ge(idx_ready, i * 4 + (g + 1))
                    wait_again(pool, z_ready, i * 4 + (g - 3))
                    wait_again(pool, stored[g], i * 16)
                    pool.sem_inc(pool_step, 1)
                    for j in range(U):
                        pool.indirect_dma_start(rows[g][:, j, :, :].rearrange("p h c -> p (h c)"), None, X.hrow[:, :],
                                                bass.IndirectOffsetOnAxis(ap=idx[g][:, j:j + 1], axis=0))\
                            .then_inc(T.moves.sems[g][j], 16)
                turns(pool, unit)

            @block.sync
            def _(sp):
                def unit(i, g):
                    sp.wait_ge(z_ready, i * 4 + (g + 1))
                    sp.dma_start(X.gathered[bass.ds(i * 4 * P + g * P, P), :],
                                 rows[g][:, :, :, :].rearrange("p u h c -> p (u h c)")).then_inc(stored[g], 16)
                turns(sp, unit)
                for g in range(4):
                    sp.wait_ge(stored[g], 16 * ITERS)

            @block.vector
            def _(dve):
                def take_index(i, g):
                    T.moves.wait_last(dve, i, g)
                    nc.vector.tensor_copy(idx[g][:, :], T.m_dst[:, bass.ds(i * 4 * U + g * U, U), 0]).then_inc(idx_ready, 1)

                def make_hot(i, g):
                    wait_again(dve, hot_turned, i * 4 + (g - 1))
                    nc.vector.tensor_tensor(hot[g % 2][:, :, :], repeat(T.iota1_f[:, :], U),
                                            spread(T.m_dst[:, bass.ds(i * 4 * U + g * U, U), 2], P),
                                            ALU.is_equal).then_inc(hot_ready, 1)
                for g in range(3):
                    take_index(0, g)
                make_hot(0, 0)

                def unit(i, g):
                    if then := near(i, g, 3):
                        take_index(*then)
                    if then := near(i, g, 1):
                        make_hot(*then)
                    T.moves.wait(dve, i, g)
                    dve.wait_ge(ar_read, i * 4 + (g + 1))
                    nc.vector.tensor_tensor(T.z[:, bass.ds(i * 4 * U + g * U, U), :], rows[g][:, :, :, HID],
                                            ps_a[g % 2][:, 0:U * HEADS].rearrange("p (u h) -> p u h", h=HEADS), ALU.add)\
                        .then_inc(z_ready, 1)
                turns(dve, unit)

            @block.scalar
            def _(act):
                def unit(i, g):
                    act.wait_ge(hot_turned, i * 4 + (g + 1))
                    wait_again(act, ar_read, i * 4 + (g - 1))
                    nc.scalar.copy(hot_t[g % 2][:, :], ps_t[g % 2][:, :]).then_inc(hot_copied, 1)
                turns(act, unit)

            @block.tensor
            def _(pe):
                def turn_hot(i, g):
                    pe.wait_ge(hot_ready, i * 4 + (g + 1))
                    wait_again(pe, hot_copied, i * 4 + (g - 1))
                    for j in range(U):
                        ins = nc.tensor.transpose(ps_t[g % 2][:, j * P:(j + 1) * P], hot[g % 2][:, j, :], T.ident[:, :])
                    ins.then_inc(hot_turned, 1)
                turn_hot(0, 0)

                def unit(i, g):
                    k = g % 2
                    if then := near(i, g, 1):
                        turn_hot(*then)
                    tiles = tiles_of(nc, mybir.EngineType.PE, T.tile_d, i, g)
                    pe.wait_ge(hot_copied, i * 4 + (g + 1))
                    wait_again(pe, z_ready, i * 4 + (g - 1))
                    for j in range(U):
                        ins = nc.tensor.matmul(ps_a[k][:, j * HEADS:(j + 1) * HEADS], hot_t[k][:, j * P:(j + 1) * P],
                                               T.ar[:, bass.ds(tiles[j] * HEADS, HEADS)], start=True, stop=True)
                    ins.then_inc(ar_read, 1)
                turns(pe, unit)
        T.moves.close(lambda g, j: ITERS)
        S.clear()


def build_gat_softmax(nc, T, X, name):
    with ExitStack() as ctx:
        S = Sems(nc, ctx, name)
        (dve_at, act_at, turned, taken, turned_back, taken_back, row_at, flags_in, stored, loaded, ex_stored, ex_in) = (
            S(n) for n in ("dve_at", "act_at", "turned", "taken", "turned_back", "taken_back", "row_at", "flags_in",
                           "stored", "loaded", "ex_stored", "ex_in"))

        def sb(n, shape, dt=F32):
            return ctx.enter_context(nc.sbuf_tensor(f"{name}_{n}", shape, dt))
        one = T.acc[:, 0:SLEN]
        two = T.acc[:, SLEN:2 * SLEN]
        flags = [sb(f"flags{k}", [P, SLEN], BF16) for k in range(2)]
        edge = [sb(f"edge{k}", [P, 2]) for k in range(2)]
        rowed = [sb(f"rowed{k}", [1, 2 * P]) for k in range(2)]
        handed = [sb(f"handed{k}", [1, 2 * P]) for k in range(2)]
        carry = [sb(f"carry{k}", [P, 1]) for k in range(2)]
        ps = [ctx.enter_context(nc.psum_tensor(f"{name}_ps{k}", [P, 512], F32)) for k in range(4)]
        ps_r = ctx.enter_context(nc.psum_tensor(f"{name}_ps_r", [P, 512], F32))
        ps_c = ctx.enter_context(nc.psum_tensor(f"{name}_ps_c", [P, 512], F32))
        groups = [(h, a, min(4, CBLK - a)) for h in range(HEADS) for a in range(0, CBLK, 4)]
        by_chunk = one[:, :].rearrange("p (h b s) -> p h b s", h=HEADS, b=CBLK)

        def chunked(x, h):
            return x[h].rearrange("(b c p) -> c b p", b=CBLK, c=P)

        def strips(x):
            return x.rearrange("h (b s) -> (h b) s", s=SLEN)

        with nc.Block() as block:
            @block.sync
            def _(sp):
                for k, x in enumerate((X.reset_dst, X.ends_dst)):
                    for h in range(HEADS):
                        sp.dma_start(flags[k][h * STRIPS:(h + 1) * STRIPS, :], x.rearrange("(b s) -> b s", s=SLEN))\
                            .then_inc(flags_in, 16)
                for h in range(HEADS):
                    sp.wait_ge(taken, len(groups) // HEADS * (h + 1))
                    sp.dma_start(chunked(X.logits, h), by_chunk[:, h]).then_inc(stored, 16)
                sp.wait_ge(stored, 16 * HEADS)
                sp.dma_start(one[:, :], strips(X.logits)).then_inc(loaded, 16)
                sp.wait_ge(act_at, 1)
                sp.dma_start(strips(X.exps), two[:, :]).then_inc(ex_stored, 16)
                sp.wait_ge(ex_stored, 16)
                for h in range(HEADS):
                    sp.dma_start(by_chunk[:, h], chunked(X.exps, h)).then_inc(ex_in, 16)

            @block.vector
            def _(dve):
                link = chain(dve, dve_at)
                z = T.z[:, :, :]
                link(nc.vector.scalar_tensor_tensor(out=z, in0=z, scalar=0.2, in1=z, op0=ALU.mult, op1=ALU.max))
                link(nc.vector.tensor_tensor(z, z, spread(T.m_dst[:, :, 1], HEADS), ALU.mult))
                for n, (h, a, m) in enumerate(groups):
                    dve.wait_ge(turned, n + 1)
                    nc.vector.tensor_copy(by_chunk[:, h, a:a + m, :], ps[n % 4][:, 0:m * P].rearrange("c (b p) -> c b p", p=P))\
                        .then_inc(taken, 1)
                dve.wait_ge(flags_in, 16 * 2 * HEADS)
                dve.wait_ge(loaded, 16)
                for k in range(2):
                    way = slice(None, None, -1) if k else slice(None)
                    mine, more = (0, SLEN - 1)[1 - k], two if k else one
                    link(nc.vector.tensor_tensor_scan(two[:, way], flags[k][:, way], more[:, way], LOW, ALU.add, ALU.max))
                    link(nc.vector.tensor_scalar(edge[k][:, 0:1], two[:, mine:mine + 1], 0.0, None, ALU.add))
                    link(nc.vector.tensor_reduce(edge[k][:, 1:2], flags[k][:, :], AX.X, ALU.min))
                    link(nc.vector.tensor_scalar(edge[k][:, 1:2], edge[k][:, 1:2], 0.0, None, ALU.is_lt))
                    dve.wait_ge(row_at, 2 * k + 1)
                    link(nc.vector.tensor_copy(rowed[k][:, 0:P], ps_r[0:1, 0:P]))
                    link(nc.vector.tensor_scalar(rowed[k][:, P:2 * P], ps_r[0:1, P:2 * P], NEG, None, ALU.mult))
                    first = STRIPS - 1 if k else 0
                    link(nc.vector.memset(rowed[k][:, P:2 * P].rearrange("o (h b) -> o h b", h=HEADS)[:, :, first:first + 1], NEG))
                    link(nc.vector.tensor_tensor_scan(handed[k][:, 0:P][:, way], rowed[k][:, P:2 * P][:, way],
                                                      rowed[k][:, 0:P][:, way], LOW, ALU.add, ALU.max))
                    to, frm = (slice(P, 2 * P - 1), slice(1, P)) if k else (slice(P + 1, 2 * P), slice(0, P - 1))
                    link(nc.vector.tensor_copy(handed[k][:, to], handed[k][:, frm]))
                    link(nc.vector.memset(handed[k][:, P:2 * P].rearrange("o (h b) -> o h b", h=HEADS)[:, :, first:first + 1], LOW))
                    dve.wait_ge(row_at, 2 * k + 2)
                    link(nc.vector.tensor_copy(carry[k][:, :], ps_c[:, k:k + 1]))
                    link(nc.vector.tensor_tensor_scan(two[:, way], flags[k][:, way], two[:, way], carry[k][:, :],
                                                      ALU.add, ALU.max))
                link(nc.vector.tensor_tensor(two[:, :], one[:, :], two[:, :], ALU.subtract))
                for n, (h, a, m) in enumerate(groups):
                    dve.wait_ge(turned_back, n + 1)
                    nc.vector.tensor_copy(T.z[:, a * P:(a + m) * P, h], ps[n % 4][:, 0:m * P]).then_inc(taken_back, 1)

            @block.scalar
            def _(act):
                act.wait_ge(dve_at, 27)
                nc.scalar.activation(two[:, :], two[:, :], ACT.Exp).then_inc(act_at, 1)

            @block.tensor
            def _(pe):
                pe.wait_ge(dve_at, 2)
                for n, (h, a, m) in enumerate(groups):
                    if n >= 4:
                        pe.wait_ge(taken, n - 3)
                    for j in range(m):
                        ins = nc.tensor.transpose(ps[n % 4][:, j * P:(j + 1) * P], T.z[:, (a + j) * P:(a + j + 1) * P, h],
                                                  T.ident[:, :])
                    ins.then_inc(turned, 1)
                for k in range(2):
                    pe.wait_ge(dve_at, 2 + 12 * k + 4)
                    for j in range(2):
                        ins = nc.tensor.matmul(ps_r[0:1, j * P:(j + 1) * P], edge[k][:, j:j + 1], T.ident[:, :],
                                               start=True, stop=True)
                    ins.then_inc(row_at, 1)
                    pe.wait_ge(dve_at, 2 + 12 * k + 10)
                    nc.tensor.matmul(ps_c[:, k:k + 1], handed[k][:, P:2 * P], T.ones[0:1, 0:1], start=True, stop=True)\
                        .then_inc(row_at, 1)
                for n, (h, a, m) in enumerate(groups):
                    pe.wait_ge(ex_in, 16 * HEADS)
                    if n < 4:
                        pe.wait_ge(taken, len(groups) - 3 + n)
                    else:
                        pe.wait_ge(taken_back, n - 3)
                    for j in range(m):
                        ins = nc.tensor.transpose(ps[n % 4][:, j * P:(j + 1) * P], by_chunk[:, h, a + j, :], T.ident[:, :])
                    ins.then_inc(turned_back, 1)
        S.clear()


def build_gat_sums(nc, T, X, name):
    with ExitStack() as ctx:
        S = Sems(nc, ctx, name)
        hot_ready, ex_ready, hx_ready, summed, added, cleared = (S(n) for n in (
            "hot_ready", "ex_ready", "hx_ready", "summed", "added", "cleared"))
        rows_in = [S(f"rows_in{k}") for k in range(4)]

        def sb(n, shape, dt=F32):
            return ctx.enter_context(nc.sbuf_tensor(f"{name}_{n}", shape, dt))
        rows = [sb(f"rows{k}", [P, U * HEADS, HID + 1]) for k in range(4)]
        hot = [sb(f"hot{k}", [P, U, P]) for k in range(4)]
        hx = [sb(f"hx{k}", [P, U * HEADS, HID + 1]) for k in range(4)]
        ps = [[ctx.enter_context(nc.psum_tensor(f"{name}_ps{k}{h}", [P, 512], F32)) for h in range(2)] for k in range(4)]

        def exps(i, g):
            return T.z[:, bass.ds(i * 4 * U + g * U, U), :]

        with nc.Block() as block:
            @block.sync
            def _(sp):
                def unit(i, g):
                    wait_again(sp, hx_ready, i * 4 + (g - 3))
                    sp.dma_start(rows[g][:, :, :].rearrange("p u c -> p (u c)"),
                                 X.gathered[bass.ds(i * 4 * P + g * P, P), :]).then_inc(rows_in[g], 16)
                turns(sp, unit)

            @block.vector
            def _(dve):
                nc.vector.memset(T.acc[:, :], 0.0).then_inc(cleared, 1)

                found = []

                def tiles(i, g):
                    if g % 2 == 0:
                        found[:] = tiles_of(nc, mybir.EngineType.DVE, T.tile_d, i, g, 2)
                    dve.wait_ge(summed, i * 4 + (g + 1))
                    return found[g % 2 * U:(g % 2 + 1) * U]

                def add(i, g, j, tiles):
                    wait_again(dve, added, i * 16 + (U * g + j))
                    acc = T.acc[:, bass.ds(tiles[j] * ROW, ROW)]
                    nc.vector.tensor_tensor(acc, acc, ps[g][j // 2][:, (j % 2) * ROW:(j % 2 + 1) * ROW], ALU.add)\
                        .then_inc(added, 1)

                def make_hot(i, g, j):
                    key = T.m_dst[:, bass.ds(i * 4 * U + (g * U + j), 2), 2]
                    return nc.vector.tensor_tensor(hot[g][:, j:j + 2, :], repeat(T.iota1_f[:, :], 2), spread(key, P),
                                                   ALU.is_equal)

                dve.wait_ge(cleared, 1)

                def unit(i, g):
                    past = near(i, g, -2)
                    if past:
                        at = tiles(*past)
                        add(*past, 0, at)
                    make_hot(i, g, 0)
                    if past:
                        add(*past, 1, at)
                    make_hot(i, g, 2).then_inc(hot_ready, 1)
                    if past:
                        add(*past, 2, at)
                        add(*past, 3, at)
                turns(dve, unit)
                for g in (2, 3):
                    at = tiles(ITERS - 1, g)
                    for j in range(U):
                        add(ITERS - 1, g, j, at)

            @block.gpsimd
            def _(pool):
                def unit(i, g):
                    wait_again(pool, summed, i * 4 + (g - 3))
                    pool.wait_ge(rows_in[g], i * 16 + 16)
                    nc.gpsimd.tensor_tensor(hx[g][:, :, 0:HID], rows[g][:, :, 0:HID],
                                            spread(exps(i, g).rearrange("p u h -> p (u h)"), HID), ALU.mult)\
                        .then_inc(hx_ready, 1)
                turns(pool, unit)

            @block.scalar
            def _(act):
                def unit(i, g):
                    wait_again(act, summed, i * 4 + (g - 3))
                    nc.scalar.copy(hx[g][:, :, HID], exps(i, g).rearrange("p u h -> p (u h)")).then_inc(ex_ready, 1)
                turns(act, unit)

            @block.tensor
            def _(pe):
                def unit(i, g):
                    n = i * 4 + g
                    pe.wait_ge(hot_ready, n + 1)
                    pe.wait_ge(ex_ready, n + 1)
                    pe.wait_ge(hx_ready, n + 1)
                    wait_again(pe, added, i * 16 + (4 * (g - 3)))
                    for j in range(U):
                        ins = nc.tensor.matmul(ps[g][j // 2][:, (j % 2) * ROW:(j % 2 + 1) * ROW], hot[g][:, j, :],
                                               hx[g][:, j * HEADS:(j + 1) * HEADS, :].rearrange("p h c -> p (h c)"),
                                               start=True, stop=True)
                    ins.then_inc(summed, 1)
                turns(pe, unit)
        S.clear()


def build_mlp_edges(nc, T, X):
    with ExitStack() as ctx:
        S = Sems(nc, ctx, "ml")
        (idx_ready, hot_ready, hot_turned, hot_copied, own_read, part_ready, in_ready, turned, act_in, hid_ready,
         act_hid, theta_ready, msg_ready, summed, added, pool_step, cleared, widened) = (S(n) for n in (
             "idx_ready", "hot_ready", "hot_turned", "hot_copied", "own_read", "part_ready", "in_ready", "turned",
             "act_in", "hid_ready", "act_hid", "theta_ready", "msg_ready", "summed", "added", "pool_step", "cleared",
             "widened"))
        attr_in = [S(f"attr_in{k}") for k in range(4)]

        def sb(n, shape, dt=F32):
            return ctx.enter_context(nc.sbuf_tensor("ml_" + n, shape, dt))

        def pb(n):
            return ctx.enter_context(nc.psum_tensor("ml_" + n, [P, 512], F32))
        idx = [sb(f"idx{k}", [P, U], U32) for k in range(4)]
        rows = [sb(f"rows{k}", [P, U, D]) for k in range(4)]
        attr = [sb(f"attr{k}", [P, U, D]) for k in range(4)]
        hot = [sb(f"hot{k}", [P, U, P]) for k in range(4)]
        hot_b = [sb(f"hot_b{k}", [P, U, P], BF16) for k in range(4)]
        hot_t = [sb(f"hot_t{k}", [P, U * P]) for k in range(2)]
        sin = sb("sin", [P, U * P])
        hid = [sb(f"hid{k}", [P, U * P]) for k in range(2)]
        msg = sb("msg", [P, U, D])
        ps_t = ctx.enter_context(nc.psum_tensor("ml_ps_t", [P, 2 * U * P], BF16))
        ps_o, ps_f, ps_s = pb("ps_o"), pb("ps_f"), pb("ps_s")
        ps_x = pb("ps_x")
        ps_h = [pb(f"ps_h{k}") for k in range(2)]
        PE_T, DVE_T = mybir.EngineType.PE, mybir.EngineType.DVE

        with nc.Block() as block:
            @block.gpsimd
            def _(pool):
                def unit(i, g):
                    pool.wait_ge(idx_ready, i * 4 + (g + 1))
                    wait_again(pool, msg_ready, i * 4 + (g - 3))
                    pool.sem_inc(pool_step, 1)
                    for j in range(U):
                        pool.indirect_dma_start(rows[g][:, j, :], None, X.h2row[:, :],
                                                bass.IndirectOffsetOnAxis(ap=idx[g][:, j:j + 1], axis=0))\
                            .then_inc(T.moves.sems[g][j], 16)
                turns(pool, unit)

            @block.sync
            def _(sp):
                def unit(i, g):
                    wait_again(sp, turned, i * 4 + (g - 3))
                    a = X.rec_src[bass.ds(i * 4 * U * P + g * U * P, U * P), :]
                    sp.dma_start(attr[g][:, :, :], a.rearrange("(j e) f -> e j f", e=P)[:, :, 0:D]).then_inc(attr_in[g], 16)
                turns(sp, unit)

            @block.vector
            def _(dve):
                nc.vector.memset(T.acc[:, :], 0.0).then_inc(cleared, 1)

                def take_index(i, g):
                    T.moves.wait_last(dve, i, g)
                    nc.vector.tensor_copy(idx[g][:, :], T.m_src[:, bass.ds(i * 4 * U + g * U, U), 0]).then_inc(idx_ready, 1)

                def make_hot(i, g):
                    wait_again(dve, hot_turned, i * 4 + (g - 3))
                    wait_again(dve, widened, i * 4 + (g - 3))
                    nc.vector.tensor_tensor(hot_b[g][:, :, :], repeat(T.iota1_f[:, :], U),
                                            spread(T.m_src[:, bass.ds(i * 4 * U + g * U, U), 2], P),
                                            ALU.is_equal).then_inc(hot_ready, 1)

                def sum_input(i, g):
                    T.moves.wait(dve, i, g)
                    dve.wait_ge(attr_in[g], i * 16 + 16)
                    nc.vector.tensor_tensor(attr[g][:, :, :], attr[g][:, :, :], rows[g][:, :, :], ALU.add)\
                        .then_inc(part_ready, 1)
                    dve.wait_ge(own_read, i * 4 + (g + 1))
                    dve.wait_ge(part_ready, i * 4 + (g + 1))
                    nc.vector.tensor_tensor(attr[g][:, :, :], attr[g][:, :, :],
                                            ps_o[:, :].rearrange("p (j f) -> p j f", f=D), ALU.add).then_inc(in_ready, 1)

                def message(i, g):
                    dve.wait_ge(theta_ready, i * 4 + (g + 1))
                    wait_again(dve, summed, i * 4 + g)
                    nc.vector.tensor_tensor(msg[:, :, :], rows[g][:, :, :],
                                            ps_f[:, :].rearrange("p (j f) -> p j f", f=D), ALU.mult).then_inc(msg_ready, 1)

                def add(i, g):
                    tiles = tiles_of(nc, DVE_T, T.tile_s, i, g)
                    dve.wait_ge(summed, i * 4 + (g + 1))
                    for j in range(U):
                        wait_again(dve, added, i * 16 + (U * g + j))
                        to = T.acc[:, bass.ds(tiles[j] * ROW, D)]
                        nc.vector.tensor_tensor(to, to, ps_s[:, j * D:(j + 1) * D], ALU.add).then_inc(added, 1)

                for g in range(3):
                    take_index(0, g)
                dve.wait_ge(cleared, 1)
                for g in range(3):
                    make_hot(0, g)
                sum_input(0, 0)

                def unit(i, g):
                    if then := near(i, g, 3):
                        take_index(*then)
                    if then := near(i, g, 1):
                        sum_input(*then)
                    if then := near(i, g, 3):
                        make_hot(*then)
                    if past := near(i, g, -1):
                        add(*past)
                    message(i, g)
                turns(dve, unit)
                add(ITERS - 1, 3)

            @block.scalar
            def _(act):
                def copy_hot(i, g):
                    act.wait_ge(hot_turned, i * 4 + (g + 1))
                    wait_again(act, own_read, i * 4 + (g - 1))
                    nc.scalar.copy(hot_t[g % 2][:, :], ps_t[:, 0:U * P]).then_inc(hot_copied, 1)

                def widen(i, g):
                    act.wait_ge(hot_ready, i * 4 + (g + 1))
                    wait_again(act, summed, i * 4 + (g - 3))
                    nc.scalar.copy(hot[g][:, :, :], hot_b[g][:, :, :]).then_inc(widened, 1)
                copy_hot(0, 0)
                copy_hot(0, 1)
                widen(0, 0)

                def unit(i, g):
                    n = i * 4 + g
                    act.wait_ge(turned, n + 1)
                    wait_again(act, hid_ready, 2 * n)
                    nc.scalar.activation(sin[:, :], ps_x[:, :], ACT.Silu).then_inc(act_in, 1)
                    if then := near(i, g, 2):
                        copy_hot(*then)
                    for h in range(2):
                        act.wait_ge(hid_ready, 2 * n + (h + 1))
                        wait_again(act, theta_ready, n)
                        nc.scalar.activation(hid[h][:, :], ps_h[h][:, :], ACT.Silu, bias=T.b1c[:, h:h + 1])\
                            .then_inc(act_hid, 1)
                    if then := near(i, g, 1):
                        widen(*then)
                turns(act, unit)

            @block.tensor
            def _(pe):
                def turn_hot(i, g):
                    pe.wait_ge(hot_ready, i * 4 + (g + 1))
                    wait_again(pe, hot_copied, i * 4 + g)
                    for j in range(U):
                        ins = nc.tensor.transpose(ps_t[:, j * P:(j + 1) * P], hot_b[g][:, j, :], T.ident_b[:, :])
                    ins.then_inc(hot_turned, 1)

                def read_own(i, g):
                    tiles = tiles_of(nc, PE_T, T.tile_s, i, g)
                    pe.wait_ge(hot_copied, i * 4 + (g + 1))
                    wait_again(pe, in_ready, i * 4 + g)
                    for j in range(U):
                        ins = nc.tensor.matmul(ps_o[:, j * D:(j + 1) * D], hot_t[g % 2][:, j * P:(j + 1) * P],
                                               T.nodes[:, bass.ds(tiles[j] * D, D)], start=True, stop=True)
                    ins.then_inc(own_read, 1)

                def turn_input(i, g):
                    pe.wait_ge(in_ready, i * 4 + (g + 1))
                    wait_again(pe, act_in, i * 4 + g)
                    for j in range(U):
                        ins = nc.tensor.transpose(ps_x[:, j * P:(j + 1) * P], attr[g][:, j, :], T.ident[:, :])
                    ins.then_inc(turned, 1)

                def hidden(i, g):
                    pe.wait_ge(act_in, i * 4 + (g + 1))
                    for h in range(2):
                        wait_again(pe, act_hid, 2 * (i * 4 + g) + (h - 1))
                        nc.tensor.matmul(ps_h[h][:, :], T.w1[:, h * P:(h + 1) * P], sin[:, :], start=True, stop=True)\
                            .then_inc(hid_ready, 1)

                def theta(i, g):
                    pe.wait_ge(act_hid, 2 * (i * 4 + g) + 2)
                    wait_again(pe, msg_ready, i * 4 + g)
                    nc.tensor.matmul(ps_f[:, :], T.ones_b[0:3, :], T.b2_parts[0:3, :], start=True, stop=False,
                                     skip_group_check=True)
                    for j in range(U):
                        part = ps_f[:, j * D:(j + 1) * D]
                        for h in range(2):
                            ins = nc.tensor.matmul(part, hid[h][:, j * P:(j + 1) * P], T.w2[:, h, :], start=False, stop=(h == 1),
                                                   skip_group_check=True)
                    ins.then_inc(theta_ready, 1)

                def sum_up(i, g):
                    pe.wait_ge(msg_ready, i * 4 + (g + 1))
                    pe.wait_ge(widened, i * 4 + (g + 1))
                    wait_again(pe, added, i * 16 + U * g)
                    for j in range(U):
                        ins = nc.tensor.matmul(ps_s[:, j * D:(j + 1) * D], hot[g][:, j, :], msg[:, j, :], start=True, stop=True)
                    ins.then_inc(summed, 1)
                turn_hot(0, 0)
                turn_hot(0, 1)
                read_own(0, 0)

                def unit(i, g):
                    turn_input(i, g)
                    if then := near(i, g, 1):
                        read_own(*then)
                    if then := near(i, g, 2):
                        turn_hot(*then)
                    hidden(i, g)
                    if past := near(i, g, -1):
                        sum_up(*past)
                    theta(i, g)
                turns(pe, unit)
                sum_up(ITERS - 1, 3)
        T.moves.close(lambda g, j: ITERS)
        S.clear()


def build_gcn_edges(nc, T, X):
    with ExitStack() as ctx:
        S = Sems(nc, ctx, "gc")
        idx_ready, hot_ready, summed, added, pool_step, cleared = (
            S("idx_ready"), S("hot_ready"), S("summed"), S("added"), S("pool_step"), S("cleared"))
        idx = [ctx.enter_context(nc.sbuf_tensor(f"gc_idx{k}", [P, U], U32)) for k in range(4)]
        rows = [ctx.enter_context(nc.sbuf_tensor(f"gc_rows{k}", [P, U, D], F32)) for k in range(4)]
        hot = [ctx.enter_context(nc.sbuf_tensor(f"gc_hot{k}", [P, U, P], F32)) for k in range(2)]
        ps = [ctx.enter_context(nc.psum_tensor(f"gc_ps{k}", [P, 512], F32)) for k in range(2)]

        with nc.Block() as block:
            @block.gpsimd
            def _(pool):
                def unit(i, g):
                    pool.wait_ge(idx_ready, i * 4 + (g + 1))
                    wait_again(pool, summed, i * 4 + (g - 3))
                    pool.sem_inc(pool_step, 1)
                    for j in range(U):
                        pool.indirect_dma_start(rows[g][:, j, :], None, X.h3row[:, :],
                                                bass.IndirectOffsetOnAxis(ap=idx[g][:, j:j + 1], axis=0))\
                            .then_inc(T.moves.sems[g][j], 16)
                turns(pool, unit)

            @block.vector
            def _(dve):
                nc.vector.memset(T.acc[:, :], 0.0).then_inc(cleared, 1)

                def take_index(i, g):
                    T.moves.wait_last(dve, i, g)
                    nc.vector.tensor_copy(idx[g][:, :], T.m_src[:, bass.ds(i * 4 * U + g * U, U), 0]).then_inc(idx_ready, 1)

                def add(i, g):
                    tiles = tiles_of(nc, mybir.EngineType.DVE, T.tile_s, i, g)
                    dve.wait_ge(summed, i * 4 + (g + 1))
                    for j in range(U):
                        wait_again(dve, added, i * 16 + (U * g + j))
                        to = T.acc[:, bass.ds(tiles[j] * ROW, D)]
                        nc.vector.tensor_tensor(to, to, ps[g % 2][:, j * D:(j + 1) * D], ALU.add).then_inc(added, 1)

                for g in range(3):
                    take_index(0, g)
                dve.wait_ge(cleared, 1)

                def unit(i, g):
                    if then := near(i, g, 3):
                        take_index(*then)
                    wait_again(dve, summed, i * 4 + (g - 1))
                    for j in range(U):
                        c = i * 4 * U + (g * U + j)
                        ins = nc.vector.tensor_scalar(hot[g % 2][:, j, :], T.iota1_f[:, :], T.m_src[:, bass.ds(c, 1), 2],
                                                      T.m_src[:, bass.ds(c, 1), 1], ALU.is_equal, ALU.mult)
                    ins.then_inc(hot_ready, 1)
                    if past := near(i, g, -1):
                        add(*past)
                turns(dve, unit)
                add(ITERS - 1, 3)

            @block.tensor
            def _(pe):
                def unit(i, g):
                    pe.wait_ge(hot_ready, i * 4 + (g + 1))
                    wait_again(pe, added, i * 16 + U * (g - 1))
                    for j in range(U):
                        T.moves.wait(pe, i, g, [j])
                        ins = nc.tensor.matmul(ps[g % 2][:, j * D:(j + 1) * D], hot[g % 2][:, j, :], rows[g][:, j, :],
                                               start=True, stop=True)
                    ins.then_inc(summed, 1)
                turns(pe, unit)
        T.moves.close(lambda g, j: ITERS)
        S.clear()


W = 14
NTURN = NT // W
assert NT % W == 0 and W % 2 == 0
WROW = HEADS * (HID + 1)
WCAT = WROW + HEADS


def build_weights(nc, T, X):
    with ExitStack() as ctx:
        S = Sems(nc, ctx, "wt")
        loaded, turned, dve_at = S("loaded"), S("turned"), S("dve_at")
        w0 = ctx.enter_context(nc.sbuf_tensor("wt_w0", [P, 2 * D], F32))
        w = [ctx.enter_context(nc.sbuf_tensor(f"wt_gat{k}", [P, D], F32)) for k in range(2)]
        att = [ctx.enter_context(nc.sbuf_tensor(f"wt_att{k}", [P, D], F32)) for k in range(4)]
        prod = ctx.enter_context(nc.sbuf_tensor("wt_prod", [P, D], F32))
        dots = ctx.enter_context(nc.sbuf_tensor("wt_dots", [P, HEADS], F32))
        b2w = ctx.enter_context(nc.sbuf_tensor("wt_b2w", [3, 3, D], F32))
        b2p = ctx.enter_context(nc.sbuf_tensor("wt_b2p", [3, D], BF16))
        ps = ctx.enter_context(nc.psum_tensor("wt_ps", [P, 512], F32))
        loads = [(w0[:, :], X.L0_gnn_W), (w[0][:, :], X.L1_gnn_W1), (w[1][:, :], X.L1_gnn_W2),
                 (T.w1[:, :], X.L2_gnn_W1), (T.w2[:, :, :], X.L2_gnn_W2.rearrange("(h k) n -> k h n", h=2)),
                 (T.wt[:, :], X.L2_gnn_Wt), (T.w3[:, :], X.L3_gnn_W), (T.wres[:, :], X.L3_gnn_Wres),
                 (T.b1c[:, :], X.L2_gnn_b1.rearrange("(h k) -> k h", h=2))]
        loads += [(t[0:1, :], a.unsqueeze(0)) for t, a in (
            (T.b0r, X.L0_gnn_b), (T.btr, X.L2_gnn_bt), (T.b3r, X.L3_gnn_b), (T.bresr, X.L3_gnn_bres))]
        loads += [(t[:, :], a.partition_broadcast(P)) for t, a in (
            (T.bg1, X.L1_gnn_b1), (T.bg2, X.L1_gnn_b2), (T.gamma, X.L2_gnn_ln_gamma), (T.beta, X.L2_gnn_ln_beta))]
        loads += [(t[:, :], a.rearrange("h c -> (h c)").partition_broadcast(P)) for t, a in zip(
            att, (X.L1_gnn_att_l1, X.L1_gnn_att_r1, X.L1_gnn_att_l2, X.L1_gnn_att_r2))]
        loads.append((b2w[:, 0, :], X.L2_gnn_b2.partition_broadcast(3)))
        with nc.Block() as block:
            @block.sync
            def _(sp):
                with nc.allow_non_contiguous_dma(reason="256 biases, once"):
                    for to, frm in loads:
                        sp.dma_start(to, frm).then_inc(loaded, 16)

            @block.vector
            def _(dve):
                dve.wait_ge(loaded, 16 * len(loads))
                link = chain(dve, dve_at)
                link(nc.vector.memset(T.acc[:, 0:1], 0.0))
                for k, cat in enumerate((T.cat1, T.cat2)):
                    wide = cat[:, 0:WROW].rearrange("p (h c) -> p h c", h=HEADS)
                    link(nc.vector.tensor_copy(wide[:, :, 0:HID], w[k][:, :].rearrange("p (h c) -> p h c", h=HEADS)))
                    for side in range(2):
                        link(nc.vector.tensor_tensor(prod[:, :], w[k][:, :], att[2 * k + side][:, :], ALU.mult))
                        link(nc.vector.tensor_reduce(dots[:, :], prod[:, :].rearrange("p (h c) -> p h c", h=HEADS),
                                                     AX.X, ALU.add))
                        to = wide[:, :, HID] if side == 0 else cat[:, WROW:WCAT]
                        link(nc.vector.tensor_copy(to, dots[:, :]))
                rest = b2w[:, 0, :]
                for k in range(3):
                    link(nc.vector.tensor_copy(b2p[:, :], rest))
                    link(nc.vector.tensor_copy(b2w[:, 1, :], b2p[:, :]))
                    link(nc.vector.tensor_tensor(rest, rest, b2w[:, 1, :], ALU.subtract))
                    if k == 0:
                        link(nc.vector.tensor_scalar(b2w[:, 2, :], b2w[:, 1, :], T.ident[0:3, 0:1], None, ALU.mult))
                    else:
                        link(nc.vector.scalar_tensor_tensor(out=b2w[:, 2, :], in0=b2w[:, 1, :], scalar=T.ident[0:3, k:k + 1],
                                                            in1=b2w[:, 2, :], op0=ALU.mult, op1=ALU.add))
                link(nc.vector.tensor_copy(T.b2_parts[:, :].rearrange("k (j f) -> k j f", f=D), repeat(b2w[:, 2, :], U)))
                dve.wait_ge(turned, 1)
                link(nc.vector.tensor_copy(T.w0t[:, :], ps[:, 0:2 * D]))

            @block.tensor
            def _(pe):
                pe.wait_ge(loaded, 16 * len(loads))
                for h in range(2):
                    ins = nc.tensor.transpose(ps[:, h * D:(h + 1) * D], w0[:, h * D:(h + 1) * D], T.ident[:, :])
                ins.then_inc(turned, 1)
        S.clear()


def build_nodes(nc, T, X, kind):
    resid = {"sage": X.xpad, "gat_mid": None, "gat_end": X.x1, "mlp": X.x2, "gcn": X.x3}[kind]
    weight, bias = {"sage": (T.w0t, T.b0r), "gat_mid": (T.cat2, None), "gat_end": (None, None),
                    "mlp": (T.wt, T.btr), "gcn": (T.wres, T.bresr)}[kind]
    gat = kind.startswith("gat")
    width = WCAT if kind == "gat_mid" else D
    with ExitStack() as ctx:
        S = Sems(nc, ctx, "n" + kind)
        taken, scaled, turned, copied, multiplied, plus, noted, told, silued, inv, joined = (S(n) for n in (
            "taken", "scaled", "turned", "copied", "multiplied", "plus", "noted", "told", "silued", "inv", "joined"))
        resid_in = [S(f"resid_in{k}") for k in range(W)]
        stored = [S(f"stored{k}") for k in range(W)]

        def sb(n, shape, dt=F32):
            return ctx.enter_context(nc.sbuf_tensor(f"n{kind}_{n}", shape, dt))
        xr = [sb(f"xr{k}", [P, D]) for k in range(W) if resid is not None]
        pre = [sb(f"pre{k}", [P, D]) for k in range(2)]
        v = [sb(f"v{k}", [P, D]) for k in range(W)]
        vt = [sb(f"vt{k}", [P, 2 * P]) for k in range(2)]
        mid = [sb(f"mid{k}", [P, D]) for k in range(2)]
        hb = [sb(f"hb{k}", [P, WROW]) for k in range(W) if kind == "gat_mid"]
        rs = sb("rs", [P, NT * HEADS])
        pa = [ctx.enter_context(nc.psum_tensor(f"n{kind}_pa{k}", [P, 512], F32)) for k in range(2)]
        py = [ctx.enter_context(nc.psum_tensor(f"n{kind}_py{k}", [P, 512], F32)) for k in range(2)]

        def loop(eng, step):
            turns(eng, step, depth=W, count=NTURN)

        with nc.Block() as block:
            @block.sync
            def _(sp):
                if resid is not None:
                    def load(i, k):
                        wait_again(sp, noted if width == D else taken, i * W + (k + 1 - W))
                        sp.dma_start(xr[k][:, :], resid[bass.ds(i * W * P + k * P, P), :]).then_inc(resid_in[k], 16)
                    loop(sp, load)
                if kind == "gat_mid":
                    def store(i, k):
                        sp.wait_ge(plus, i * W + (k + 1))
                        sp.dma_start(X.hrow[bass.ds(i * W * P + k * P, P), :], hb[k][:, :]).then_inc(stored[k], 16)
                    loop(sp, store)
                    for k in range(W):
                        sp.wait_ge(stored[k], 16 * NTURN)

            @block.vector
            def _(dve):
                if gat:
                    sums = T.acc[:, 0:NT * ROW].rearrange("p (t c) -> p t c", c=HID + 1)[:, :, HID]
                    nc.vector.tensor_scalar(rs[:, :], sums, 1e-16, None, ALU.add).then_inc(inv, 1)
                    dve.wait_ge(inv, 1)
                    nc.vector.reciprocal(rs[:, :], rs[:, :]).then_inc(inv, 1)
                    dve.wait_ge(inv, 2)

                def before(i, k):
                    n = i * W + k
                    acc = T.acc[:, bass.ds(i * W * ROW + k * ROW, ROW)]
                    if gat:
                        wait_again(dve, taken, n - 1)
                        nc.vector.tensor_tensor(pre[k % 2][:, :].rearrange("p (h c) -> p h c", h=HEADS),
                                                acc.rearrange("p (h c) -> p h c", h=HEADS)[:, :, 0:HID],
                                                spread(rs[:, bass.ds(i * W * HEADS + k * HEADS, HEADS)], HID), ALU.mult)\
                            .then_inc(scaled, 1)
                        dve.wait_ge(scaled, n + 1)
                        wait_again(dve, turned if weight is not None else joined, i * W + (k + 1 - W))
                        nc.vector.tensor_tensor(v[k][:, :], pre[k % 2][:, :], (T.bg1 if kind == "gat_mid" else T.bg2)[:, :],
                                                ALU.add).then_inc(taken, 1)
                    elif kind == "sage":
                        wait_again(dve, turned, i * W + (k + 1 - W))
                        nc.vector.tensor_copy(v[k][:, :], acc[:, 0:D]).then_inc(taken, 1)
                    elif kind == "mlp":
                        wait_again(dve, silued, n - 1)
                        nc.vector.tensor_tensor(pre[k % 2][:, :], acc[:, 0:D], T.nodes[:, bass.ds(i * W * D + k * D, D)], ALU.add)\
                            .then_inc(taken, 1)
                    else:
                        wait_again(dve, turned, i * W + (k + 1 - W))
                        wait_again(dve, plus, i * W + (k + 1 - W))
                        nc.vector.tensor_scalar(v[k][:, :], acc[:, 0:D], 0.0, None, ALU.max).then_inc(taken, 1)

                def after(i, k):
                    n = i * W + k
                    if weight is not None:
                        dve.wait_ge(multiplied, n + 1)
                    if kind == "gat_mid":
                        wait_again(dve, stored[k], 16 * i)
                        nc.vector.tensor_copy(hb[k][:, :], py[k % 2][:, 0:WROW]).then_inc(plus, 1)
                        nc.vector.tensor_copy(T.ar[:, bass.ds(i * W * HEADS + k * HEADS, HEADS)], py[k % 2][:, WROW:WCAT])\
                            .then_inc(noted, 1)
                        return
                    dve.wait_ge(resid_in[k], i * 16 + 16)
                    to = T.nodes[:, bass.ds(i * W * D + k * D, D)]
                    if kind == "gcn":
                        wait_again(dve, joined, n - 1)
                        nc.vector.tensor_tensor(mid[k % 2][:, :], v[k][:, :], py[k % 2][:, 0:D], ALU.add).then_inc(plus, 1)
                        dve.wait_ge(plus, n + 1)
                        nc.vector.tensor_tensor(to, mid[k % 2][:, :], xr[k][:, :], ALU.add).then_inc(joined, 1)
                    elif kind == "gat_end":
                        dve.wait_ge(taken, n + 1)
                        nc.vector.tensor_tensor(to, v[k][:, :], xr[k][:, :], ALU.add).then_inc(joined, 1)
                    else:
                        nc.vector.tensor_tensor(to, xr[k][:, :], py[k % 2][:, 0:D], ALU.add).then_inc(joined, 1)
                    dve.wait_ge(joined, n + 1)
                    dve.sem_inc(told, 1)
                    nc.vector.bn_stats(T.stats[:, bass.ds(i * 6 * W + 6 * k, 6)], to).then_inc(noted, 1)

                before(0, 0)
                before(0, 1)

                def step(i, k):
                    if then := near(i, k, 2, W, NTURN):
                        before(*then)
                    after(i, k)
                loop(dve, step)

            @block.scalar
            def _(act):
                if weight is None:
                    return

                def step(i, k):
                    n = i * W + k
                    if kind == "mlp":
                        act.wait_ge(taken, n + 1)
                        wait_again(act, turned, n - 1)
                        nc.scalar.activation(v[k][:, :], pre[k % 2][:, :], ACT.Silu).then_inc(silued, 1)
                    act.wait_ge(turned, n + 1)
                    wait_again(act, multiplied, n - 1)
                    w = 2 * P if kind == "sage" else P
                    nc.scalar.copy(vt[k % 2][:, 0:w], pa[k % 2][:, 0:w]).then_inc(copied, 1)
                loop(act, step)

            @block.tensor
            def _(pe):
                if weight is None:
                    return

                def turn(i, k):
                    n = i * W + k
                    pe.wait_ge(silued if kind == "mlp" else taken, n + 1)
                    wait_again(pe, copied, n - 1)
                    if kind == "sage":
                        pe.wait_ge(resid_in[k], i * 16 + 16)
                        nc.tensor.transpose(pa[k % 2][:, P:2 * P], xr[k][:, :], T.ident[:, :])
                    nc.tensor.transpose(pa[k % 2][:, 0:P], v[k][:, :], T.ident[:, :]).then_inc(turned, 1)
                turn(0, 0)

                def step(i, k):
                    n = i * W + k
                    if then := near(i, k, 1, W, NTURN):
                        turn(*then)
                    pe.wait_ge(copied, n + 1)
                    wait_again(pe, noted, n - 1)
                    y = py[k % 2][:, 0:width]
                    if bias is not None:
                        nc.tensor.matmul(y, T.ones[0:1, :], bias[0:1, :], start=True, stop=False)
                    if kind == "sage":
                        nc.tensor.matmul(y, vt[k % 2][:, P:2 * P], weight[:, 0:D], start=False, stop=False)
                        ins = nc.tensor.matmul(y, vt[k % 2][:, 0:P], weight[:, D:2 * D], start=False, stop=True)
                    else:
                        ins = nc.tensor.matmul(y, vt[k % 2][:, 0:P], weight[:, 0:width], start=bias is None, stop=True)
                    ins.then_inc(multiplied, 1)
                loop(pe, step)
        S.clear()


def build_norm(nc, T, X, kind):
    store = {"x1": X.x1, "x2": X.x2, "h2": X.h2row, "x3": X.x3, "out": X.out}[kind]
    weight, bias, width, rows = {"x1": (T.cat1, None, WCAT, X.hrow), "x3": (T.w3, T.b3r, D, X.h3row)}\
        .get(kind, (None, None, 0, None))
    wrow = min(width, WROW)
    with ExitStack() as ctx:
        S = Sems(nc, ctx, "m" + kind)
        step_at, rooted, normed, turned, copied, multiplied, out_ready, noted, told, times, plus = (S(n) for n in (
            "step_at", "rooted", "normed", "turned", "copied", "multiplied", "out_ready", "noted", "told", "times", "plus"))
        stored = [S(f"stored{k}") for k in range(W)]
        sent = [S(f"sent{k}") for k in range(W)]

        def sb(n, shape, dt=F32):
            return ctx.enter_context(nc.sbuf_tensor(f"m{kind}_{n}", shape, dt))
        dev = sb("dev", [P, NT])
        std = sb("std", [P, NT])
        mean = sb("mean", [P, NT])
        apart = sb("apart", [P, NT])
        ob = [sb(f"ob{k}", [P, D]) for k in range(W)]
        raw = [sb(f"raw{k}", [P, D]) for k in range(2)]
        mul = [sb(f"mul{k}", [P, D]) for k in range(2)]
        vt = [sb(f"vt{k}", [P, P]) for k in range(2)]
        hb = [sb(f"hb{k}", [P, WROW]) for k in range(W) if weight is not None]
        pa = [ctx.enter_context(nc.psum_tensor(f"m{kind}_pa{k}", [P, 512], F32)) for k in range(2)]
        py = [ctx.enter_context(nc.psum_tensor(f"m{kind}_py{k}", [P, 512], F32)) for k in range(2)]
        LAST = N - (NT - 1) * P

        def loop(eng, step):
            turns(eng, step, depth=W, count=NTURN)

        with nc.Block() as block:
            @block.sync
            def _(sp):
                def save(i, k):
                    sp.wait_ge(normed, i * W + (k + 1))
                    if kind == "out" and isinstance(i, int) and i == NTURN - 1 and k == W - 1:
                        sp.dma_start(store[N - LAST:N, :], ob[k][0:LAST, :]).then_inc(stored[k], 16)
                    else:
                        sp.dma_start(store[bass.ds(i * W * P + k * P, P), :], ob[k][:, :]).then_inc(stored[k], 16)
                loop(sp, save)
                for k in range(W):
                    sp.wait_ge(stored[k], 16 * NTURN)

            @block.scalar
            def _(act):
                act.wait_ge(step_at, 7)
                nc.scalar.activation(std[:, :], dev[:, :], ACT.Sqrt).then_inc(rooted, 1)
                if weight is None:
                    return

                def step(i, k):
                    n = i * W + k
                    act.wait_ge(turned, n + 1)
                    wait_again(act, multiplied, n - 1)
                    nc.scalar.copy(vt[k % 2][:, :], pa[k % 2][:, 0:P]).then_inc(copied, 1)
                    if past := near(i, k, -3, W, NTURN):
                        send(*past)

                def send(i, k):
                    act.wait_ge(out_ready, i * W + (k + 1))
                    act.dma_start(rows[bass.ds(i * W * P + k * P, P), :], hb[k][:, 0:wrow]).then_inc(sent[k], 16)
                loop(act, step)
                for k in range(W - 3, W):
                    send(NTURN - 1, k)
                for k in range(W):
                    act.wait_ge(sent[k], 16 * NTURN)

            @block.vector
            def _(dve):
                st = T.stats[:, :].rearrange("p (t s) -> p t s", s=6)
                link = chain(dve, step_at)
                link(nc.vector.tensor_tensor(mean[:, :], st[:, :, 1], st[:, :, 4], ALU.add))
                link(nc.vector.tensor_scalar(mean[:, :], mean[:, :], 0.5, None, ALU.mult))
                link(nc.vector.tensor_tensor(apart[:, :], st[:, :, 1], st[:, :, 4], ALU.subtract))
                link(nc.vector.tensor_tensor(apart[:, :], apart[:, :], apart[:, :], ALU.mult))
                link(nc.vector.tensor_scalar(apart[:, :], apart[:, :], 0.25, LN_EPS, ALU.mult, ALU.add))
                link(nc.vector.tensor_tensor(dev[:, :], st[:, :, 2], st[:, :, 5], ALU.add))
                link(nc.vector.scalar_tensor_tensor(out=dev[:, :], in0=dev[:, :], scalar=1.0 / D, in1=apart[:, :],
                                                    op0=ALU.mult, op1=ALU.add))
                dve.wait_ge(rooted, 1)
                link(nc.vector.reciprocal(dev[:, :], std[:, :]))

                def norm(i, k):
                    n = i * W + k
                    here = T.nodes[:, bass.ds(i * W * D + k * D, D)]
                    m, d = mean[:, bass.ds(i * W + k, 1)], dev[:, bass.ds(i * W + k, 1)]
                    wait_again(dve, stored[k], 16 * i)
                    if kind == "h2":
                        wait_again(dve, times, n - 1)
                        nc.vector.tensor_scalar(raw[k % 2][:, :], here, m, d, ALU.subtract, ALU.mult).then_inc(out_ready, 1)
                        dve.wait_ge(out_ready, n + 1)
                        wait_again(dve, plus, n - 1)
                        nc.vector.tensor_tensor(mul[k % 2][:, :], raw[k % 2][:, :], T.gamma[:, :], ALU.mult).then_inc(times, 1)
                        dve.wait_ge(times, n + 1)
                        nc.vector.tensor_tensor(ob[k][:, :], mul[k % 2][:, :], T.beta[:, :], ALU.add).then_inc(normed, 1)
                    else:
                        if weight is not None:
                            wait_again(dve, turned, n - 1)
                        if kind == "x2":
                            wait_again(dve, plus, n - 1)
                            wait_again(dve, noted, n - 1)
                        nc.vector.tensor_scalar(ob[k][:, :], here, m, d, ALU.subtract, ALU.mult).then_inc(normed, 1)
                    if kind in ("x2", "h2"):
                        dve.wait_ge(normed, n + 1)
                        nc.vector.tensor_scalar(here, ob[k][:, :], 0.0, None, ALU.add).then_inc(plus, 1)
                    if kind == "x2":
                        dve.sem_inc(told, 1)
                        nc.vector.bn_stats(T.stats[:, bass.ds(i * 6 * W + 6 * k, 6)], ob[k][:, :]).then_inc(noted, 1)

                def give(i, k):
                    n = i * W + k
                    dve.wait_ge(multiplied, n + 1)
                    wait_again(dve, sent[k], 16 * i)
                    nc.vector.tensor_copy(hb[k][:, 0:wrow], py[k % 2][:, 0:wrow]).then_inc(out_ready, 1)
                    if kind == "x1":
                        nc.vector.tensor_copy(T.ar[:, bass.ds(i * W * HEADS + k * HEADS, HEADS)], py[k % 2][:, WROW:WCAT])\
                            .then_inc(noted, 1)

                def step(i, k):
                    norm(i, k)
                    if weight is not None:
                        if past := near(i, k, -2, W, NTURN):
                            give(*past)
                loop(dve, step)
                if weight is not None:
                    give(NTURN - 1, W - 2)
                    give(NTURN - 1, W - 1)

            @block.tensor
            def _(pe):
                if weight is None:
                    return

                def turn(i, k):
                    n = i * W + k
                    pe.wait_ge(normed, n + 1)
                    wait_again(pe, copied, n - 1)
                    nc.tensor.transpose(pa[k % 2][:, 0:P], ob[k][:, :], T.ident[:, :]).then_inc(turned, 1)
                turn(0, 0)

                def step(i, k):
                    n = i * W + k
                    if then := near(i, k, 1, W, NTURN):
                        turn(*then)
                    pe.wait_ge(copied, n + 1)
                    wait_again(pe, noted if kind == "x1" else out_ready, n - 1)
                    y = py[k % 2][:, 0:width]
                    if bias is not None:
                        nc.tensor.matmul(y, T.ones[0:1, :], bias[0:1, :], start=True, stop=False)
                    nc.tensor.matmul(y, vt[k % 2][:, :], weight[:, 0:width], start=bias is None, stop=True)\
                        .then_inc(multiplied, 1)
                loop(pe, step)
        S.clear()


class Bag:
    pass




def build(nc, X):
    with ExitStack() as ctx:
        T = Bag()
        T.moves = Moves(nc, ctx)

        def sb(c, name, shape, dt):
            t = c.enter_context(nc.sbuf_tensor(name, shape, dt))
            return t
        T.ident = sb(ctx, "ident", [P, P], F32)
        T.ident_b = sb(ctx, "ident_b", [P, P], BF16)
        T.ones = sb(ctx, "ones", [P, P], F32)
        T.ones_b = sb(ctx, "ones_b", [P, P], BF16)
        T.iota1_f = sb(ctx, "iota1_f", [P, P], F32)
        T.tile_s = sb(ctx, "tile_s", [1, C], I32)
        T.tile_d = sb(ctx, "tile_d", [1, C], I32)
        T.m_src = sb(ctx, "m_src", [P, C, 4], F32)
        with ExitStack() as sort:
            T.before = sb(sort, "before", [P, P], F32)
            T.upto = sb(sort, "upto", [P, P], F32)
            T.zero_b = sb(sort, "zero_b", [P, P], BF16)
            T.iota_i = sb(sort, "iota_i", [P, P], I32)
            T.iota_b = sb(sort, "iota_b", [P, P], BF16)
            T.part_i = sb(sort, "part_i", [P, 1], I32)
            T.part_f = sb(sort, "part_f", [P, 1], F32)
            T.ident128_b = sb(sort, "ident128_b", [P, P], BF16)
            T.chunk_i = sb(sort, "chunk_i", [P, C], I32)
            T.chunk_f = sb(sort, "chunk_f", [P, C], F32)
            T.slo_b = sb(sort, "slo_b", [R, ROWE], BF16)
            T.shi_b = sb(sort, "shi_b", [R, ROWE], BF16)
            T.dlo_b = sb(sort, "dlo_b", [R, ROWE], BF16)
            T.dhi_b = sb(sort, "dhi_b", [R, ROWE], BF16)
            T.scol = sb(sort, "scol", [P, ROWCH * R], F32)
            T.dcol = sb(sort, "dcol", [P, ROWCH * R], F32)
            T.shicol = sb(sort, "shicol", [P, ROWCH * R], F32)
            T.dhicol = sb(sort, "dhicol", [P, ROWCH * R], F32)
            T.colp = sb(sort, "colp", [P, ROWCH * R], I32)
            T.meta_src = sb(sort, "meta_src", [P, ROWCH, R, 4], F32)
            T.meta_dst = sb(sort, "meta_dst", [P, ROWCH, R, 4], F32)
            T.hist_s = sb(sort, "hist_s", [P, NT], F32)
            T.hist_d = sb(sort, "hist_d", [P, NT], F32)
            T.first_s = sb(sort, "first_s", [P, NT], F32)
            T.first_d = sb(sort, "first_d", [P, NT], F32)
            build_constants(nc, T)
            build_prepare(nc, T, X)
            build_histogram(nc, T, X)
            build_offsets(nc, T)
            build_place(nc, T, X, True)
            build_place(nc, T, X, False)
        T.acc = sb(ctx, "acc", [P, max(NT * ROW, 2 * SLEN)], F32)
        T.cat1 = sb(ctx, "cat1", [P, WCAT], F32)
        T.cat2 = sb(ctx, "cat2", [P, WCAT], F32)
        T.w0t = sb(ctx, "w0t", [P, 2 * D], F32)
        T.w1 = sb(ctx, "w1", [P, 2 * D], F32)
        T.w2 = sb(ctx, "w2", [P, 2, D], F32)
        T.wt = sb(ctx, "wt", [P, D], F32)
        T.w3 = sb(ctx, "w3", [P, D], F32)
        T.wres = sb(ctx, "wres", [P, D], F32)
        T.b1c = sb(ctx, "b1c", [P, 2], F32)
        T.b0r = sb(ctx, "b0r", [1, D], F32)
        T.b2_parts = sb(ctx, "b2_parts", [3, U * D], BF16)
        T.btr = sb(ctx, "btr", [1, D], F32)
        T.b3r = sb(ctx, "b3r", [1, D], F32)
        T.bresr = sb(ctx, "bresr", [1, D], F32)
        T.bg1 = sb(ctx, "bg1", [P, D], F32)
        T.bg2 = sb(ctx, "bg2", [P, D], F32)
        T.gamma = sb(ctx, "gamma", [P, D], F32)
        T.beta = sb(ctx, "beta", [P, D], F32)
        T.stats = sb(ctx, "stats", [P, NT * 6], F32)
        build_weights(nc, T, X)
        with ExitStack() as gat:
            T.m_dst = sb(gat, "m_dst", [P, C, 4], F32)
            with ExitStack() as sage:
                T.last_src = sb(sage, "last_src", [P, C], F32)
                build_flags(nc, T, X, True)
                build_max_edges(nc, T, X)
            build_flags(nc, T, X, False)
            T.ar = sb(gat, "ar", [P, NT * HEADS], F32)
            with ExitStack() as table:
                T.nodes = sb(table, "nodes_a", [P, NT * D], F32)
                build_nodes(nc, T, X, "sage")
                build_norm(nc, T, X, "x1")
            T.z = sb(gat, "z", [P, C, HEADS], F32)
            for name in ("ga", "gb"):
                build_gat_logits(nc, T, X, name + "l")
                build_gat_softmax(nc, T, X, name + "m")
                build_gat_sums(nc, T, X, name + "s")
                if name == "ga":
                    build_nodes(nc, T, X, "gat_mid")
        T.nodes = sb(ctx, "nodes_b", [P, NT * D], F32)
        build_nodes(nc, T, X, "gat_end")
        build_norm(nc, T, X, "x2")
        build_norm(nc, T, X, "h2")
        build_mlp_edges(nc, T, X)
        build_nodes(nc, T, X, "mlp")
        build_norm(nc, T, X, "x3")
        build_gcn_edges(nc, T, X)
        build_nodes(nc, T, X, "gcn")
        build_norm(nc, T, X, "out")


_INS = ['x', 'src', 'dst', 'edge_attr_128', 'edge_weight', 'L0_gnn_W', 'L0_gnn_b', 'L1_gnn_W1', 'L1_gnn_att_l1', 'L1_gnn_att_r1', 'L1_gnn_b1', 'L1_gnn_W2', 'L1_gnn_att_l2', 'L1_gnn_att_r2', 'L1_gnn_b2', 'L2_gnn_ln_gamma', 'L2_gnn_ln_beta', 'L2_gnn_W1', 'L2_gnn_b1', 'L2_gnn_W2', 'L2_gnn_b2', 'L2_gnn_Wt', 'L2_gnn_bt', 'L3_gnn_W', 'L3_gnn_b', 'L3_gnn_Wres', 'L3_gnn_bres']


def kernel(**inputs):
    import numpy as _np
    import concourse.bacc as _bacc
    from concourse import mybir as _mybir
    from concourse.bass_utils import run_bass_kernel_spmd as _run

    nc = _bacc.Bacc("TRN2", target_bir_lowering=False, num_devices=1)
    X = Bag()
    arrays = {}
    for name in _INS:
        a = _np.ascontiguousarray(inputs[name])
        arrays[f"in_{name}_dram"] = a
        X.__dict__[name] = nc.dram_tensor(f"in_{name}_dram", a.shape, _mybir.dt.from_np(a.dtype), kind="ExternalInput").ap()
    X.out = nc.dram_tensor("out_0_dram", (N, D), F32, kind="ExternalOutput").ap()
    for name, shape, dt in (("xpad", (NPAD, D), F32), ("rec_src", (Q, REC), F32), ("rec_dst", (Q, 4), F32),
                            ("keys_src", (Q + 2,), F32), ("keys_dst", (Q + 2,), F32),
                            ("reset_src", (Q,), BF16), ("reset_dst", (Q,), BF16),
                            ("ends_dst", (Q,), BF16), ("logits", (HEADS, Q), F32), ("exps", (HEADS, Q), F32),
                            ("gathered", (NU * P, UROW), F32),
                            ("hrow", (NPAD, WROW), F32), ("x1", (NPAD, D), F32), ("x2", (NPAD, D), F32),
                            ("h2row", (NPAD, D), F32), ("x3", (NPAD, D), F32), ("h3row", (NPAD, D), F32)):
        X.__dict__[name] = nc.dram_tensor(f"s_{name}", shape, dt, kind="Internal").ap()
    build(nc, X)
    r = _run(nc, [arrays], core_ids=[0])
    return r.results[0]["out_0_dram"]
```
